# Optimizing a Trainium2 kernel written in Bass

```python
import numpy as np
import jax
import jax.numpy as jnp

def _softmax(x, axis=-1):
    return jax.nn.softmax(x, axis=axis)

def _gelu(x):
    return jax.nn.gelu(x, approximate=True)

def _silu(x):
    return jax.nn.silu(x)

def _sigmoid(x):
    return jax.nn.sigmoid(x)

def _layernorm(x, axis=-1, eps=1e-05):
    m = jnp.mean(x, axis=axis, keepdims=True)
    v = jnp.var(x, axis=axis, keepdims=True)
    return (x - m) / jnp.sqrt(v + eps)

def _scatter_add(tgt, idx, src, axis=0):
    return tgt.at[idx].add(src)

def _segment_sum(src, seg, n):
    return jax.ops.segment_sum(src, seg, n)
kernel_name = 'mk_audio_tower_d1_tok_aud1d1024_r4_793f22'

def setup_inputs(seed: int=0):
    np.random.seed(seed)
    _w = jnp.asarray

    def _rec_inputs():
        import jax
        import jax.numpy as jnp
        _rk = jax.random.key(seed)
        x = -9.80646e-05 + 1.00041 * jax.random.normal(jax.random.fold_in(_rk, 1), (16, 4000), jnp.float32)
        return x
    x = _rec_inputs()

    def _L0_tok_setup():
        import jax, jax.numpy as jnp
        import numpy as np
        P = 16
        key = jax.random.key(seed)
        ks = jax.random.split(key, 7)
        B, L = (128, 1024)
        I, H = (512, 256)
        F = 2 * P
        s_in = 1.0 / np.sqrt(F)
        s_mid = 1.0 / np.sqrt(I)
        return {'x': jax.random.normal(ks[0], (B, L), jnp.float32), 'W_h': jax.random.normal(ks[1], (I, F), jnp.float32) * s_in, 'b_h': jax.random.normal(ks[2], (I,), jnp.float32) * s_in, 'W_o': jax.random.normal(ks[3], (H, I), jnp.float32) * s_mid, 'b_o': jax.random.normal(ks[4], (H,), jnp.float32) * s_mid, 'W_r': jax.random.normal(ks[5], (H, F), jnp.float32) * s_in, 'b_r': jax.random.normal(ks[6], (H,), jnp.float32) * s_in}
    _L0_tok_all = _L0_tok_setup()
    _L0_tok_in = {k: v for k, v in _L0_tok_all.items() if k in ('W_h', 'b_h', 'W_o', 'b_o', 'W_r', 'b_r')}
    del _L0_tok_all

    def _L0_attn_setup():
        import math
        import jax, jax.numpy as jnp
        import numpy as np
        D_MODEL = 256
        N_HEADS = 16
        D_K = D_MODEL // N_HEADS
        D_C = 64
        B, S = (2, 512)
        key = jax.random.key(seed)
        ks = jax.random.split(key, 7)
        sd = lambda fan_in: 1.0 / math.sqrt(fan_in)
        return {'x': jax.random.normal(ks[0], (B, S, D_MODEL), dtype=jnp.float32), 'W_dq': jax.random.uniform(ks[1], (D_MODEL, D_C), minval=-sd(D_MODEL), maxval=sd(D_MODEL), dtype=jnp.float32), 'W_uq': jax.random.uniform(ks[2], (D_C, N_HEADS * D_K), minval=-sd(D_C), maxval=sd(D_C), dtype=jnp.float32), 'W_dkv': jax.random.uniform(ks[3], (D_MODEL, D_C), minval=-sd(D_MODEL), maxval=sd(D_MODEL), dtype=jnp.float32), 'W_uk': jax.random.uniform(ks[4], (D_C, N_HEADS * D_K), minval=-sd(D_C), maxval=sd(D_C), dtype=jnp.float32), 'W_uv': jax.random.uniform(ks[5], (D_C, N_HEADS * D_K), minval=-sd(D_C), maxval=sd(D_C), dtype=jnp.float32), 'W_o': jax.random.uniform(ks[6], (N_HEADS * D_K, D_MODEL), minval=-sd(N_HEADS * D_K), maxval=sd(N_HEADS * D_K), dtype=jnp.float32)}
    _L0_attn_all = _L0_attn_setup()
    _L0_attn_in = {k: v for k, v in _L0_attn_all.items() if k in ('W_dq', 'W_uq', 'W_dkv', 'W_uk', 'W_uv', 'W_o')}
    del _L0_attn_all

    def _L0_ffn_setup():
        import jax, jax.numpy as jnp
        import numpy as np
        TOPK = 2
        key = jax.random.key(seed)
        ks = jax.random.split(key, 7)
        B, S, D, E = (4, 1024, 256, 8)
        F = 4 * D
        s = 0.02
        return {'x': jax.random.normal(ks[0], (B, S, D), dtype=jnp.float32), 'router_w': jax.random.normal(ks[1], (D, E), dtype=jnp.float32) * s, 'router_b': jax.random.normal(ks[2], (E,), dtype=jnp.float32) * s, 'w1': jax.random.normal(ks[3], (E, D, F), dtype=jnp.float32) * s, 'b1': jax.random.normal(ks[4], (E, F), dtype=jnp.float32) * s, 'w2': jax.random.normal(ks[5], (E, F, D), dtype=jnp.float32) * s, 'b2': jax.random.normal(ks[6], (E, D), dtype=jnp.float32) * s}
    _L0_ffn_all = _L0_ffn_setup()
    _L0_ffn_in = {k: v for k, v in _L0_ffn_all.items() if k in ('router_w', 'router_b', 'w1', 'b1', 'w2', 'b2')}
    del _L0_ffn_all
    return {'x': x, 'L0_tok_W_h': _L0_tok_in['W_h'], 'L0_tok_b_h': _L0_tok_in['b_h'], 'L0_tok_W_o': _L0_tok_in['W_o'], 'L0_tok_b_o': _L0_tok_in['b_o'], 'L0_tok_W_r': _L0_tok_in['W_r'], 'L0_tok_b_r': _L0_tok_in['b_r'], 'L0_attn_W_dq': _L0_attn_in['W_dq'], 'L0_attn_W_uq': _L0_attn_in['W_uq'], 'L0_attn_W_dkv': _L0_attn_in['W_dkv'], 'L0_attn_W_uk': _L0_attn_in['W_uk'], 'L0_attn_W_uv': _L0_attn_in['W_uv'], 'L0_attn_W_o': _L0_attn_in['W_o'], 'L0_ffn_router_w': _L0_ffn_in['router_w'], 'L0_ffn_router_b': _L0_ffn_in['router_b'], 'L0_ffn_w1': _L0_ffn_in['w1'], 'L0_ffn_b1': _L0_ffn_in['b1'], 'L0_ffn_w2': _L0_ffn_in['w2'], 'L0_ffn_b2': _L0_ffn_in['b2']}

def reference(x, L0_tok_W_h, L0_tok_b_h, L0_tok_W_o, L0_tok_b_o, L0_tok_W_r, L0_tok_b_r, L0_attn_W_dq, L0_attn_W_uq, L0_attn_W_dkv, L0_attn_W_uk, L0_attn_W_uv, L0_attn_W_o, L0_ffn_router_w, L0_ffn_router_b, L0_ffn_w1, L0_ffn_b1, L0_ffn_w2, L0_ffn_b2):
    import jax
    import jax.numpy as jnp

    def _L0_tok_ref(x, W_h, b_h, W_o, b_o, W_r, b_r):
        import jax, jax.numpy as jnp
        import numpy as np
        P = 16
        B, L = x.shape
        pad = -L % P
        mask = jnp.ones_like(x)
        if pad > 0:
            x = jnp.pad(x, ((0, 0), (pad, 0)))
            mask = jnp.pad(mask, ((0, 0), (pad, 0)))
        xp = x.reshape(B, -1, P)
        mp = mask.reshape(B, -1, P)
        x_cat = jnp.concatenate([xp, mp], axis=-1)
        hid = jax.nn.silu(jnp.einsum('bnf,if->bni', x_cat, W_h) + b_h)
        out = jnp.einsum('bni,hi->bnh', hid, W_o) + b_o
        res = jnp.einsum('bnf,hf->bnh', x_cat, W_r) + b_r
        return out + res

    def _L0_attn_ref(x, W_dq, W_uq, W_dkv, W_uk, W_uv, W_o):
        import math
        import jax, jax.numpy as jnp
        import numpy as np
        D_MODEL = 256
        N_HEADS = 16
        D_K = D_MODEL // N_HEADS
        D_C = 64
        B, S = (2, 512)
        Bx, Sx, _ = x.shape
        c_q = x @ W_dq
        Q = (c_q @ W_uq).reshape(Bx, Sx, N_HEADS, D_K)
        c_kv = x @ W_dkv
        K = (c_kv @ W_uk).reshape(Bx, Sx, N_HEADS, D_K)
        V = (c_kv @ W_uv).reshape(Bx, Sx, N_HEADS, D_K)
        scores = jnp.einsum('bqhd,bkhd->bhqk', Q, K) / math.sqrt(D_K)
        causal = jnp.tril(jnp.ones((Sx, Sx), dtype=bool))
        scores = jnp.where(causal, scores, -jnp.inf)
        attn = jax.nn.softmax(scores, axis=-1)
        out = jnp.einsum('bhqk,bkhd->bqhd', attn, V).reshape(Bx, Sx, N_HEADS * D_K)
        return out @ W_o

    def _L0_ffn_ref(x, router_w, router_b, w1, b1, w2, b2):
        import jax, jax.numpy as jnp
        import numpy as np
        TOPK = 2
        E = w1.shape[0]
        logits = jnp.einsum('bsd,de->bse', x, router_w) + router_b
        probs = jax.nn.softmax(logits, axis=-1)
        topv, topi = jax.lax.top_k(probs, TOPK)
        gates = jnp.sum(jax.nn.one_hot(topi, E, dtype=x.dtype) * topv[..., None], axis=-2)
        out = jnp.zeros_like(x)
        for e in range(E):
            h = jax.nn.gelu(jnp.einsum('bsd,df->bsf', x, w1[e]) + b1[e], approximate=False)
            y = jnp.einsum('bsf,fd->bsd', h, w2[e]) + b2[e]
            out = out + gates[..., e:e + 1] * y
        return out
    h = _L0_tok_ref(x, L0_tok_W_h, L0_tok_b_h, L0_tok_W_o, L0_tok_b_o, L0_tok_W_r, L0_tok_b_r)
    h = h + _L0_attn_ref(_layernorm(h, axis=-1), L0_attn_W_dq, L0_attn_W_uq, L0_attn_W_dkv, L0_attn_W_uk, L0_attn_W_uv, L0_attn_W_o)
    h = h + _L0_ffn_ref(_layernorm(h, axis=-1), L0_ffn_router_w, L0_ffn_router_b, L0_ffn_w1, L0_ffn_b1, L0_ffn_w2, L0_ffn_b2)
    return h

_drawn_inputs = setup_inputs


def setup_inputs(seed=0):
    import zlib

    import numpy as np

    out = dict(_drawn_inputs(seed))
    spreads = {}
    factors = {'L0_attn_W_dq': 8.0,
     'L0_attn_W_uq': 8.0,
     'L0_attn_W_uk': 8.0,
     'L0_ffn_router_w': 2.71,
     'L0_ffn_router_b': 8.0,
     'L0_ffn_w1': 2.696,
     'L0_ffn_b1': 23.314,
     'L0_ffn_b2': 8.0}
    for name, (base, spread) in spreads.items():
        noise = np.random.default_rng([zlib.crc32(name.encode()), seed]).standard_normal(out[name].shape)
        drawn = base * np.exp(spread * noise) if base else spread * noise
        out[name] = jnp.asarray(drawn.astype(out[name].dtype))
    for name, factor in factors.items():
        out[name] = (out[name] * factor).astype(out[name].dtype)
    return out
```

```python
from contextlib import ExitStack

import concourse.bass as bass
from concourse import mybir

F32 = mybir.dt.float32
F32R = mybir.dt.float32r
BF16 = mybir.dt.bfloat16
I32 = mybir.dt.int32
U32 = mybir.dt.uint32
ALU = mybir.AluOpType
ACT = mybir.ActivationFunctionType
AX = mybir.AxisListType

B, L = 16, 4000
PATCH = 16
S = L // PATCH
TT = S // 2
NT = B * S // TT
NTOK = B * S
D = 256
DC = D // 128
I = 512
IC = I // 128
H, DK = 16, 16
LOW = 64
NG = H // 4
E, F, TOPK = 8, 1024, 2
FC = F // 128
EPS = 1e-5
NEG = -1e30
SCALE = float(DK) ** -0.5
XT_TERMS = 6 * PATCH
KX = XT_TERMS + 3
ROWS = 128
REGION = 4224
NTILE = (NTOK * TOPK + E * (ROWS - 1)) // ROWS
NTILE += NTILE % 2
PW = 272
W16 = NTILE + 2


def build(nc, x, W_h, b_h, tW_o, b_o, W_r, b_r, W_dq, W_uq, W_dkv, W_uk, W_uv, aW_o,
          router_w, router_b, w1, b1, w2, b2, out):
    assert NTILE % 2 == 0
    with ExitStack() as ctx:
        def sem(name):
            return ctx.enter_context(nc.semaphore(name))

        def sb(name, shape, dt, c=ctx):
            return c.enter_context(nc.sbuf_tensor(name, shape, dt))

        acc = nc.dram_tensor("acc", (NTOK + S, D), F32, kind="Internal").ap()
        rows = nc.dram_tensor("rows", (E * REGION + ROWS, PW), F32, kind="Internal").ap()

        ps = ctx.enter_context(nc.psum_tensor("ps", [128, 8, 512], F32))

        w1s = sb("w1s", [128, E, DC, 2, F], BF16)
        w2s = sb("w2s", [128, E, FC, 2, D], BF16)
        b1s = sb("b1s", [128, E, FC], F32)
        ident = sb("ident", [128, 128], F32)
        identb = sb("identb", [128, 128], BF16)
        count = sb("count", [128, E], F32)
        region0 = sb("region0", [128, E], F32)

        env = dict(locals())
        tokenizer(env, ctx)
        attention(env)
        experts(env)


def tokenizer(env, ctx):
    nc, ps, ident, identb = env["nc"], env["ps"], env["ident"], env["identb"]
    x, W_h, b_h, tW_o, b_o, W_r, b_r = (env[k] for k in ("x", "W_h", "b_h", "tW_o", "b_o", "W_r", "b_r"))
    acc, w1, w2, b1, w1s, w2s, b1s = (env[k] for k in ("acc", "w1", "w2", "b1", "w1s", "w2s", "b1s"))
    sem = env["sem"]
    NJ = IC + DC
    with ExitStack() as own:
        def sb(name, shape, dt):
            return own.enter_context(nc.sbuf_tensor(name, shape, dt))

        xin = sb("xin", [TT, NT, PATCH], F32)
        xres = sb("xres", [TT, NT, PATCH], F32)
        xst = sb("xst", [TT, NT, KX], BF16)
        win = sb("win", [128, NJ, 2 * PATCH], F32)
        wres = sb("wres", [128, NJ, PATCH], F32)
        wst = sb("wst", [128, NJ, KX], BF16)
        bin_ = sb("bin", [128, NJ], F32)
        bout = sb("bout", [128, DC], F32)
        bsum = sb("bsum", [128, NJ], F32)
        bres = sb("bres", [128, NJ], F32)
        won = sb("won", [128, DC, I], F32)
        xt = sb("xt", [KX, NT * TT], BF16)
        wt = sb("wt", [KX, NJ * 128], BF16)
        wot = sb("wot", [128, IC, D], F32)
        zrow = sb("zrow", [TT, 2, D], F32)
        hid = [sb(f"hid{u}", [128, IC, S], F32) for u in range(2)]
        hout = [sb(f"hout{u}", [TT, 2, D], F32) for u in range(2)]
        wraw = [sb(f"wraw{u}", [128, 2 * F], F32) for u in range(2)]

        x_in, w_in, won_in, consts = sem("x_in"), sem("w_in"), sem("won_in"), sem("consts")
        id_zero, ident_ready = sem("id_zero"), sem("ident_ready")
        xst_ready, wst_ready = sem("xst_ready"), sem("wst_ready")
        xt_ps, wt_ps, won_ps, turned = sem("xt_ps"), sem("wt_ps"), sem("won_ps"), sem("turned")
        turned_act = sem("turned_act")
        zero_out, b1_in = sem("zero_out"), sem("b1_in")

        def split3(dve, src, rest, dst, terms):
            for k in range(3):
                first = terms[k][0]
                dve.tensor_copy(dst(first), src if k == 0 else rest)
                dve.drain()
                for t in terms[k][1:]:
                    dve.tensor_copy(dst(t), dst(first))
                if k < 2:
                    dve.tensor_tensor(rest, src if k == 0 else rest, dst(first), ALU.subtract)
                dve.drain()

        with nc.Block() as block:
            @block.sync
            def _(sp):
                sp.dma_start(xin[:, :, :], x.rearrange("b (t p i) -> p (b t) i", p=TT, i=PATCH)).then_inc(x_in, 16)
                sp.dma_start(win[:, 0:IC, :], W_h.rearrange("(c p) f -> p c f", p=128)).then_inc(w_in, 16)
                sp.dma_start(win[:, IC:NJ, :], W_r.rearrange("(c p) f -> p c f", p=128)).then_inc(w_in, 16)
                with nc.allow_non_contiguous_dma(reason="biases, once"):
                    sp.dma_start(bin_[:, 0:IC], b_h.rearrange("(c p) -> p c", p=128)).then_inc(w_in, 16)
                    sp.dma_start(bin_[:, IC:NJ], b_r.rearrange("(c p) -> p c", p=128)).then_inc(w_in, 16)
                    sp.dma_start(bout[:, :], b_o.rearrange("(c p) -> p c", p=128)).then_inc(w_in, 16)
                sp.dma_start(won[:, :, :], tW_o.rearrange("(c p) i -> p c i", p=128)).then_inc(won_in, 16)
                sp.wait_ge(consts, 1)
                sp.dma_start(acc[NTOK:NTOK + S, :].rearrange("(t p) d -> p t d", p=TT), zrow[:, :, :]).then_inc(zero_out, 16)
                sp.wait_ge(zero_out, 16)

            @block.scalar
            def _(act):
                with nc.allow_non_contiguous_dma(reason="biases, once"):
                    for e in range(E):
                        act.dma_start(b1s[:, e, :], b1[e, :].rearrange("(c p) -> p c", p=128)).then_inc(b1_in, 16)
                act.wait_ge(b1_in, 16 * E)
                for k in range(2):
                    act.wait_ge(won_ps, k + 1)
                    act.copy(wot[:, 2 * k:2 * k + 2, :].rearrange("p c n -> p (c n)"),
                             ps[:, 5 + k, :]).then_inc(turned_act, 1)

            @block.gpsimd
            def _(pool):
                pool.memset(ident[:, :], 0.0).then_inc(id_zero, 1)
                pool.memset(identb[:, :], 0.0).then_inc(id_zero, 1)
                pool.memset(zrow[:, :, :], 0.0).then_inc(consts, 1)
                pool.wait_ge(id_zero, 2)
                for m in (ident, identb):
                    pool.affine_select(out=m[:, :], in_=m[:, :], compare_op=ALU.not_equal, fill=1.0, base=0,
                                       pattern=[[-1, 128]], channel_multiplier=1).then_inc(ident_ready, 1)

            @block.vector
            def _(dve):
                dve.memset(xst[:, :, XT_TERMS:KX], 1.0)
                dve.wait_ge(w_in, 80)
                dve.tensor_reduce(bsum[:, :], win[:, :, PATCH:2 * PATCH], AX.X, ALU.add)
                dve.drain()
                dve.tensor_tensor(bsum[:, :], bsum[:, :], bin_[:, :], ALU.add)
                dve.drain()
                dve.tensor_tensor(bsum[:, IC:NJ], bsum[:, IC:NJ], bout[:, :], ALU.add)
                dve.drain()
                split3(dve, win[:, :, 0:PATCH], wres[:, :, :],
                       lambda t: wst[:, :, t * PATCH:(t + 1) * PATCH], [[0, 3, 5], [1, 4], [2]])
                split3(dve, bsum[:, :], bres[:, :], lambda t: wst[:, :, XT_TERMS + t], [[0], [1], [2]])
                dve.nop().then_inc(wst_ready, 1)
                dve.wait_ge(x_in, 16)
                split3(dve, xin[:, :, :], xres[:, :, :],
                       lambda t: xst[:, :, t * PATCH:(t + 1) * PATCH], [[0, 1, 2], [3, 4], [5]])
                dve.nop().then_inc(xst_ready, 1)
                dve.wait_ge(wt_ps, 1)
                dve.tensor_copy(wt[:, :], ps[0:KX, 4, :].bitcast(BF16)[:, 0:NJ * 128]).then_inc(turned, 1)
                for k in range(4):
                    dve.wait_ge(xt_ps, k + 1)
                    dve.tensor_copy(xt[:, k * 8 * TT:(k + 1) * 8 * TT].rearrange("k (t n) -> k t n", n=TT),
                                    ps[0:KX, k, :].bitcast(BF16).rearrange("k (t n) -> k t n", n=128)[:, :, 0:TT]
                                    ).then_inc(turned, 1)

            @block.tensor
            def _(pe):
                pe.wait_ge(ident_ready, 2)
                pe.wait_ge(won_in, 16)
                for k in range(2):
                    for q in range(4):
                        c, n = 2 * k + q // 2, q % 2
                        mm = pe.transpose(ps[:, 5 + k, q * 128:(q + 1) * 128],
                                          won[:, n, c * 128:(c + 1) * 128], ident[:, :])
                    mm.then_inc(won_ps, 1)
                pe.wait_ge(wst_ready, 1)
                for c in range(NJ):
                    mm = pe.transpose(ps[0:KX, 4, :].bitcast(BF16)[:, c * 128:(c + 1) * 128],
                                      wst[:, c, :], identb[:, :])
                mm.then_inc(wt_ps, 1)
                pe.wait_ge(xst_ready, 1)
                for t in range(NT):
                    mm = pe.transpose(ps[0:KX, t // 8, :].bitcast(BF16)[:, (t % 8) * 128:(t % 8) * 128 + TT],
                                      xst[:, t, :], identb[0:TT, 0:TT])
                    if t % 8 == 7:
                        mm.then_inc(xt_ps, 1)

        hid_ps, hid_ready, hid_used = sem("hid_ps"), sem("hid_ready"), sem("hid_used")
        h_ps, h_ready = sem("h_ps"), sem("h_ready")
        h_stored = [sem(f"h_stored{u}") for u in range(2)]
        w_loaded = [sem(f"w_loaded{u}") for u in range(2)]
        w_high, w_low = sem("w_high"), sem("w_low")

        with nc.Block() as block:
            @block.sync
            def _(sp):
                def load_w(e, u):
                    src = (w1 if u == 0 else w2)[bass.ds(e, 1), :, :]
                    src = src.rearrange("o (c p) n -> p (o c) n", p=128)
                    sp.dma_start(wraw[u][:, :].rearrange("p (c n) -> p c n", c=DC if u == 0 else FC),
                                 src).then_inc(w_loaded[u], 16)

                load_w(0, 0)
                load_w(0, 1)

                def pair(e, first, last):
                    for u in range(2):
                        if not last:
                            sp.wait_ge(w_high, 2 * e + u + 1)
                            sp.wait_ge(w_low, 2 * e + u + 1)
                            load_w(e + 1, u)
                    for u in range(2):
                        sp.wait_ge(h_ready, 2 * e + u + 1)
                        sp.dma_start(acc[bass.ds((2 * e + u) * S, S), :].rearrange("(t p) d -> p t d", p=TT),
                                     hout[u][:, :, :]).then_inc(h_stored[u], 16)

                with sp.Fori(0, E - 1) as e:
                    pair(e, False, False)
                pair(E - 1, False, True)
                for u in range(2):
                    sp.wait_ge(h_stored[u], 16 * E)

            @block.scalar
            def _(act):
                def pair(e, first):
                    for u in range(2):
                        act.wait_ge(hid_ps, 2 * e + u + 1)
                        if not first:
                            act.wait_ge(hid_used, 2 * e + u - 1)
                        act.activation(hid[u][:, :, :].rearrange("p (k c) n -> p k (c n)", k=2),
                                       ps[:, 2 * u:2 * u + 2, 0:2 * S], ACT.Silu).then_inc(hid_ready, 1)
                        act.wait_ge(w_loaded[u], (e + 1) * 16)
                        ws, c = (w1s, DC) if u == 0 else (w2s, FC)
                        act.copy(ws[:, bass.ds(e, 1), :, 0, :].rearrange("p o c n -> p (o c) n"),
                                 wraw[u][:, :].rearrange("p (c n) -> p c n", c=c)).then_inc(w_high, 1)

                pair(0, True)
                with act.Fori(1, E) as e:
                    pair(e, False)

            @block.vector
            def _(dve):
                def pair(e, first):
                    for u in range(2):
                        dve.wait_ge(h_ps, 2 * e + u + 1)
                        if not first:
                            dve.wait_ge(h_stored[u], 16 * e)
                        dve.tensor_copy(hout[u][:, :, :].rearrange("p t d -> p (t d)"),
                                        ps[0:TT, 4 + u, :]).then_inc(h_ready, 1)
                    for u in range(2):
                        dve.wait_ge(w_high, 2 * e + u + 1)
                        ws, c = (w1s, DC) if u == 0 else (w2s, FC)
                        dve.tensor_tensor(ws[:, bass.ds(e, 1), :, 1, :].rearrange("p o c n -> p (o c) n"),
                                          wraw[u][:, :].rearrange("p (c n) -> p c n", c=c),
                                          ws[:, bass.ds(e, 1), :, 0, :].rearrange("p o c n -> p (o c) n"),
                                          ALU.subtract).then_inc(w_low, 1)

                pair(0, True)
                with dve.Fori(1, E) as e:
                    pair(e, False)

            @block.tensor
            def _(pe):
                def pair(e, first):
                    for u in range(2):
                        for c in range(IC):
                            mm = pe.matmul(ps[:, 2 * u + c // 2, (c % 2) * S:(c % 2 + 1) * S],
                                           wt[:, c * 128:(c + 1) * 128],
                                           xt[:, bass.ds((2 * e + u) * S, S)], start=True, stop=True)
                        mm.then_inc(hid_ps, 1)
                    for u in range(2):
                        if not first:
                            pe.wait_ge(h_ready, 2 * e + u - 1)
                        for t in range(2):
                            o = ps[0:TT, 4 + u, t * D:(t + 1) * D]
                            pe.matmul(o, xt[:, bass.ds((2 * e + u) * S + t * TT, TT)],
                                      wt[:, IC * 128:NJ * 128], start=True, stop=False)
                            if t == 0:
                                pe.wait_ge(hid_ready, 2 * e + u + 1)
                            for c in range(IC):
                                mm = pe.matmul(o, hid[u][:, c, t * TT:(t + 1) * TT], wot[:, c, :],
                                               start=False, stop=c == IC - 1)
                        mm.then_inc(h_ps, 1)
                        pe.nop().then_inc(hid_used, 1)

                pair(0, True)
                with pe.Fori(1, E) as e:
                    pair(e, False)


def attention(env):
    nc, ps, ident, identb, sem = env["nc"], env["ps"], env["ident"], env["identb"], env["sem"]
    W_dq, W_uq, W_dkv, W_uk, W_uv, aW_o = (env[k] for k in ("W_dq", "W_uq", "W_dkv", "W_uk", "W_uv", "aW_o"))
    router_w, router_b, acc, rows = (env[k] for k in ("router_w", "router_b", "acc", "rows"))
    count, region0 = env["count"], env["region0"]
    HALF = TT + 1
    BS = HALF + S
    MAXROW = 3 * DK
    BQ, BK, BSC, BST, BO_, BM = 0, 1, 2, 4, 6, 7
    LAST = B - 1

    with ExitStack() as own:
        def sb(name, shape, dt):
            return own.enter_context(nc.sbuf_tensor(name, shape, dt))

        wd = sb("wd", [128, DC, 2, 2, LOW], F32)
        wuh = [sb(f"wuh{k}", [128, H // 2, 2, 4, DK], F32R) for k in range(2)]
        wul = [sb(f"wul{k}", [128, H // 2, 2, 4, DK], F32R) for k in range(2)]
        wvh, wvl = sb("wvh", [128, D], F32R), sb("wvl", [128, D], F32R)
        wo = sb("wo", [128, DC, D], F32)
        rw = sb("rw", [128, DC, E], F32)
        rb = sb("rb", [TT, 1, E], F32)
        ccol = sb("ccol", [128, 4], F32)
        s_q, s_k, s_c, k_one = (ccol[:, j:j + 1] for j in range(4))
        mask_q = sb("mask_q", [TT, 2, HALF], BF16)
        mask_k = sb("mask_k", [TT, 2, HALF], BF16)
        below = sb("below", [TT, TT], BF16)
        ones = sb("ones", [TT, 128], BF16)
        iota_i = sb("iota_i", [TT, E], I32)
        iota_e = sb("iota_e", [TT, 1, E], F32)
        tok_i = sb("tok_i", [TT, 2], I32)
        token = sb("token", [TT, 2], F32)
        reg_i = sb("reg_i", [128, E], I32)
        minus_half = sb("minus_half", [TT, 2], F32)
        h_ln = sb("h_ln", [TT, 2, D], F32)
        h_new = sb("h_new", [TT, 2, D], F32)
        st6 = sb("st6", [TT, 2, 2, 6], F32)
        mv = sb("mv", [TT, 2, 2, 2], F32)
        var_e = sb("var_e", [TT, 2, 2], F32)
        rstd = sb("rstd", [TT, 2, 2], F32)
        xn = sb("xn", [TT, 2, D], F32)
        xnt = sb("xnt", [128, DC, S], F32)
        cs = sb("cs", [128, 2, S], F32R)
        q_r, k_r = sb("q_r", [128, 2, S], F32R), sb("k_r", [128, 2, S], F32R)
        c_r = q_r
        qs = sb("qs", [128, NG, 2, S], F32R)
        ks = sb("ks", [128, NG, 2, S], F32R)
        v = sb("v", [TT, 2, H, 32], F32)
        mx = sb("mx", [TT, 2, 4], F32)
        mxh = sb("mxh", [TT, 2, 4], F32R)
        mxt = sb("mxt", [TT, 2, 2, 2, LOW], F32)
        p_all = sb("p", [128, 2, 4, BS], F32)
        p = p_all[0:TT]
        setup_part = p_all[:, :, :, :].rearrange("p a h n -> p (a h n)")
        wu = setup_part[:, 0:3 * D].rearrange("p (k n) -> p k n", n=D)
        crow = setup_part[0:1, 3 * D:3 * D + 512].rearrange("p (k n) -> p k n", n=128)
        os_ = sb("os", [128, NG, S], F32)
        rden = sb("rden", [TT, 2, H], F32)
        on = xn
        ont = x2t = xnt
        pay = sb("pay", [TT, 2, PW], F32)
        lg = sb("lg", [TT, 2, E], F32)
        ex = sb("ex", [TT, 2, E], F32)
        small = sb("small", [TT, 4, 2], F32)
        top = sb("top", [TT, 2, 8], F32)
        topi = sb("topi", [TT, 2, 8], U32)
        topf = sb("topf", [TT, 2, 2], F32)
        hot = sb("hot", [TT, 2, 2, E], F32)
        hotb = sb("hotb", [TT, 2, E], BF16)
        rank = sb("rank", [TT, 2, E], F32)
        slotf = sb("slotf", [TT, 2, 2], F32)
        slot = sb("slot", [TT, 2, 2], I32)

        bw_in, rb_in, ccol_in = sem("bw_in"), sem("rb_in"), sem("ccol_in")
        zeroed, consts_ready, crow_ready, weights_split = (
            sem("zeroed"), sem("consts_ready"), sem("crow_ready"), sem("weights_split"))

        with nc.Block() as block:
            @block.sync
            def _(sp):
                for c in range(DC):
                    for k, w in enumerate((W_dq, W_dkv)):
                        for r in range(2):
                            sp.dma_start(wd[:, c, k, r, :], w[c * 128:(c + 1) * 128, :]).then_inc(bw_in, 16)
                for k, w in enumerate((W_uq, W_uk, W_uv)):
                    for r in range(2):
                        sp.dma_start(wu[r * LOW:(r + 1) * LOW, k, :], w).then_inc(bw_in, 16)
                sp.dma_start(wo[:, :, :], aW_o.rearrange("(c p) n -> p c n", p=128)).then_inc(bw_in, 16)
                sp.dma_start(rw[:, :, :], router_w.rearrange("(c p) n -> p c n", p=128)).then_inc(bw_in, 16)
                sp.dma_start(rb[:, 0, :], router_b.rearrange("(o e) -> o e", o=1).broadcast_to([TT, E])).then_inc(rb_in, 16)
                sp.wait_ge(crow_ready, 1)
                with nc.allow_non_contiguous_dma(reason="512 factors, once"):
                    for j in range(4):
                        sp.dma_start(ccol[:, j:j + 1], crow[0:1, j, :]).then_inc(ccol_in, 16)
                sp.wait_ge(ccol_in, 64)

            @block.gpsimd
            def _(pool):
                for m in (mask_q, mask_k, ones):
                    pool.memset(m[:, :] if m is ones else m[:, :, :], 1.0 if m is ones else 0.0)
                pool.memset(below[:, :], 1.0)
                pool.memset(mxt[:, :, :, :, :], 0.0)
                pool.memset(v[:, :, :, :], 0.0)
                pool.memset(minus_half[:, :], -0.5)
                pool.memset(pay[:, :, :], 0.0)
                pool.iota(iota_i[:, :], pattern=[[1, E]], base=0, channel_multiplier=0)
                pool.iota(tok_i[:, :], pattern=[[TT, 2]], base=0, channel_multiplier=1)
                pool.iota(reg_i[:, :], pattern=[[REGION, E]], base=0, channel_multiplier=0)
                pool.drain()
                pool.affine_select(out=mask_q[:, :, :], in_=mask_q[:, :, :], compare_op=ALU.is_ge, fill=NEG, base=0,
                                   pattern=[[1, 2], [-1, HALF]], channel_multiplier=1)
                pool.affine_select(out=mask_k[:, :, :], in_=mask_k[:, :, :], compare_op=ALU.is_ge, fill=NEG, base=0,
                                   pattern=[[-1, 2], [1, HALF]], channel_multiplier=-1)
                pool.affine_select(out=below[:, :], in_=below[:, :], compare_op=ALU.is_gt, fill=0.0, base=0,
                                   pattern=[[1, TT]], channel_multiplier=-1)
                pool.memset(v[:, :, :, DK:DK + 1], 1.0)
                pool.tensor_copy(iota_e[:, 0, :], iota_i[:, :])
                pool.tensor_copy(token[:, :], tok_i[:, :])
                pool.tensor_copy(region0[:, :], reg_i[:, :])
                pool.tensor_copy(count[:, :], reg_i[:, :])
                pool.drain()

            @block.vector
            def _(dve):
                dve.memset(crow[:, :, :], 0.0)
                for w in (*wuh, *wul):
                    dve.memset(w[:, :, :, :, :].bitcast(F32), 0.0)
                dve.memset(wvl[:, :].bitcast(F32), 0.0)
                dve.drain()
                for a in range(2):
                    o = a * LOW
                    dve.memset(crow[:, 0, o + DK:o + 2 * DK], -1.0)
                    dve.memset(crow[:, 1, o + 2 * DK:o + 3 * DK], -1.0)
                    dve.memset(crow[:, 1, o + MAXROW:o + MAXROW + 2], 1.0)
                    dve.memset(crow[:, 3, o + MAXROW:o + MAXROW + 2], 1.0)
                dve.memset(crow[:, 2, LOW:128], -1.0)
                dve.drain()
                dve.nop().then_inc(crow_ready, 1)
                dve.wait_ge(bw_in, 16 * (4 * DC + 8))
                for k in range(2):
                    src = wu[:, k, :].rearrange("p (h a d) -> p h a d", a=2, d=DK)
                    for r in range(3):
                        dve.tensor_copy(wuh[k][:, :, :, r, :], src)
                    dve.drain()
                    for r in range(3):
                        dve.tensor_tensor(wul[k][0:LOW, :, :, r, :], src[0:LOW], wuh[k][0:LOW, :, :, 0, :],
                                          ALU.subtract)
                dve.tensor_copy(wvh[:, :], wu[:, 2, :])
                dve.drain()
                dve.tensor_tensor(wvl[0:LOW, :], wu[0:LOW, 2, :], wvh[0:LOW, :], ALU.subtract)
                dve.drain()
                dve.wait_ge(rb_in, 16)

        q_ps, k_ps, q_round, k_round, q_split, k_split = (
            sem("q_ps"), sem("k_ps"), sem("q_round"), sem("k_round"), sem("q_split"), sem("k_split"))
        s_ps, max_read, max_rows, max_ps, q_aug = (
            sem("s_ps"), sem("max_read"), sem("max_rows"), sem("max_ps"), sem("q_aug"))
        st_ps, exp_done, pv_ps, o_read = sem("st_ps"), sem("exp_done"), sem("pv_ps"), sem("o_read")
        v_ps, v_ready, c_ps, c_round, c_split = sem("v_ps"), sem("v_ready"), sem("c_ps"), sem("c_round"), sem("c_split")
        turn_o_ps, o_normed, turn_n_ps, on_turned, ao_ps, h_done = (
            sem("turn_o_ps"), sem("o_normed"), sem("turn_n_ps"), sem("on_turned"), sem("ao_ps"), sem("h_done"))
        h_kept = sem("h_kept")
        ln1_var, ln1_rstd, xn_ready, xt_ps, xn_turned = (
            sem("ln1_var"), sem("ln1_rstd"), sem("xn_ready"), sem("xn_ps"), sem("xn_turned"))
        ln2_var, ln2_rstd, x2_ready, x2_ps, x2_turned = (
            sem("ln2_var"), sem("ln2_rstd"), sem("x2_ready"), sem("x2_ps"), sem("x2_turned"))
        lg_ps, lg_ready, lg_exp, hot_ready, rank_ps, slots_ready = (
            sem("lg_ps"), sem("lg_ready"), sem("lg_exp"), sem("hot_ready"), sem("rank_ps"), sem("slots_ready"))
        ln_loaded, res_loaded, scattered = sem("ln_loaded"), sem("res_loaded"), sem("scattered")

        def seq_rows(b):
            return acc[bass.ds(b * S, S), :].rearrange("(t p) d -> p t d", p=TT)

        with nc.Block() as block:
            @block.sync
            def _(sp):
                def load_ln(b):
                    sp.dma_start(h_ln[:, :, :], seq_rows(b)).then_inc(ln_loaded, 16)

                def load_res(b, first):
                    if not first:
                        sp.wait_ge(h_kept, 16 * b)
                        sp.wait_ge(x2_ready, b)
                    sp.dma_start(h_new[:, :, :], seq_rows(b)).then_inc(res_loaded, 16)

                def keep(b):
                    sp.wait_ge(h_done, b + 1)
                    sp.dma_start(seq_rows(b), h_new[:, :, :]).then_inc(h_kept, 16)

                load_ln(0)
                load_res(0, True)
                sp.wait_ge(xn_ready, 1)
                load_ln(1)

                def body(b, first, last):
                    if not last:
                        sp.wait_ge(xn_ready, b + 2)
                        load_ln(b + 2)
                    if not first:
                        keep(b - 1)
                        load_res(b, False)

                body(0, True, False)
                with sp.Fori(1, LAST) as b:
                    body(b, False, False)
                body(LAST, False, True)
                keep(LAST)
                sp.wait_ge(h_kept, 16 * B)

            @block.scalar
            def _(act):
                def exps(n, g, q):
                    act.wait_ge(st_ps, 2 * n + q + 1)
                    act.activation(p[:, g % 2, 2 * q:2 * q + 2, :], ps[0:TT, BST:BST + 2, 0:BS],
                                   ACT.Exp, scale=SCALE).then_inc(exp_done, 1)

                def round_qk(m, g):
                    act.wait_ge(q_ps, m + 1)
                    act.activation(q_r[:, :, :].rearrange("p a n -> p (a n)"), ps[:, BQ, 0:2 * S],
                                   ACT.Copy).then_inc(q_round, 1)
                    act.wait_ge(k_ps, m + 1)
                    act.activation(k_r[:, :, :].rearrange("p a n -> p (a n)"), ps[:, BK, 0:2 * S],
                                   ACT.Identity, bias=k_one).then_inc(k_round, 1)

                def round_c(b):
                    act.wait_ge(c_ps, b + 1)
                    act.activation(c_r[:, :, :].rearrange("p a n -> p (a n)"), ps[:, BM, 0:2 * S],
                                   ACT.Copy).then_inc(c_round, 1)

                def copy_v(b, first):
                    act.wait_ge(v_ps, b + 1)
                    if not first:
                        act.wait_ge(pv_ps, NG * b)
                    act.copy(v[:, :, :, 0:DK], ps[0:TT, BM, :].rearrange("p (t h d) -> p t h d", t=2, d=DK)
                             ).then_inc(v_ready, 1)

                def copy_o(n, g):
                    act.wait_ge(pv_ps, n + 1)
                    act.copy(os_[:, g, :], ps[:, BO_, 0:S]).then_inc(o_read, 1)

                def copy_turned(ready, b, dst, done):
                    act.wait_ge(ready, b + 1)
                    act.copy(dst[:, :, :].rearrange("p c n -> p (c n)"), ps[:, BM, 0:2 * S]).then_inc(done, 1)

                def exp_logits(b):
                    act.wait_ge(lg_ready, b + 1)
                    act.activation(ex[:, :, :], lg[:, :, :], ACT.Exp).then_inc(lg_exp, 1)

                copy_turned(xt_ps, 0, xnt, xn_turned)
                round_c(0)
                copy_turned(xt_ps, 1, xnt, xn_turned)
                for m in range(3):
                    if m:
                        act.wait_ge(q_split, m)
                        act.wait_ge(k_split, m)
                    round_qk(m, m)

                def body(b, first, last):
                    for d in range(NG):
                        n = NG * b + d
                        if not (first and d < 2):
                            act.wait_ge(pv_ps, n - 1)
                        exps(n, d, 0)
                        if not (last and d > 0):
                            act.wait_ge(q_split, n + 3)
                            act.wait_ge(k_split, n + 3)
                            round_qk(n + 3, (d + 3) % NG)
                        if d == 0:
                            copy_v(b, first)
                        exps(n, d, 1)
                        if not (first and d == 0):
                            if d > 0 and not first:
                                act.wait_ge(turn_o_ps, 2 * b)
                            copy_o(n - 1, (d - 1) % NG)
                        if d == 0 and not last:
                            act.wait_ge(c_split, b + 1)
                            round_c(b + 1)
                        if not first:
                            if d == 1:
                                copy_turned(turn_n_ps, b - 1, ont, on_turned)
                            if d == 3:
                                copy_turned(x2_ps, b - 1, x2t, x2_turned)
                                exp_logits(b - 1)
                        if d == 3 and not last:
                            copy_turned(xt_ps, b + 2, xnt, xn_turned)

                body(0, True, False)
                with act.Fori(1, LAST) as b:
                    body(b, False, False)
                body(LAST, False, True)
                copy_o(NG * B - 1, NG - 1)
                copy_turned(turn_n_ps, LAST, ont, on_turned)
                copy_turned(x2_ps, LAST, x2t, x2_turned)
                exp_logits(LAST)

            @block.gpsimd
            def _(pool):
                def power(var_ready, b, k, done):
                    pool.wait_ge(var_ready, b + 1)
                    pool.tensor_tensor(rstd[:, k, :], var_e[:, k, :], minus_half[:, :], ALU.pow).then_inc(done, 1)

                def scatter(b):
                    pool.wait_ge(ln1_rstd, 1)
                    pool.wait_ge(slots_ready, b + 1)
                    for t in range(2):
                        for k in range(2):
                            pool.indirect_dma_start(
                                out=rows[:, :], out_offset=bass.IndirectOffsetOnAxis(ap=slot[:, t, k:k + 1], axis=0),
                                in_=pay[:, t, :], in_offset=None).then_inc(scattered, 16)

                power(ln1_var, 0, 0, ln1_rstd)
                power(ln1_var, 1, 0, ln1_rstd)
                power(ln1_var, 2, 0, ln1_rstd)
                with pool.Fori(1, LAST) as b:
                    power(ln2_var, b - 1, 1, ln2_rstd)
                    power(ln1_var, b + 2, 0, ln1_rstd)
                    scatter(b - 1)
                power(ln2_var, LAST - 1, 1, ln2_rstd)
                scatter(LAST - 1)
                power(ln2_var, LAST, 1, ln2_rstd)
                scatter(LAST)
                pool.wait_ge(scattered, 64 * B)

            @block.vector
            def _(dve):
                def split(out, r, factor, src, done):
                    dve.scalar_tensor_tensor(out=out, in0=r, scalar=factor, in1=src,
                                             op0=ALU.mult, op1=ALU.add).then_inc(done, 1)

                def split_qk(m, g):
                    dve.wait_ge(q_round, m + 1)
                    split(qs[:, g, :, :].rearrange("p a n -> p (a n)"), q_r[:, :, :].rearrange("p a n -> p (a n)"),
                          s_q, ps[:, BQ, 0:2 * S], q_split)
                    dve.wait_ge(k_round, m + 1)
                    split(ks[:, g, :, :].rearrange("p a n -> p (a n)"), k_r[:, :, :].rearrange("p a n -> p (a n)"),
                          s_k, ps[:, BK, 0:2 * S], k_split)

                def split_c(b):
                    dve.wait_ge(c_round, b + 1)
                    split(cs[:, :, :].rearrange("p a n -> p (a n)"), c_r[:, :, :].rearrange("p a n -> p (a n)"),
                          s_c, ps[:, BM, 0:2 * S], c_split)

                def maxima(m, q, first=False):
                    if q == 0 and not first:
                        dve.wait_ge(max_rows, m)
                    dve.wait_ge(s_ps, 2 * m + q + 1)
                    dve.tensor_reduce(mx[:, 0, 2 * q:2 * q + 2], ps[0:TT, BSC:BSC + 2, 0:HALF], AX.X, ALU.max)
                    dve.tensor_reduce(mx[:, 1, 2 * q:2 * q + 2], ps[0:TT, BSC:BSC + 2, HALF:BS], AX.X,
                                      ALU.max).then_inc(max_read, 1)

                def rows_of_max(m):
                    dve.drain()
                    dve.tensor_scalar(mxh[:, :, :], mx[:, :, :], -1.0, None, ALU.mult)
                    dve.drain()
                    mh = mxh[:, :, :].rearrange("p t (r a) -> p t r a", a=2)
                    dve.tensor_copy(mxt[:, :, :, :, MAXROW], mh)
                    dve.scalar_tensor_tensor(out=mxt[:, :, :, :, MAXROW + 1],
                                             in0=mx[:, :, :].rearrange("p t (r a) -> p t r a", a=2), scalar=-1.0,
                                             in1=mh, op0=ALU.mult, op1=ALU.subtract).then_inc(max_rows, 1)

                def augment(n, g):
                    dve.wait_ge(max_ps, n + 1)
                    o = qs[:, g, :, :].rearrange("p a n -> p (a n)")
                    dve.tensor_tensor(o, ps[:, BQ, 0:2 * S], o, ALU.add).then_inc(q_aug, 1)

                def norm_o(b, t):
                    dve.wait_ge(turn_o_ps, 2 * b + t + 1)
                    o = ps[0:TT, BM, :].rearrange("p (h c) -> p h c", c=32)
                    dve.reciprocal(rden[:, t, :], o[:, :, DK])
                    dve.drain()
                    dve.tensor_tensor(on[:, t, :].rearrange("p (h c) -> p h c", c=DK), o[:, :, 0:DK],
                                      rden[:, t, :].unsqueeze(2).broadcast_to([TT, H, DK]),
                                      ALU.mult).then_inc(o_normed, 1)

                def stats(h, k, done):
                    for t in range(2):
                        dve.bn_stats(st6[:, k, t, :], h[:, t, :])
                    dve.drain()
                    for t in range(2):
                        dve.bn_aggr(mv[:, k, t, :], st6[:, k, t, :])
                    dve.drain()
                    dve.tensor_scalar(var_e[:, k, :], mv[:, k, :, 1], EPS, None, ALU.add).then_inc(done, 1)

                def apply(h, k, rstd_ready, b, dst, done):
                    dve.wait_ge(rstd_ready, b + 1)
                    for t in range(2):
                        ins = dve.tensor_scalar(dst(t), h[:, t, :], mv[:, k, t, 0:1], rstd[:, k, t:t + 1],
                                                ALU.subtract, ALU.mult)
                        if t == 1:
                            ins.then_inc(done, 1)
                        else:
                            dve.drain()

                def ln1_stats(b):
                    dve.wait_ge(ln_loaded, 16 * b + 16)
                    stats(h_ln, 0, ln1_var)

                def ln1_apply(b):
                    apply(h_ln, 0, ln1_rstd, b, lambda t: xn[:, t, :], xn_ready)

                def add_res(b, first):
                    dve.wait_ge(ao_ps, b + 1)
                    dve.wait_ge(res_loaded, 16 * b + 16)
                    if not first:
                        dve.wait_ge(h_kept, 16 * b)
                    dve.tensor_tensor(h_new[:, :, :].rearrange("p t d -> p (t d)"), ps[0:TT, BM, :],
                                      h_new[:, :, :].rearrange("p t d -> p (t d)"), ALU.add).then_inc(h_done, 1)
                    dve.drain()
                    stats(h_new, 1, ln2_var)

                def ln2_apply(b, first):
                    if not first:
                        dve.wait_ge(scattered, 64 * b)
                    apply(h_new, 1, ln2_rstd, b, lambda t: pay[:, t, 0:D], x2_ready)

                def logits(b):
                    dve.wait_ge(lg_ps, b + 1)
                    dve.tensor_tensor(lg[:, :, :], ps[0:TT, BM, 0:2 * E].rearrange("p (t e) -> p t e", e=E),
                                      rb[:, :, :].broadcast_to([TT, 2, E]), ALU.add)
                    dve.drain()
                    dve.tensor_reduce(small[:, 0, :], lg[:, :, :], AX.X, ALU.max)
                    dve.drain()
                    dve.tensor_tensor(lg[:, :, :], lg[:, :, :],
                                      small[:, 0, :].unsqueeze(2).broadcast_to([TT, 2, E]), ALU.subtract
                                      ).then_inc(lg_ready, 1)

                def choose(b):
                    dve.wait_ge(lg_exp, b + 1)
                    dve.tensor_reduce(small[:, 1, :], ex[:, :, :], AX.X, ALU.add)
                    dve.drain()
                    dve.reciprocal(small[:, 2, :], small[:, 1, :])
                    dve.drain()
                    dve.tensor_tensor(ex[:, :, :], ex[:, :, :],
                                      small[:, 2, :].unsqueeze(2).broadcast_to([TT, 2, E]), ALU.mult)
                    dve.drain()
                    for t in range(2):
                        dve.max(top[:, t, :], ex[:, t, :])
                    dve.drain()
                    for t in range(2):
                        dve.max_index(topi[:, t, :], top[:, t, :], ex[:, t, :])
                    dve.drain()
                    dve.tensor_copy(topf[:, :, :], topi[:, :, 0:2])
                    dve.drain()
                    for k in range(2):
                        dve.tensor_tensor(hot[:, k, :, :], iota_e[:, :, :].broadcast_to([TT, 2, E]),
                                          topf[:, :, k:k + 1].broadcast_to([TT, 2, E]), ALU.is_equal)
                    dve.drain()
                    dve.tensor_tensor(hotb[:, :, :], hot[:, 0, :, :], hot[:, 1, :, :], ALU.add).then_inc(hot_ready, 1)
                    dve.drain()
                    dve.tensor_tensor(pay[:, :, D:D + E], ex[:, :, :], hotb[:, :, :], ALU.mult)
                    dve.tensor_copy(pay[:, :, D + E], token[:, :])
                    dve.drain()
                    dve.tensor_scalar(token[:, :], token[:, :], float(S), None, ALU.add)

                def place(b):
                    dve.wait_ge(rank_ps, b + 1)
                    r = ps[0:TT, BM, 0:3 * E].rearrange("p (t e) -> p t e", e=E)
                    dve.tensor_tensor(rank[:, :, :], r[:, 0:2, :],
                                      count[0:TT, :].unsqueeze(1).broadcast_to([TT, 2, E]), ALU.add)
                    dve.drain()
                    dve.tensor_tensor(count[:, :], count[:, :], ps[:, BM, 2 * E:3 * E], ALU.add)
                    for k in range(2):
                        dve.tensor_tensor(hot[:, k, :, :], hot[:, k, :, :], rank[:, :, :], ALU.mult)
                    dve.drain()
                    for k in range(2):
                        dve.tensor_reduce(slotf[:, :, k:k + 1], hot[:, k, :, :], AX.X, ALU.add)
                    dve.drain()
                    dve.tensor_copy(slot[:, :, :], slotf[:, :, :]).then_inc(slots_ready, 1)

                for b in range(2):
                    ln1_stats(b)
                    if b:
                        dve.wait_ge(xt_ps, b)
                    ln1_apply(b)
                    if b == 0:
                        split_c(0)
                for m in range(3):
                    split_qk(m, m)
                    if m < 2:
                        for q in range(2):
                            maxima(m, q, m == 0)
                        rows_of_max(m)
                    if m == 0:
                        augment(0, 0)

                def body(b, first, last):
                    for d in range(NG):
                        n = NG * b + d
                        if not (last and d > 0):
                            if not (first and d == 0):
                                dve.wait_ge(st_ps, 2 * n)
                            split_qk(n + 3, (d + 3) % NG)
                        more = not (last and d > 1)
                        if more:
                            maxima(n + 2, 0)
                        if not (last and d == 3):
                            augment(n + 1, (d + 1) % NG)
                        if more:
                            maxima(n + 2, 1)
                            rows_of_max(n + 2)
                        if d == 0 and not last:
                            split_c(b + 1)
                        if not first:
                            if d == 0:
                                norm_o(b - 1, 0)
                            if d == 1:
                                norm_o(b - 1, 1)
                            if d == 2:
                                add_res(b - 1, False)
                        if d == 2 and not last:
                            ln1_stats(b + 2)
                        if d == 2 and not first:
                            ln2_apply(b - 1, False)
                        if d == 2 and not last:
                            dve.wait_ge(xt_ps, b + 2)
                            ln1_apply(b + 2)
                        if d == 3 and not first:
                            logits(b - 1)
                            choose(b - 1)
                            place(b - 1)

                body(0, True, False)
                with dve.Fori(1, LAST) as b:
                    body(b, False, False)
                body(LAST, False, True)
                norm_o(LAST, 0)
                norm_o(LAST, 1)
                add_res(LAST, False)
                ln2_apply(LAST, False)
                logits(LAST)
                choose(LAST)
                place(LAST)

            @block.tensor
            def _(pe):
                def project(m, g):
                    for k, bank, done in ((0, BQ, q_ps), (1, BK, k_ps)):
                        for r in range(2):
                            o = ps[:, bank, r * S:(r + 1) * S]
                            w = 2 * g + r
                            pe.matmul(o, wuh[k][:, w, :, :, :].rearrange("p a r d -> p (a r d)"), cs[:, k, :],
                                      start=True, stop=False)
                            mm = pe.matmul(o, wul[k][:, w, :, :, :].rearrange("p a r d -> p (a r d)"), cs[:, k, :],
                                           start=False, stop=True)
                        mm.then_inc(done, 1)

                def masked(bank, mask, parts):
                    both = ps[0:TT, bank, 0:2 * S].rearrange("p (k n) -> p k n", k=2)[:, :, 0:HALF]
                    pe.matmul(both, identb[0:TT, 0:TT], mask[:, :, :], start=True, stop=False,
                              skip_group_check=True)
                    for lhs, rhs, o in parts:
                        mm = pe.matmul(o, lhs, rhs, start=False, stop=True, skip_group_check=True)
                    return mm

                def scores(m, g, q):
                    for a in range(2):
                        rr = slice(a * LOW, (a + 1) * LOW)
                        mm = masked(BSC + a, mask_q, [
                            (qs[rr, g, q, 0:TT], ks[rr, g, q, 0:HALF], ps[0:TT, BSC + a, 0:HALF]),
                            (qs[rr, g, q, TT:S], ks[rr, g, q, :], ps[0:TT, BSC + a, HALF:BS])])
                    mm.then_inc(s_ps, 1)

                def scores_t(n, g, q):
                    for a in range(2):
                        rr = slice(a * LOW, (a + 1) * LOW)
                        mm = masked(BST + a, mask_k, [
                            (ks[rr, g, q, 0:TT], qs[rr, g, q, :], ps[0:TT, BST + a, 0:S]),
                            (ks[rr, g, q, TT:S], qs[rr, g, q, S - HALF:S], ps[0:TT, BST + a, S:BS])])
                    mm.then_inc(st_ps, 1)

                def values(n, g):
                    for j in range(4):
                        h = 4 * g + j
                        o = ps[32 * j:32 * j + 32, BO_, 0:S]
                        pe.matmul(o, v[:, 0, h, :], p[:, g % 2, j, 0:S], start=True, stop=False,
                                  skip_group_check=True)
                        mm = pe.matmul(o[:, S - HALF:S], v[:, 1, h, :], p[:, g % 2, j, S:BS], start=False, stop=True,
                                       skip_group_check=True)
                    mm.then_inc(pv_ps, 1)

                def turn_max(n, g):
                    for r in range(2):
                        for t in range(2):
                            mm = pe.transpose(ps[:, BQ, r * S + t * TT:r * S + (t + 1) * TT],
                                              mxt[:, t, r, :, :].rearrange("p a c -> p (a c)"), ident[0:TT, 0:TT])
                    mm.then_inc(max_ps, 1)

                def values_of(b):
                    for t in range(2):
                        o = ps[0:TT, BM, t * D:(t + 1) * D]
                        c = cs[:, 1, t * TT:(t + 1) * TT]
                        pe.matmul(o, c, wvh[:, :], start=True, stop=False)
                        mm = pe.matmul(o, c, wvl[:, :], start=False, stop=True)
                    mm.then_inc(v_ps, 1)

                def compress(b):
                    for k in range(2):
                        for c in range(DC):
                            mm = pe.matmul(ps[:, BM, k * S:(k + 1) * S],
                                           wd[:, c, k, :, :].rearrange("p r l -> p (r l)"), xnt[:, c, :],
                                           start=c == 0, stop=c == DC - 1)
                    mm.then_inc(c_ps, 1)

                def turn(src, done):
                    for c in range(DC):
                        for t in range(2):
                            mm = pe.transpose(ps[:, BM, c * S + t * TT:c * S + (t + 1) * TT],
                                              src[:, t, c * 128:(c + 1) * 128], ident[0:TT, 0:TT])
                    mm.then_inc(done, 1)

                def turn_o(t):
                    for g in range(NG):
                        mm = pe.transpose(ps[0:TT, BM, g * 128:(g + 1) * 128],
                                          os_[:, g, t * TT:(t + 1) * TT], ident[:, :])
                    mm.then_inc(turn_o_ps, 1)

                def out_proj():
                    for t in range(2):
                        for c in range(DC):
                            mm = pe.matmul(ps[0:TT, BM, t * D:(t + 1) * D], ont[:, c, t * TT:(t + 1) * TT],
                                           wo[:, c, :], start=c == 0, stop=c == DC - 1)
                    mm.then_inc(ao_ps, 1)

                def route_logits():
                    for t in range(2):
                        for c in range(DC):
                            mm = pe.matmul(ps[0:TT, BM, t * E:(t + 1) * E], x2t[:, c, t * TT:(t + 1) * TT],
                                           rw[:, c, :], start=c == 0, stop=c == DC - 1)
                    mm.then_inc(lg_ps, 1)

                def ranks():
                    o = [ps[0:TT if k < 2 else 128, BM, k * E:(k + 1) * E] for k in range(3)]
                    pe.matmul(o[0], below[:, :], hotb[:, 0, :], start=True, stop=True)
                    pe.matmul(o[1], below[:, :], hotb[:, 1, :], start=True, stop=False)
                    pe.matmul(o[1], ones[:, 0:TT], hotb[:, 0, :], start=False, stop=True)
                    pe.matmul(o[2], ones[:, :], hotb[:, 0, :], start=True, stop=False)
                    pe.matmul(o[2], ones[:, :], hotb[:, 1, :], start=False, stop=True).then_inc(rank_ps, 1)

                pe.wait_ge(xn_ready, 1)
                turn(xn, xt_ps)
                pe.wait_ge(xn_turned, 1)
                compress(0)
                pe.wait_ge(xn_ready, 2)
                pe.wait_ge(c_split, 1)
                turn(xn, xt_ps)
                for m in range(3):
                    if m:
                        pe.wait_ge(q_split, m)
                        pe.wait_ge(k_split, m)
                    project(m, m)
                    if m < 2:
                        pe.wait_ge(q_split, m + 1)
                        pe.wait_ge(k_split, m + 1)
                        for q in range(2):
                            if m or q:
                                pe.wait_ge(max_read, 2 * m + q)
                            scores(m, m, q)
                    if m == 0:
                        pe.wait_ge(max_rows, 1)
                        turn_max(0, 0)
                        pe.wait_ge(max_ps, 1)
                        pe.wait_ge(q_aug, 1)

                def body(b, first, last):
                    for d in range(NG):
                        n = NG * b + d
                        proj, ahead, turned = not (last and d > 0), not (last and d > 1), not (last and d == 3)
                        pe.wait_ge(q_aug, n + 1)
                        if not (first and d == 0):
                            pe.wait_ge(exp_done, 2 * n)
                        scores_t(n, d, 0)
                        if proj:
                            pe.wait_ge(c_split, b + 1 if d == 0 else b + 2)
                            pe.wait_ge(k_split, n + 3)
                            project(n + 3, (d + 3) % NG)
                        if ahead:
                            pe.wait_ge(k_split, n + 3)
                            pe.wait_ge(max_read, 2 * n + 4)
                            scores(n + 2, (d + 2) % NG, 0)
                        if not (first and d == 0):
                            if d == 1:
                                pe.wait_ge(v_ready, b + 1)
                            if not (first and d == 1):
                                pe.wait_ge(o_read, n - 1)
                            values(n - 1, (d - 1) % NG)
                        if d == 0:
                            if first:
                                pe.wait_ge(xn_turned, 2)
                            values_of(b)
                        pe.wait_ge(exp_done, 2 * n + 1)
                        scores_t(n, d, 1)
                        if turned:
                            pe.wait_ge(max_rows, n + 2)
                            if proj:
                                pe.wait_ge(q_split, n + 4)
                            turn_max(n + 1, (d + 1) % NG)
                        if d == 0 and not last:
                            pe.wait_ge(v_ready, b + 1)
                            pe.wait_ge(xn_turned, b + 2)
                            compress(b + 1)
                        if ahead:
                            pe.wait_ge(max_read, 2 * n + 5)
                            scores(n + 2, (d + 2) % NG, 1)
                        if not first:
                            if d == 0:
                                pe.wait_ge(o_read, NG * b)
                                if last:
                                    pe.wait_ge(v_ready, b + 1)
                                else:
                                    pe.wait_ge(c_split, b + 2)
                                turn_o(0)
                            if d == 1:
                                pe.wait_ge(o_normed, 2 * b - 1)
                                turn_o(1)
                                pe.wait_ge(o_normed, 2 * b)
                                turn(on, turn_n_ps)
                            if d == 2:
                                pe.wait_ge(on_turned, b)
                                out_proj()
                            if d == 3:
                                pe.wait_ge(x2_ready, b)
                                turn(pay, x2_ps)
                                pe.wait_ge(x2_turned, b)
                                route_logits()
                        if d == 3 and not last:
                            if first:
                                pe.wait_ge(c_split, b + 2)
                            else:
                                pe.wait_ge(lg_ready, b)
                            pe.wait_ge(xn_ready, b + 3)
                            turn(xn, xt_ps)
                        if d == 3 and not first:
                            if not last:
                                pe.wait_ge(xn_turned, b + 3)
                            else:
                                pe.wait_ge(lg_ready, b)
                            pe.wait_ge(hot_ready, b)
                            ranks()
                            pe.wait_ge(slots_ready, b)
                        elif d == 3:
                            pe.wait_ge(xn_turned, b + 3)

                body(0, True, False)
                with pe.Fori(1, LAST) as b:
                    body(b, False, False)
                body(LAST, False, True)
                pe.wait_ge(exp_done, 2 * NG * B)
                pe.wait_ge(o_read, NG * B - 1)
                values(NG * B - 1, NG - 1)
                pe.wait_ge(o_read, NG * B)
                turn_o(0)
                pe.wait_ge(o_normed, 2 * B - 1)
                turn_o(1)
                pe.wait_ge(o_normed, 2 * B)
                turn(on, turn_n_ps)
                pe.wait_ge(on_turned, B)
                out_proj()
                pe.wait_ge(x2_ready, B)
                turn(pay, x2_ps)
                pe.wait_ge(x2_turned, B)
                route_logits()
                pe.wait_ge(lg_ready, B)
                pe.wait_ge(hot_ready, B)
                ranks()


def experts(env):
    nc, ps, ident, sem = env["nc"], env["ps"], env["ident"], env["sem"]
    acc, rows, out, b2 = (env[k] for k in ("acc", "rows", "out", "b2"))
    w1s, w2s, b1s, count, region0 = (env[k] for k in ("w1s", "w2s", "b1s", "count", "region0"))
    SPARE = E * REGION
    STEPS = NTOK // ROWS + 1

    with ExitStack() as own:
        def sb(name, shape, dt):
            return own.enter_context(nc.sbuf_tensor(name, shape, dt))

        step_i = sb("step_i", [1, STEPS], I32)
        step = sb("step", [1, 1, STEPS], F32)
        tile_i = sb("tile_i", [1, W16], I32)
        tile = sb("tile", [1, W16, 1], F32)
        exp_i = sb("exp_i", [1, E], I32)
        expert = sb("expert", [1, 1, E], F32)
        over = sb("over", [1, E, STEPS], F32)
        used = sb("used", [1, E], F32)
        need = sb("need", [1, E], F32)
        ends = [sb(f"ends{k}", [1, E], F32) for k in range(2)]
        begin = sb("begin", [1, E], F32)
        base = sb("base", [1, E], F32)
        mine = sb("mine", [1, W16, E], F32)
        work = sb("work", [1, W16, E], F32)
        row_f = sb("row_f", [1, W16], F32)
        any_f = sb("any_f", [1, W16], F32)
        exp_f = sb("exp_f", [1, W16], F32)
        table = sb("table", [1, 2, W16], I32)
        part_i = sb("part_i", [128, 1], I32)
        part = sb("part", [128, 1], F32)
        padding = sb("padding", [128, PW], F32)
        pad_f = sb("pad_f", [128, E], F32)
        pad_slot = sb("pad_slot", [128, E], I32)
        b2_all = sb("b2_all", [128, E, D], F32)
        target = sb("target", [128, 1], I32)
        zero = sb("zero", [128, 1], I32)

        base_ready, pads_ready, padded, spare_out, b2_in = (
            sem("base_ready"), sem("pads_ready"), sem("padded"), sem("spare_out"), sem("b2_in"))

        with nc.Block() as block:
            @block.sync
            def _(sp):
                sp.dma_start(b2_all[:, :, :], b2.rearrange("(o e) d -> o e d", o=1).broadcast_to([128, E, D])
                             ).then_inc(b2_in, 16)
                sp.wait_ge(pads_ready, 1)
                sp.dma_start(rows[SPARE:SPARE + ROWS, :], padding[:, :]).then_inc(spare_out, 16)
                sp.wait_ge(spare_out, 16)
                sp.wait_ge(b2_in, 16)

            @block.gpsimd
            def _(pool):
                pool.iota(step_i[:, :], pattern=[[ROWS, STEPS]], base=0, channel_multiplier=0)
                pool.iota(tile_i[:, :], pattern=[[1, W16]], base=0, channel_multiplier=0)
                pool.iota(exp_i[:, :], pattern=[[1, E]], base=0, channel_multiplier=0)
                pool.iota(part_i[:, :], pattern=[[0, 1]], base=0, channel_multiplier=1)
                pool.memset(padding[:, :], 0.0)
                pool.memset(zero[:, :], 0)
                pool.drain()
                pool.nop().then_inc(base_ready, 1)
                pool.wait_ge(pads_ready, 1)
                for e in range(E):
                    pool.indirect_dma_start(
                        out=rows[:, :], out_offset=bass.IndirectOffsetOnAxis(ap=pad_slot[:, e:e + 1], axis=0),
                        in_=padding[:, :], in_offset=None).then_inc(padded, 16)
                pool.wait_ge(padded, 16 * E)

            @block.vector
            def _(dve):
                def tt(o, a, b, op):
                    dve.tensor_tensor(o, a, b, op)
                    dve.drain()

                dve.wait_ge(base_ready, 1)
                dve.tensor_copy(part[:, :], part_i[:, :])
                dve.tensor_copy(step[:, 0, :], step_i[:, :])
                dve.tensor_copy(tile[:, :, 0], tile_i[:, :])
                dve.tensor_copy(expert[:, 0, :], exp_i[:, :])
                dve.drain()
                dve.tensor_scalar(pad_f[:, :], count[:, :], part[:, 0:1], None, ALU.add)
                dve.tensor_scalar(padding[:, D + E:D + E + 1], part[:, :], float(NTOK), None, ALU.add)
                dve.drain()
                dve.tensor_copy(pad_slot[:, :], pad_f[:, :])
                dve.drain()
                dve.nop().then_inc(pads_ready, 1)
                tt(used[:, :], count[0:1, :], region0[0:1, :], ALU.subtract)
                tt(over[:, :, :], used[:, :].unsqueeze(2).broadcast_to([1, E, STEPS]),
                   step[:, :, :].broadcast_to([1, E, STEPS]), ALU.is_gt)
                dve.tensor_reduce(need[:, :], over[:, :, :], AX.X, ALU.add)
                dve.drain()
                src = need
                for k, shift in enumerate((1, 2, 4)):
                    dst = ends[k % 2]
                    dve.tensor_copy(dst[:, 0:shift], src[:, 0:shift])
                    tt(dst[:, shift:E], src[:, shift:E], src[:, 0:E - shift], ALU.add)
                    src = dst
                last = src
                tt(begin[:, :], last[:, :], need[:, :], ALU.subtract)
                dve.scalar_tensor_tensor(out=base[:, :], in0=begin[:, :], scalar=-float(ROWS), in1=region0[0:1, :],
                                         op0=ALU.mult, op1=ALU.add)
                dve.drain()
                wide = [1, W16, E]
                tt(mine[:, :, :], tile[:, :, :].broadcast_to(wide), begin[:, :].unsqueeze(1).broadcast_to(wide), ALU.is_ge)
                tt(work[:, :, :], tile[:, :, :].broadcast_to(wide), last[:, :].unsqueeze(1).broadcast_to(wide), ALU.is_lt)
                tt(mine[:, :, :], mine[:, :, :], work[:, :, :], ALU.mult)
                tt(work[:, :, :], mine[:, :, :], expert[:, :, :].broadcast_to(wide), ALU.mult)
                dve.tensor_reduce(exp_f[:, :], work[:, :, :], AX.X, ALU.add)
                dve.tensor_reduce(any_f[:, :], mine[:, :, :], AX.X, ALU.add)
                dve.drain()
                tt(work[:, :, :], mine[:, :, :], base[:, :].unsqueeze(1).broadcast_to(wide), ALU.mult)
                dve.tensor_reduce(row_f[:, :], work[:, :, :], AX.X, ALU.add)
                dve.drain()
                dve.scalar_tensor_tensor(out=tile[:, :, 0], in0=tile[:, :, 0], scalar=float(ROWS), in1=any_f[:, :],
                                         op0=ALU.mult, op1=ALU.mult)
                dve.drain()
                tt(row_f[:, :], row_f[:, :], tile[:, :, 0], ALU.add)
                dve.scalar_tensor_tensor(out=row_f[:, :], in0=any_f[:, :], scalar=-float(SPARE), in1=row_f[:, :],
                                         op0=ALU.mult, op1=ALU.add)
                dve.drain()
                dve.tensor_scalar(row_f[:, :], row_f[:, :], float(SPARE), None, ALU.add)
                dve.drain()
                dve.tensor_copy(table[:, 0, :], row_f[:, :])
                dve.tensor_copy(table[:, 1, :], exp_f[:, :])
                dve.drain()

        pay = [sb(f"tile_in{u}", [128, PW], F32) for u in range(2)]
        xs = [sb(f"xs{u}", [128, DC, 2, ROWS], BF16) for u in range(2)]
        hg = [sb(f"hg{u}", [128, FC, ROWS], F32) for u in range(2)]
        hs = [sb(f"hs{u}", [128, FC, 2, ROWS], BF16) for u in range(2)]
        yt = [sb(f"yt{u}", [128, D], F32) for u in range(2)]
        gate = [sb(f"gate{u}", [128, 1], F32) for u in range(2)]
        tokf = [sb(f"tokf{u}", [128, 1], F32) for u in range(2)]
        toki = [sb(f"toki{u}", [128, 1], I32) for u in range(2)]

        rows_in = [sem(f"rows_in{u}") for u in range(2)]
        xt_ps, x_high, x_split, meta_read = sem("rt_ps"), sem("x_high"), sem("x_split"), sem("meta_read")
        h_ps, h_act, h_high, h_split = sem("f1_ps"), sem("h_act"), sem("h_high"), sem("h_split")
        y_ps, y_ready, y_added = sem("y_ps"), sem("y_ready"), sem("y_added")
        out_done = sem("out_done")
        BT, BH, BY = 0, 1, 5
        HB = FC // 2

        with nc.Block() as block:
            @block.sync
            def _(sp):
                def load(i, u):
                    r = sp.value_load(table[0:1, 0, bass.ds(i, 1)], min_val=0, max_val=SPARE)
                    sp.dma_start(pay[u][:, :], rows[bass.ds(r, ROWS), :]).then_inc(rows_in[u], 16)

                load(0, 0)
                load(1, 1)
                with sp.Fori(0, NTILE // 2 - 1) as k:
                    for u in range(2):
                        sp.wait_ge(xt_ps, 2 * k + u + 1)
                        sp.wait_ge(meta_read, 2 * k + u + 1)
                        load(2 * k + u + 2, u)
                sp.wait_ge(y_added, 16 * NTILE)
                sp.dma_start(out.rearrange("b s d -> (b s d)").rearrange("(q n) -> q n", q=128),
                             acc[0:NTOK, :].rearrange("t d -> (t d)").rearrange("(q n) -> q n", q=128)
                             ).then_inc(out_done, 16)
                sp.wait_ge(out_done, 16)

            @block.scalar
            def _(act):
                def high_x(i, u):
                    act.wait_ge(xt_ps, i + 1)
                    act.copy(xs[u][:, :, 0, :], ps[:, BT, 0:DC * ROWS].rearrange("p (c n) -> p c n", c=DC)
                             ).then_inc(x_high, 1)

                def gelu(i, u):
                    e = act.value_load(table[0:1, 1, bass.ds(i, 1)], min_val=0, max_val=E - 1)
                    for j in range(FC):
                        if j % HB == 0:
                            act.wait_ge(h_ps, 2 * i + j // HB + 1)
                        ins = act.activation(hg[u][:, j, :],
                                             ps[:, BH + 2 * u + j // HB, (j % HB) * ROWS:(j % HB + 1) * ROWS],
                                             ACT.Gelu, bias=b1s[:, bass.ds(e, 1), j])
                        if j % HB == HB - 1:
                            ins.then_inc(h_act, 1)

                high_x(0, 0)
                gelu(0, 0)
                high_x(1, 1)

                def step_(k, u, first, more):
                    i = 2 * k + u
                    if u == 0 or more:
                        if not first:
                            act.wait_ge(h_split, 2 * i)
                        gelu(i + 1, 1 - u)
                    if more:
                        high_x(i + 2, u)

                step_(0, 0, True, True)
                step_(0, 1, False, True)
                with act.Fori(1, NTILE // 2 - 1) as k:
                    step_(k, 0, False, True)
                    step_(k, 1, False, True)
                step_(NTILE // 2 - 1, 0, False, False)

            @block.vector
            def _(dve):
                def low_x(i, u):
                    dve.wait_ge(x_high, i + 1)
                    dve.tensor_tensor(xs[u][:, :, 1, :], ps[:, BT, 0:DC * ROWS].rearrange("p (c n) -> p c n", c=DC),
                                      xs[u][:, :, 0, :], ALU.subtract).then_inc(x_split, 1)

                def meta(i, u):
                    e = dve.value_load(table[0:1, 1, bass.ds(i, 1)], min_val=0, max_val=E - 1)
                    dve.wait_ge(rows_in[u], 8 * i + 16 - 8 * u)
                    dve.tensor_copy(gate[u][:, :], pay[u][:, bass.ds(e + D, 1)])
                    dve.tensor_copy(tokf[u][:, :], pay[u][:, D + E:D + E + 1]).then_inc(meta_read, 1)

                def split_h(i, u):
                    for q in range(2):
                        a, b = q * HB, (q + 1) * HB
                        dve.wait_ge(h_act, 2 * i + q + 1)
                        dve.tensor_copy(hs[u][:, a:b, 0, :], hg[u][:, a:b, :]).then_inc(h_high, 1)
                        dve.wait_ge(h_high, 2 * i + q + 1)
                        dve.tensor_tensor(hs[u][:, a:b, 1, :], hg[u][:, a:b, :], hs[u][:, a:b, 0, :],
                                          ALU.subtract).then_inc(h_split, 1)

                def result(i, u, first):
                    e = dve.value_load(table[0:1, 1, bass.ds(i, 1)], min_val=0, max_val=E - 1)
                    dve.wait_ge(y_ps, i + 1)
                    if not first:
                        dve.wait_ge(y_added, 16 * i - 16)
                    dve.tensor_copy(toki[u][:, :], tokf[u][:, :])
                    dve.tensor_tensor(yt[u][:, :], ps[:, BY + u, 0:D], b2_all[:, bass.ds(e, 1), :].rearrange("p o d -> p (o d)"), ALU.add)
                    dve.drain()
                    dve.tensor_scalar(yt[u][:, :], yt[u][:, :], gate[u][:, 0:1], None, ALU.mult).then_inc(y_ready, 1)

                low_x(0, 0)
                meta(0, 0)
                split_h(0, 0)
                low_x(1, 1)
                meta(1, 1)

                def step_(k, u, first, more):
                    i = 2 * k + u
                    if u == 0 or more:
                        if not first:
                            dve.wait_ge(y_ps, i)
                        split_h(i + 1, 1 - u)
                    if more:
                        low_x(i + 2, u)
                    result(i, u, first)
                    if more:
                        dve.drain()
                        meta(i + 2, u)

                step_(0, 0, True, True)
                step_(0, 1, True, True)
                with dve.Fori(1, NTILE // 2 - 1) as k:
                    step_(k, 0, False, True)
                    step_(k, 1, False, True)
                step_(NTILE // 2 - 1, 0, False, False)
                step_(NTILE // 2 - 1, 1, False, False)

            @block.gpsimd
            def _(pool):
                def add(i, u, first):
                    if not first:
                        pool.wait_ge(y_added, 16 * i)
                    pool.wait_ge(y_ready, i + 1)
                    pool.tensor_tensor(target[:, :], toki[u][:, :], zero[:, :], ALU.add)
                    pool.drain()
                    pool.indirect_dma_start(
                        out=acc[:, :], out_offset=bass.IndirectOffsetOnAxis(ap=target[:, :], axis=0),
                        in_=yt[u][:, :], in_offset=None, compute_op=ALU.add).then_inc(y_added, 16)

                add(0, 0, True)
                add(1, 1, False)
                with pool.Fori(1, NTILE // 2) as k:
                    for u in range(2):
                        add(2 * k + u, u, False)

            @block.tensor
            def _(pe):
                def turn(i, u):
                    pe.wait_ge(rows_in[u], 8 * i + 16 - 8 * u)
                    for c in range(DC):
                        mm = pe.transpose(ps[:, BT, c * ROWS:(c + 1) * ROWS], pay[u][:, c * 128:(c + 1) * 128],
                                          ident[:, :])
                    mm.then_inc(xt_ps, 1)

                def up(i, u, first=True):
                    e = pe.value_load(table[0:1, 1, bass.ds(i, 1)], min_val=0, max_val=E - 1)
                    if not first:
                        pe.wait_ge(h_act, 2 * i - 2)
                    pe.wait_ge(x_split, i + 1)
                    for j in range(FC):
                        o = ps[:, BH + 2 * u + j // HB, (j % HB) * ROWS:(j % HB + 1) * ROWS]
                        n = 0
                        for c in range(DC):
                            for wp, xp in ((0, 0), (0, 1), (1, 0)):
                                w = w1s[:, bass.ds(e, 1), c, wp, j * 128:(j + 1) * 128].rearrange("p o f -> p (o f)")
                                mm = pe.matmul(o, w, xs[u][:, c, xp, :], start=n == 0, stop=n == 3 * DC - 1)
                                n += 1
                        if j % HB == HB - 1:
                            mm.then_inc(h_ps, 1)

                def down(i, u, first):
                    e = pe.value_load(table[0:1, 1, bass.ds(i, 1)], min_val=0, max_val=E - 1)
                    if not first:
                        pe.wait_ge(y_ready, i - 1)
                    for j in range(FC):
                        if j % HB == 0:
                            pe.wait_ge(h_split, 2 * i + j // HB + 1)
                        for hp, wp in ((0, 0), (0, 1), (1, 0)):
                            w = w2s[:, bass.ds(e, 1), j, wp, :].rearrange("p o d -> p (o d)")
                            mm = pe.matmul(ps[:, BY + u, 0:D], hs[u][:, j, hp, :], w,
                                           start=j == 0 and hp == 0 and wp == 0, stop=j == FC - 1 and hp == 1)
                    mm.then_inc(y_ps, 1)

                turn(0, 0)
                up(0, 0)
                turn(1, 1)

                def step_(k, u, first, more):
                    i = 2 * k + u
                    if u == 0 or more:
                        up(i + 1, 1 - u, first)
                    if more:
                        turn(i + 2, u)
                    down(i, u, first)

                step_(0, 0, True, True)
                step_(0, 1, True, True)
                with pe.Fori(1, NTILE // 2 - 1) as k:
                    step_(k, 0, False, True)
                    step_(k, 1, False, True)
                step_(NTILE // 2 - 1, 0, False, False)
                step_(NTILE // 2 - 1, 1, False, False)


_INS = ["x", "L0_tok_W_h", "L0_tok_b_h", "L0_tok_W_o", "L0_tok_b_o", "L0_tok_W_r", "L0_tok_b_r",
        "L0_attn_W_dq", "L0_attn_W_uq", "L0_attn_W_dkv", "L0_attn_W_uk", "L0_attn_W_uv", "L0_attn_W_o",
        "L0_ffn_router_w", "L0_ffn_router_b", "L0_ffn_w1", "L0_ffn_b1", "L0_ffn_w2", "L0_ffn_b2"]


def kernel(**inputs):
    import numpy as _np
    import concourse.bacc as _bacc
    from concourse.bass_utils import run_bass_kernel_spmd as _run

    nc = _bacc.Bacc("TRN2", target_bir_lowering=False, num_devices=1)
    arrays, args = {}, []
    for name in _INS:
        a = _np.ascontiguousarray(inputs[name])
        arrays[f"in_{name}"] = a
        args.append(nc.dram_tensor(f"in_{name}", a.shape, mybir.dt.from_np(a.dtype), kind="ExternalInput").ap())
    args.append(nc.dram_tensor("out_0", (B, S, D), F32, kind="ExternalOutput").ap())
    build(nc, *args)
    r = _run(nc, [arrays], core_ids=[0])
    return r.results[0]["out_0"]
```

```python
from contextlib import ExitStack

import concourse.bass as bass
from concourse import mybir

F32 = mybir.dt.float32
F32R = mybir.dt.float32r
BF16 = mybir.dt.bfloat16
I32 = mybir.dt.int32
U32 = mybir.dt.uint32
ALU = mybir.AluOpType
ACT = mybir.ActivationFunctionType
AX = mybir.AxisListType

B, L = 16, 4000
PATCH = 16
S = L // PATCH
TT = S // 2
NT = B * S // TT
NTOK = B * S
D = 256
DC = D // 128
I = 512
IC = I // 128
H, DK = 16, 16
LOW = 64
NG = H // 4
E, F, TOPK = 8, 1024, 2
FC = F // 128
EPS = 1e-5
NEG = -1e30
SCALE = float(DK) ** -0.5
XT_TERMS = 6 * PATCH
KX = XT_TERMS + 3
ROWS = 256
RP = ROWS // 128
REGION = 4256
NTILE = (NTOK * TOPK + E * (ROWS - 1)) // ROWS
PW = 272
W16 = NTILE + 2


def build(nc, x, W_h, b_h, tW_o, b_o, W_r, b_r, W_dq, W_uq, W_dkv, W_uk, W_uv, aW_o,
          router_w, router_b, w1, b1, w2, b2, out):
    with ExitStack() as ctx:
        def sem(name):
            return ctx.enter_context(nc.semaphore(name))

        def sb(name, shape, dt, c=ctx):
            return c.enter_context(nc.sbuf_tensor(name, shape, dt))

        acc = nc.dram_tensor("acc", (NTOK + ROWS, D), F32, kind="Internal").ap()
        rows = nc.dram_tensor("rows", (E * REGION + ROWS, PW), F32, kind="Internal").ap()

        ps = ctx.enter_context(nc.psum_tensor("ps", [128, 8, 512], F32))

        w1s = sb("w1s", [128, E, DC, 2, F], BF16)
        w2s = sb("w2s", [128, E, FC, 2, D], BF16)
        b1s = sb("b1s", [128, E, FC], F32)
        ident = sb("ident", [128, 128], F32)
        identb = sb("identb", [128, 128], BF16)
        count = sb("count", [128, E], F32)
        region0 = sb("region0", [128, E], F32)

        env = dict(locals())
        tokenizer(env, ctx)
        attention(env)
        experts(env)


def tokenizer(env, ctx):
    nc, ps, ident, identb = env["nc"], env["ps"], env["ident"], env["identb"]
    x, W_h, b_h, tW_o, b_o, W_r, b_r = (env[k] for k in ("x", "W_h", "b_h", "tW_o", "b_o", "W_r", "b_r"))
    acc, w1, w2, b1, w1s, w2s, b1s = (env[k] for k in ("acc", "w1", "w2", "b1", "w1s", "w2s", "b1s"))
    sem = env["sem"]
    NJ = IC + DC
    with ExitStack() as own:
        def sb(name, shape, dt):
            return own.enter_context(nc.sbuf_tensor(name, shape, dt))

        xin = sb("xin", [TT, NT, PATCH], F32)
        xres = sb("xres", [TT, NT, PATCH], F32)
        xst = sb("xst", [TT, NT, KX], BF16)
        win = sb("win", [128, NJ, 2 * PATCH], F32)
        wres = sb("wres", [128, NJ, PATCH], F32)
        wst = sb("wst", [128, NJ, KX], BF16)
        bin_ = sb("bin", [128, NJ], F32)
        bout = sb("bout", [128, DC], F32)
        bsum = sb("bsum", [128, NJ], F32)
        bres = sb("bres", [128, NJ], F32)
        won = sb("won", [128, DC, I], F32)
        xt = sb("xt", [KX, NT * TT], BF16)
        wt = sb("wt", [KX, NJ * 128], BF16)
        wot = sb("wot", [128, IC, D], F32)
        zrow = sb("zrow", [128, RP, D], F32)
        hid = [sb(f"hid{u}", [128, IC, S], F32) for u in range(2)]
        hout = [sb(f"hout{u}", [TT, 2, D], F32) for u in range(2)]
        wraw = [sb(f"wraw{u}", [128, 2 * F], F32) for u in range(2)]

        x_in, w_in, won_in, consts = sem("x_in"), sem("w_in"), sem("won_in"), sem("consts")
        id_zero, ident_ready = sem("id_zero"), sem("ident_ready")
        xst_ready, wst_ready = sem("xst_ready"), sem("wst_ready")
        xt_ps, wt_ps, won_ps, turned = sem("xt_ps"), sem("wt_ps"), sem("won_ps"), sem("turned")
        turned_act = sem("turned_act")
        zero_out, b1_in = sem("zero_out"), sem("b1_in")

        def split3(dve, src, rest, dst, terms):
            for k in range(3):
                first = terms[k][0]
                dve.tensor_copy(dst(first), src if k == 0 else rest)
                dve.drain()
                for t in terms[k][1:]:
                    dve.tensor_copy(dst(t), dst(first))
                if k < 2:
                    dve.tensor_tensor(rest, src if k == 0 else rest, dst(first), ALU.subtract)
                dve.drain()

        with nc.Block() as block:
            @block.sync
            def _(sp):
                sp.dma_start(xin[:, :, :], x.rearrange("b (t p i) -> p (b t) i", p=TT, i=PATCH)).then_inc(x_in, 16)
                sp.dma_start(win[:, 0:IC, :], W_h.rearrange("(c p) f -> p c f", p=128)).then_inc(w_in, 16)
                sp.dma_start(win[:, IC:NJ, :], W_r.rearrange("(c p) f -> p c f", p=128)).then_inc(w_in, 16)
                with nc.allow_non_contiguous_dma(reason="biases, once"):
                    sp.dma_start(bin_[:, 0:IC], b_h.rearrange("(c p) -> p c", p=128)).then_inc(w_in, 16)
                    sp.dma_start(bin_[:, IC:NJ], b_r.rearrange("(c p) -> p c", p=128)).then_inc(w_in, 16)
                    sp.dma_start(bout[:, :], b_o.rearrange("(c p) -> p c", p=128)).then_inc(w_in, 16)
                sp.dma_start(won[:, :, :], tW_o.rearrange("(c p) i -> p c i", p=128)).then_inc(won_in, 16)
                sp.wait_ge(consts, 1)
                sp.dma_start(acc[NTOK:NTOK + ROWS, :].rearrange("(t p) d -> p t d", p=128), zrow[:, :, :]).then_inc(zero_out, 16)
                sp.wait_ge(zero_out, 16)

            @block.scalar
            def _(act):
                with nc.allow_non_contiguous_dma(reason="biases, once"):
                    for e in range(E):
                        act.dma_start(b1s[:, e, :], b1[e, :].rearrange("(c p) -> p c", p=128)).then_inc(b1_in, 16)
                act.wait_ge(b1_in, 16 * E)
                for k in range(2):
                    act.wait_ge(won_ps, k + 1)
                    act.copy(wot[:, 2 * k:2 * k + 2, :].rearrange("p c n -> p (c n)"),
                             ps[:, 5 + k, :]).then_inc(turned_act, 1)

            @block.gpsimd
            def _(pool):
                pool.memset(ident[:, :], 0.0).then_inc(id_zero, 1)
                pool.memset(identb[:, :], 0.0).then_inc(id_zero, 1)
                pool.memset(zrow[:, :, :], 0.0).then_inc(consts, 1)
                pool.wait_ge(id_zero, 2)
                for m in (ident, identb):
                    pool.affine_select(out=m[:, :], in_=m[:, :], compare_op=ALU.not_equal, fill=1.0, base=0,
                                       pattern=[[-1, 128]], channel_multiplier=1).then_inc(ident_ready, 1)

            @block.vector
            def _(dve):
                dve.memset(xst[:, :, XT_TERMS:KX], 1.0)
                dve.wait_ge(w_in, 80)
                dve.tensor_reduce(bsum[:, :], win[:, :, PATCH:2 * PATCH], AX.X, ALU.add)
                dve.drain()
                dve.tensor_tensor(bsum[:, :], bsum[:, :], bin_[:, :], ALU.add)
                dve.drain()
                dve.tensor_tensor(bsum[:, IC:NJ], bsum[:, IC:NJ], bout[:, :], ALU.add)
                dve.drain()
                split3(dve, win[:, :, 0:PATCH], wres[:, :, :],
                       lambda t: wst[:, :, t * PATCH:(t + 1) * PATCH], [[0, 3, 5], [1, 4], [2]])
                split3(dve, bsum[:, :], bres[:, :], lambda t: wst[:, :, XT_TERMS + t], [[0], [1], [2]])
                dve.nop().then_inc(wst_ready, 1)
                dve.wait_ge(x_in, 16)
                split3(dve, xin[:, :, :], xres[:, :, :],
                       lambda t: xst[:, :, t * PATCH:(t + 1) * PATCH], [[0, 1, 2], [3, 4], [5]])
                dve.nop().then_inc(xst_ready, 1)
                dve.wait_ge(wt_ps, 1)
                dve.tensor_copy(wt[:, :], ps[0:KX, 4, :].bitcast(BF16)[:, 0:NJ * 128]).then_inc(turned, 1)
                for k in range(4):
                    dve.wait_ge(xt_ps, k + 1)
                    dve.tensor_copy(xt[:, k * 8 * TT:(k + 1) * 8 * TT].rearrange("k (t n) -> k t n", n=TT),
                                    ps[0:KX, k, :].bitcast(BF16).rearrange("k (t n) -> k t n", n=128)[:, :, 0:TT]
                                    ).then_inc(turned, 1)

            @block.tensor
            def _(pe):
                pe.wait_ge(ident_ready, 2)
                pe.wait_ge(won_in, 16)
                for k in range(2):
                    for q in range(4):
                        c, n = 2 * k + q // 2, q % 2
                        mm = pe.transpose(ps[:, 5 + k, q * 128:(q + 1) * 128],
                                          won[:, n, c * 128:(c + 1) * 128], ident[:, :])
                    mm.then_inc(won_ps, 1)
                pe.wait_ge(wst_ready, 1)
                for c in range(NJ):
                    mm = pe.transpose(ps[0:KX, 4, :].bitcast(BF16)[:, c * 128:(c + 1) * 128],
                                      wst[:, c, :], identb[:, :])
                mm.then_inc(wt_ps, 1)
                pe.wait_ge(xst_ready, 1)
                for t in range(NT):
                    mm = pe.transpose(ps[0:KX, t // 8, :].bitcast(BF16)[:, (t % 8) * 128:(t % 8) * 128 + TT],
                                      xst[:, t, :], identb[0:TT, 0:TT])
                    if t % 8 == 7:
                        mm.then_inc(xt_ps, 1)

        hid_ps, hid_ready, hid_used = sem("hid_ps"), sem("hid_ready"), sem("hid_used")
        h_ps, h_ready = sem("h_ps"), sem("h_ready")
        h_stored = [sem(f"h_stored{u}") for u in range(2)]
        w_loaded = [sem(f"w_loaded{u}") for u in range(2)]
        w_high, w_low = sem("w_high"), sem("w_low")

        with nc.Block() as block:
            @block.sync
            def _(sp):
                def load_w(e, u):
                    src = (w1 if u == 0 else w2)[bass.ds(e, 1), :, :]
                    src = src.rearrange("o (c p) n -> p (o c) n", p=128)
                    sp.dma_start(wraw[u][:, :].rearrange("p (c n) -> p c n", c=DC if u == 0 else FC),
                                 src).then_inc(w_loaded[u], 16)

                load_w(0, 0)
                load_w(0, 1)

                def pair(e, first, last):
                    for u in range(2):
                        if not last:
                            sp.wait_ge(w_high, 2 * e + u + 1)
                            sp.wait_ge(w_low, 2 * e + u + 1)
                            load_w(e + 1, u)
                    for u in range(2):
                        sp.wait_ge(h_ready, 2 * e + u + 1)
                        sp.dma_start(acc[bass.ds((2 * e + u) * S, S), :].rearrange("(t p) d -> p t d", p=TT),
                                     hout[u][:, :, :]).then_inc(h_stored[u], 16)

                with sp.Fori(0, E - 1) as e:
                    pair(e, False, False)
                pair(E - 1, False, True)
                for u in range(2):
                    sp.wait_ge(h_stored[u], 16 * E)

            @block.scalar
            def _(act):
                def pair(e, first):
                    for u in range(2):
                        act.wait_ge(hid_ps, 2 * e + u + 1)
                        if not first:
                            act.wait_ge(hid_used, 2 * e + u - 1)
                        act.activation(hid[u][:, :, :].rearrange("p (k c) n -> p k (c n)", k=2),
                                       ps[:, 2 * u:2 * u + 2, 0:2 * S], ACT.Silu).then_inc(hid_ready, 1)
                        act.wait_ge(w_loaded[u], (e + 1) * 16)
                        ws, c = (w1s, DC) if u == 0 else (w2s, FC)
                        act.copy(ws[:, bass.ds(e, 1), :, 0, :].rearrange("p o c n -> p (o c) n"),
                                 wraw[u][:, :].rearrange("p (c n) -> p c n", c=c)).then_inc(w_high, 1)

                pair(0, True)
                with act.Fori(1, E) as e:
                    pair(e, False)

            @block.vector
            def _(dve):
                def pair(e, first):
                    for u in range(2):
                        dve.wait_ge(h_ps, 2 * e + u + 1)
                        if not first:
                            dve.wait_ge(h_stored[u], 16 * e)
                        dve.tensor_copy(hout[u][:, :, :].rearrange("p t d -> p (t d)"),
                                        ps[0:TT, 4 + u, :]).then_inc(h_ready, 1)
                    for u in range(2):
                        dve.wait_ge(w_high, 2 * e + u + 1)
                        ws, c = (w1s, DC) if u == 0 else (w2s, FC)
                        dve.tensor_tensor(ws[:, bass.ds(e, 1), :, 1, :].rearrange("p o c n -> p (o c) n"),
                                          wraw[u][:, :].rearrange("p (c n) -> p c n", c=c),
                                          ws[:, bass.ds(e, 1), :, 0, :].rearrange("p o c n -> p (o c) n"),
                                          ALU.subtract).then_inc(w_low, 1)

                pair(0, True)
                with dve.Fori(1, E) as e:
                    pair(e, False)

            @block.tensor
            def _(pe):
                def pair(e, first):
                    for u in range(2):
                        for c in range(IC):
                            mm = pe.matmul(ps[:, 2 * u + c // 2, (c % 2) * S:(c % 2 + 1) * S],
                                           wt[:, c * 128:(c + 1) * 128],
                                           xt[:, bass.ds((2 * e + u) * S, S)], start=True, stop=True)
                        mm.then_inc(hid_ps, 1)
                    for u in range(2):
                        if not first:
                            pe.wait_ge(h_ready, 2 * e + u - 1)
                        for t in range(2):
                            o = ps[0:TT, 4 + u, t * D:(t + 1) * D]
                            pe.matmul(o, xt[:, bass.ds((2 * e + u) * S + t * TT, TT)],
                                      wt[:, IC * 128:NJ * 128], start=True, stop=False)
                            if t == 0:
                                pe.wait_ge(hid_ready, 2 * e + u + 1)
                            for c in range(IC):
                                mm = pe.matmul(o, hid[u][:, c, t * TT:(t + 1) * TT], wot[:, c, :],
                                               start=False, stop=c == IC - 1)
                        mm.then_inc(h_ps, 1)
                        pe.nop().then_inc(hid_used, 1)

                pair(0, True)
                with pe.Fori(1, E) as e:
                    pair(e, False)


def attention(env):
    nc, ps, ident, identb, sem = env["nc"], env["ps"], env["ident"], env["identb"], env["sem"]
    W_dq, W_uq, W_dkv, W_uk, W_uv, aW_o = (env[k] for k in ("W_dq", "W_uq", "W_dkv", "W_uk", "W_uv", "aW_o"))
    router_w, router_b, acc, rows = (env[k] for k in ("router_w", "router_b", "acc", "rows"))
    count, region0 = env["count"], env["region0"]
    HALF = TT + 1
    BS = HALF + S
    MAXROW = 3 * DK
    BQ, BK, BSC, BST, BO_, BM = 0, 1, 2, 4, 6, 7
    BR = BS + 2 * E
    LAST = B - 1

    with ExitStack() as own:
        def sb(name, shape, dt):
            return own.enter_context(nc.sbuf_tensor(name, shape, dt))

        wd = sb("wd", [128, DC, 2, 2, LOW], F32)
        wuh = [sb(f"wuh{k}", [128, H // 2, 2, 4, DK], F32R) for k in range(2)]
        wul = [sb(f"wul{k}", [128, H // 2, 2, 4, DK], F32R) for k in range(2)]
        wvh, wvl = sb("wvh", [128, D], F32R), sb("wvl", [128, D], F32R)
        wo = sb("wo", [128, DC, D], F32)
        rw = sb("rw", [128, DC, E], F32)
        rb = sb("rb", [TT, 1, E], F32)
        ccol = sb("ccol", [128, 4], F32)
        s_q, s_k, s_c, k_one = (ccol[:, j:j + 1] for j in range(4))
        mask_q = sb("mask_q", [TT, 2, HALF], BF16)
        mask_k = sb("mask_k", [TT, 2, HALF], BF16)
        below = sb("below", [TT, TT], BF16)
        ones = sb("ones", [TT, 128], BF16)
        iota_i = sb("iota_i", [TT, E], I32)
        iota_e = sb("iota_e", [TT, 1, E], F32)
        tok_i = sb("tok_i", [TT, 2], I32)
        token = sb("token", [TT, 2], F32)
        reg_i = sb("reg_i", [128, E], I32)
        minus_half = sb("minus_half", [TT, 2], F32)
        h_ln = sb("h_ln", [TT, 2, D], F32)
        h_new = sb("h_new", [TT, 2, D], F32)
        st6 = sb("st6", [TT, 2, 2, 6], F32)
        mv = sb("mv", [TT, 2, 2, 2], F32)
        var_e = sb("var_e", [TT, 2, 2], F32)
        rstd = sb("rstd", [TT, 2, 2], F32)
        less_mean = sb("less_mean", [TT, 2, 2], F32)
        shift = sb("shift", [TT, 2, 2], F32)
        xn = sb("xn", [TT, 2, D], F32)
        xnt = sb("xnt", [128, DC, S], F32)
        cs = sb("cs", [128, 2, S], F32R)
        q_r, k_r = sb("q_r", [128, 2, S], F32R), sb("k_r", [128, 2, S], F32R)
        c_r = q_r
        qs = sb("qs", [128, NG, 2, S], F32R)
        ks = sb("ks", [128, NG, 2, S], F32R)
        v = sb("v", [TT, 2, H, DK + 1], F32)
        mx = sb("mx", [TT, 2, 4], F32)
        mxt = sb("mxt", [TT, 2, 2, 2, LOW], F32)
        p_all = sb("p", [128, 2, 4, BS], F32)
        p = p_all[0:TT]
        setup_part = p_all[:, :, :, :].rearrange("p a h n -> p (a h n)")
        wu = setup_part[:, 0:3 * D].rearrange("p (k n) -> p k n", n=D)
        crow = setup_part[0:1, 3 * D:3 * D + 512].rearrange("p (k n) -> p k n", n=128)
        os_ = sb("os", [128, NG, S], F32)
        rden = sb("rden", [TT, 2, H], F32)
        on = xn
        ont = xnt
        x2t = sb("x2t", [128, DC, S], F32)
        pay = sb("pay", [TT, 2, PW], F32)
        lg = sb("lg", [TT, 2, E], F32)
        lgx = sb("lgx", [TT, 2, E], F32)
        ex = sb("ex", [TT, 2, E], F32)
        small = sb("small", [TT, 4, 2], F32)
        top = sb("top", [TT, 2, 8], F32)
        topi = sb("topi", [TT, 2, 8], U32)
        topf = sb("topf", [TT, 2, 2], F32)
        hot = sb("hot", [TT, 2, 2, E], F32)
        hotb = sb("hotb", [TT, 2, E], BF16)
        rank = sb("rank", [TT, 2, E], F32)
        slotf = sb("slotf", [TT, 2, 2], F32)
        slot = sb("slot", [TT, 2, 2], I32)

        bw_in, rb_in, ccol_in = sem("bw_in"), sem("rb_in"), sem("ccol_in")
        zeroed, consts_ready, crow_ready, weights_split = (
            sem("zeroed"), sem("consts_ready"), sem("crow_ready"), sem("weights_split"))

        with nc.Block() as block:
            @block.sync
            def _(sp):
                for c in range(DC):
                    for k, w in enumerate((W_dq, W_dkv)):
                        for r in range(2):
                            sp.dma_start(wd[:, c, k, r, :], w[c * 128:(c + 1) * 128, :]).then_inc(bw_in, 16)
                for k, w in enumerate((W_uq, W_uk, W_uv)):
                    for r in range(2):
                        sp.dma_start(wu[r * LOW:(r + 1) * LOW, k, :], w).then_inc(bw_in, 16)
                sp.dma_start(wo[:, :, :], aW_o.rearrange("(c p) n -> p c n", p=128)).then_inc(bw_in, 16)
                sp.dma_start(rw[:, :, :], router_w.rearrange("(c p) n -> p c n", p=128)).then_inc(bw_in, 16)
                sp.dma_start(rb[:, 0, :], router_b.rearrange("(o e) -> o e", o=1).broadcast_to([TT, E])).then_inc(rb_in, 16)
                sp.wait_ge(crow_ready, 1)
                with nc.allow_non_contiguous_dma(reason="512 factors, once"):
                    for j in range(4):
                        sp.dma_start(ccol[:, j:j + 1], crow[0:1, j, :]).then_inc(ccol_in, 16)
                sp.wait_ge(ccol_in, 64)

            @block.gpsimd
            def _(pool):
                for m in (mask_q, mask_k, ones):
                    pool.memset(m[:, :] if m is ones else m[:, :, :], 1.0 if m is ones else 0.0)
                pool.memset(below[:, :], 1.0)
                pool.memset(mxt[:, :, :, :, :], 0.0)
                pool.memset(v[:, :, :, :], 0.0)
                pool.memset(minus_half[:, :], -0.5)
                pool.memset(pay[:, :, :], 0.0)
                pool.iota(iota_i[:, :], pattern=[[1, E]], base=0, channel_multiplier=0)
                pool.iota(tok_i[:, :], pattern=[[TT, 2]], base=0, channel_multiplier=1)
                pool.iota(reg_i[:, :], pattern=[[REGION, E]], base=0, channel_multiplier=0)
                pool.drain()
                pool.affine_select(out=mask_q[:, :, :], in_=mask_q[:, :, :], compare_op=ALU.is_ge, fill=NEG, base=0,
                                   pattern=[[1, 2], [-1, HALF]], channel_multiplier=1)
                pool.affine_select(out=mask_k[:, :, :], in_=mask_k[:, :, :], compare_op=ALU.is_ge, fill=NEG, base=0,
                                   pattern=[[-1, 2], [1, HALF]], channel_multiplier=-1)
                pool.affine_select(out=below[:, :], in_=below[:, :], compare_op=ALU.is_gt, fill=0.0, base=0,
                                   pattern=[[1, TT]], channel_multiplier=-1)
                pool.memset(v[:, :, :, DK:DK + 1], 1.0)
                pool.tensor_copy(iota_e[:, 0, :], iota_i[:, :])
                pool.tensor_copy(token[:, :], tok_i[:, :])
                pool.tensor_copy(region0[:, :], reg_i[:, :])
                pool.tensor_copy(count[:, :], reg_i[:, :])
                pool.drain()

            @block.vector
            def _(dve):
                dve.memset(ps[:, BO_, 0:S], 0.0)
                dve.memset(crow[:, :, :], 0.0)
                for w in (*wuh, *wul):
                    dve.memset(w[:, :, :, :, :].bitcast(F32), 0.0)
                dve.memset(wvl[:, :].bitcast(F32), 0.0)
                dve.drain()
                for a in range(2):
                    o = a * LOW
                    dve.memset(crow[:, 0, o + DK:o + 2 * DK], -1.0)
                    dve.memset(crow[:, 1, o + 2 * DK:o + 3 * DK], -1.0)
                    dve.memset(crow[:, 1, o + MAXROW:o + MAXROW + 2], 1.0)
                    dve.memset(crow[:, 3, o + MAXROW:o + MAXROW + 2], 1.0)
                dve.memset(crow[:, 2, LOW:128], -1.0)
                dve.drain()
                dve.nop().then_inc(crow_ready, 1)
                dve.wait_ge(bw_in, 16 * (4 * DC + 8))
                for k in range(2):
                    src = wu[:, k, :].rearrange("p (h a d) -> p h a d", a=2, d=DK)
                    for r in range(3):
                        dve.tensor_copy(wuh[k][:, :, :, r, :], src)
                    dve.drain()
                    for r in range(3):
                        dve.tensor_tensor(wul[k][0:LOW, :, :, r, :], src[0:LOW], wuh[k][0:LOW, :, :, 0, :],
                                          ALU.subtract)
                dve.tensor_copy(wvh[:, :], wu[:, 2, :])
                dve.drain()
                dve.tensor_tensor(wvl[0:LOW, :], wu[0:LOW, 2, :], wvh[0:LOW, :], ALU.subtract)
                dve.drain()
                dve.wait_ge(rb_in, 16)

        q_ps, k_ps, q_round, k_round, q_split, k_split = (
            sem("q_ps"), sem("k_ps"), sem("q_round"), sem("k_round"), sem("q_split"), sem("k_split"))
        s_ps, max_read, max_rows, max_ps, q_aug = (
            sem("s_ps"), sem("max_read"), sem("max_rows"), sem("max_ps"), sem("q_aug"))
        st_ps, exp_done, pv_ps, o_read = sem("st_ps"), sem("exp_done"), sem("pv_ps"), sem("o_read")
        v_ps, v_ready, c_ps, c_round, c_split = sem("v_ps"), sem("v_ready"), sem("c_ps"), sem("c_round"), sem("c_split")
        turn_o_ps, o_normed, turn_n_ps, on_turned, ao_ps, h_done = (
            sem("turn_o_ps"), sem("o_normed"), sem("turn_n_ps"), sem("on_turned"), sem("ao_ps"), sem("h_done"))
        h_kept = sem("h_kept")
        ln1_var, ln1_ready, xn_ready, xt_ps, xn_turned = (
            sem("ln1_var"), sem("ln1_ready"), sem("xn_ready"), sem("xn_ps"), sem("xn_turned"))
        ln2_var, ln2_ready, x2_ready, x2_ps, x2_turned = (
            sem("ln2_var"), sem("ln2_ready"), sem("x2_ready"), sem("x2_ps"), sem("x2_turned"))
        lg_ps, lg_ready, lg_exp, hot_ready, rank_ps, slots_ready = (
            sem("lg_ps"), sem("lg_ready"), sem("lg_exp"), sem("hot_ready"), sem("rank_ps"), sem("slots_ready"))
        rank_read = sem("rank_read")
        ln_loaded, res_loaded, scattered = sem("ln_loaded"), sem("res_loaded"), sem("scattered")

        def seq_rows(b):
            return acc[bass.ds(b * S, S), :].rearrange("(t p) d -> p t d", p=TT)

        with nc.Block() as block:
            @block.sync
            def _(sp):
                def load_ln(b):
                    sp.dma_start(h_ln[:, :, :], seq_rows(b)).then_inc(ln_loaded, 16)

                def load_res(b, first):
                    if not first:
                        sp.wait_ge(h_kept, 16 * b)
                        sp.wait_ge(x2_ready, b)
                    sp.dma_start(h_new[:, :, :], seq_rows(b)).then_inc(res_loaded, 16)

                def keep(b):
                    sp.wait_ge(h_done, b + 1)
                    sp.dma_start(seq_rows(b), h_new[:, :, :]).then_inc(h_kept, 16)

                load_ln(0)
                load_res(0, True)
                sp.wait_ge(xn_ready, 1)
                load_ln(1)
                sp.wait_ge(xn_ready, 2)
                load_ln(2)

                def ahead(b):
                    sp.wait_ge(xn_ready, b + 2)
                    load_ln(b + 2)

                ahead(1)
                keep(0)
                with sp.Fori(2, LAST) as b:
                    ahead(b)
                    load_res(b - 1, False)
                    keep(b - 1)
                for b in (LAST - 1, LAST):
                    load_res(b, False)
                    keep(b)
                sp.wait_ge(h_kept, 16 * B)

            @block.scalar
            def _(act):
                def exps(n, g, q):
                    act.wait_ge(st_ps, 2 * n + q + 1)
                    act.activation(p[:, g % 2, 2 * q:2 * q + 2, :], ps[0:TT, BST:BST + 2, 0:BS],
                                   ACT.Exp, scale=SCALE).then_inc(exp_done, 1)

                def round_qk(m, g):
                    act.wait_ge(q_ps, m + 1)
                    act.activation(q_r[:, :, :].rearrange("p a n -> p (a n)"), ps[:, BQ, 0:2 * S],
                                   ACT.Copy).then_inc(q_round, 1)
                    act.wait_ge(k_ps, m + 1)
                    act.activation(k_r[:, :, :].rearrange("p a n -> p (a n)"), ps[:, BK, 0:2 * S],
                                   ACT.Identity, bias=k_one).then_inc(k_round, 1)

                def round_c(b):
                    act.wait_ge(c_ps, b + 1)
                    act.activation(c_r[:, :, :].rearrange("p a n -> p (a n)"), ps[:, BM, 0:2 * S],
                                   ACT.Copy).then_inc(c_round, 1)

                def copy_v(b, first):
                    act.wait_ge(v_ps, b + 1)
                    if not first:
                        act.wait_ge(pv_ps, NG * b)
                    act.copy(v[:, :, :, 0:DK], ps[0:TT, BM, :].rearrange("p (t h d) -> p t h d", t=2, d=DK)
                             ).then_inc(v_ready, 1)

                def copy_o(n, g):
                    act.wait_ge(pv_ps, n + 1)
                    act.copy(os_[:, g, :], ps[:, BO_, 0:S]).then_inc(o_read, 1)

                def copy_turned(ready, b, dst, done):
                    act.wait_ge(ready, b + 1)
                    act.copy(dst[:, :, :].rearrange("p c n -> p (c n)"), ps[:, BM, 0:2 * S]).then_inc(done, 1)

                def exp_logits(b):
                    act.wait_ge(lg_ready, b + 1)
                    act.activation(ex[:, :, :], lgx[:, :, :], ACT.Exp).then_inc(lg_exp, 1)

                def normalise(h, k, dst, done):
                    for t in range(2):
                        ins = act.activation(dst[:, t, 0:D], h[:, t, :], ACT.Identity, bias=shift[:, k, t:t + 1],
                                             scale=rstd[:, k, t:t + 1])
                    ins.then_inc(done, 1)

                def ln1(b, turned=None, n=0):
                    act.wait_ge(ln1_ready, b + 1)
                    if turned is not None:
                        act.wait_ge(turned, n)
                    normalise(h_ln, 0, xn, xn_ready)

                def ln2(b, first=False):
                    act.wait_ge(ln2_ready, b + 1)
                    if not first:
                        act.wait_ge(scattered, 64 * b)
                    normalise(h_new, 1, pay, x2_ready)

                ln1(0)
                copy_turned(xt_ps, 0, xnt, xn_turned)
                round_c(0)
                ln1(1)
                copy_turned(xt_ps, 1, xnt, xn_turned)
                for m in range(3):
                    if m:
                        act.wait_ge(q_split, m)
                        act.wait_ge(k_split, m)
                    round_qk(m, m)

                def body(b, before, last):
                    back1, back2 = before > 0, before > 1
                    for d in range(NG):
                        n = NG * b + d
                        if d == 1 and back2:
                            ln2(b - 2, before == 2)
                        if back1 or d >= 2:
                            act.wait_ge(pv_ps, n - 1)
                        exps(n, d, 0)
                        if not (last and d > 0):
                            act.wait_ge(q_split, n + 3)
                            act.wait_ge(k_split, n + 3)
                            round_qk(n + 3, (d + 3) % NG)
                        if d == 3 and not last:
                            if back1:
                                ln1(b + 2, turn_n_ps, b)
                            else:
                                ln1(2)
                        if d == 2 and back2:
                            exp_logits(b - 2)
                        if d == 2:
                            if back1:
                                act.wait_ge(turn_o_ps, 2 * b)
                            copy_o(n - 2, 0)
                        if d == 1 and back2:
                            copy_turned(x2_ps, b - 2, x2t, x2_turned)
                        if d == 0 and back1 or d > 1:
                            copy_o(n - 1, (d - 1) % NG)
                        if d == 0:
                            copy_v(b, not back1)
                        if d == 2 and back1:
                            copy_turned(turn_n_ps, b - 1, ont, on_turned)
                        if d == 0 and not last:
                            round_c(b + 1)
                        exps(n, d, 1)
                        if d == 3 and not last:
                            copy_turned(xt_ps, b + 2, xnt, xn_turned)

                for b in range(3):
                    body(b, b, False)
                with act.Fori(3, LAST) as b:
                    body(b, 3, False)
                body(LAST, 3, True)
                ln2(LAST - 1)
                copy_turned(x2_ps, LAST - 1, x2t, x2_turned)
                copy_o(NG * B - 1, NG - 1)
                exp_logits(LAST - 1)
                copy_turned(turn_n_ps, LAST, ont, on_turned)
                ln2(LAST)
                copy_turned(x2_ps, LAST, x2t, x2_turned)
                exp_logits(LAST)

            @block.gpsimd
            def _(pool):
                def factors(b, k, var_ready, done):
                    pool.wait_ge(var_ready, b + 1)
                    pool.tensor_tensor(rstd[:, k, :], var_e[:, k, :], minus_half[:, :], ALU.pow)
                    pool.drain()
                    pool.tensor_tensor(shift[:, k, :], less_mean[:, k, :], rstd[:, k, :], ALU.mult).then_inc(done, 1)

                def scatter(placed):
                    pool.wait_ge(ln1_var, 1)
                    pool.wait_ge(slots_ready, placed)
                    for t in range(2):
                        for k in range(2):
                            pool.indirect_dma_start(
                                out=rows[:, :], out_offset=bass.IndirectOffsetOnAxis(ap=slot[:, t, k:k + 1], axis=0),
                                in_=pay[:, t, :], in_offset=None).then_inc(scattered, 16)

                for b in range(4):
                    factors(b, 0, ln1_var, ln1_ready)
                factors(0, 1, ln2_var, ln2_ready)
                with pool.Fori(1, LAST - 1) as placed:
                    factors(placed + 3, 0, ln1_var, ln1_ready)
                    scatter(placed)
                    factors(placed, 1, ln2_var, ln2_ready)
                for b in (LAST - 1, LAST):
                    scatter(b)
                    factors(b, 1, ln2_var, ln2_ready)
                scatter(B)
                pool.wait_ge(scattered, 64 * B)

            @block.vector
            def _(dve):
                def split(out, r, factor, src, done):
                    dve.scalar_tensor_tensor(out=out, in0=r, scalar=factor, in1=src,
                                             op0=ALU.mult, op1=ALU.add).then_inc(done, 1)

                def split_qk(m, g):
                    dve.wait_ge(q_round, m + 1)
                    split(qs[:, g, :, :].rearrange("p a n -> p (a n)"), q_r[:, :, :].rearrange("p a n -> p (a n)"),
                          s_q, ps[:, BQ, 0:2 * S], q_split)
                    dve.wait_ge(k_round, m + 1)
                    split(ks[:, g, :, :].rearrange("p a n -> p (a n)"), k_r[:, :, :].rearrange("p a n -> p (a n)"),
                          s_k, ps[:, BK, 0:2 * S], k_split)

                def split_c(b):
                    dve.wait_ge(c_round, b + 1)
                    split(cs[:, :, :].rearrange("p a n -> p (a n)"), c_r[:, :, :].rearrange("p a n -> p (a n)"),
                          s_c, ps[:, BM, 0:2 * S], c_split)

                def maxima(m, q, first=False):
                    if q == 0 and not first:
                        dve.wait_ge(max_rows, m)
                    dve.wait_ge(s_ps, 2 * m + q + 1)
                    dve.tensor_reduce(mx[:, 0, 2 * q:2 * q + 2], ps[0:TT, BSC:BSC + 2, 0:HALF], AX.X, ALU.max)
                    dve.tensor_reduce(mx[:, 1, 2 * q:2 * q + 2], ps[0:TT, BSC:BSC + 2, HALF:BS], AX.X,
                                      ALU.max).then_inc(max_read, 1)

                def rows_of_max(m):
                    dve.drain()
                    m4 = mx[:, :, :].rearrange("p t (r a) -> p t r a", a=2)
                    dve.tensor_scalar(mxt[:, :, :, :, MAXROW].bitcast(F32R), m4, -1.0, None, ALU.mult)
                    dve.drain()
                    dve.scalar_tensor_tensor(out=mxt[:, :, :, :, MAXROW + 1], in0=m4, scalar=-1.0,
                                             in1=mxt[:, :, :, :, MAXROW], op0=ALU.mult,
                                             op1=ALU.subtract).then_inc(max_rows, 1)

                def augment(n, g):
                    dve.wait_ge(max_ps, n + 1)
                    o = qs[:, g, :, :].rearrange("p a n -> p (a n)")
                    dve.tensor_tensor(o, ps[:, BQ, 0:2 * S], o, ALU.add).then_inc(q_aug, 1)

                def norm_o(b, t):
                    dve.wait_ge(turn_o_ps, 2 * b + t + 1)
                    o = ps[0:TT, BM, :].rearrange("p (h c) -> p h c", c=32)
                    dve.reciprocal(rden[:, t, :], o[:, :, DK])
                    dve.drain()
                    dve.tensor_tensor(on[:, t, :].rearrange("p (h c) -> p h c", c=DK), o[:, :, 0:DK],
                                      rden[:, t, :].unsqueeze(2).broadcast_to([TT, H, DK]),
                                      ALU.mult).then_inc(o_normed, 1)

                def stats(h, k, done):
                    for t in range(2):
                        dve.bn_stats(st6[:, k, t, :], h[:, t, :])
                    dve.drain()
                    for t in range(2):
                        dve.bn_aggr(mv[:, k, t, :], st6[:, k, t, :])
                    dve.drain()
                    dve.tensor_scalar(less_mean[:, k, :], mv[:, k, :, 0], -1.0, None, ALU.mult)
                    dve.tensor_scalar(var_e[:, k, :], mv[:, k, :, 1], EPS, None, ALU.add).then_inc(done, 1)

                def ln1_stats(b):
                    dve.wait_ge(ln_loaded, 16 * b + 16)
                    stats(h_ln, 0, ln1_var)

                def add_res(b, first):
                    dve.wait_ge(ao_ps, b + 1)
                    dve.wait_ge(res_loaded, 16 * b + 16)
                    if not first:
                        dve.wait_ge(h_kept, 16 * b)
                    dve.tensor_tensor(h_new[:, :, :].rearrange("p t d -> p (t d)"), ps[0:TT, BM, :],
                                      h_new[:, :, :].rearrange("p t d -> p (t d)"), ALU.add).then_inc(h_done, 1)

                def ln2_stats():
                    dve.drain()
                    stats(h_new, 1, ln2_var)

                def logits(b):
                    dve.wait_ge(lg_ps, b + 1)
                    dve.tensor_tensor(lg[:, :, :], ps[0:TT, BSC, BS:BS + 2 * E].rearrange("p (t e) -> p t e", e=E),
                                      rb[:, :, :].broadcast_to([TT, 2, E]), ALU.add)
                    dve.drain()
                    for t in range(2):
                        dve.max(top[:, t, :], lg[:, t, :])
                    dve.drain()
                    dve.tensor_tensor(lgx[:, :, :], lg[:, :, :], top[:, :, 0:1].broadcast_to([TT, 2, E]),
                                      ALU.subtract).then_inc(lg_ready, 1)

                def choose(b):
                    for t in range(2):
                        dve.max_index(topi[:, t, :], top[:, t, :], lg[:, t, :])
                    dve.drain()
                    dve.tensor_copy(topf[:, :, :], topi[:, :, 0:2])
                    dve.drain()
                    for k in range(2):
                        dve.tensor_tensor(hot[:, k, :, :], iota_e[:, :, :].broadcast_to([TT, 2, E]),
                                          topf[:, :, k:k + 1].broadcast_to([TT, 2, E]), ALU.is_equal)
                    dve.drain()
                    dve.tensor_tensor(hotb[:, :, :], hot[:, 0, :, :], hot[:, 1, :, :], ALU.add).then_inc(hot_ready, 1)

                def gates(b):
                    dve.wait_ge(lg_exp, b + 1)
                    dve.tensor_reduce(small[:, 0, :], ex[:, :, :], AX.X, ALU.add)
                    dve.drain()
                    dve.reciprocal(small[:, 1, :], small[:, 0, :])
                    dve.drain()
                    dve.tensor_tensor(ex[:, :, :], ex[:, :, :],
                                      small[:, 1, :].unsqueeze(2).broadcast_to([TT, 2, E]), ALU.mult)
                    dve.drain()
                    dve.tensor_tensor(pay[:, :, D:D + E], ex[:, :, :], hotb[:, :, :], ALU.mult)
                    dve.tensor_copy(pay[:, :, D + E], token[:, :])
                    dve.drain()
                    dve.tensor_scalar(token[:, :], token[:, :], float(S), None, ALU.add)

                def take_ranks(b):
                    dve.wait_ge(rank_ps, b + 1)
                    dve.tensor_tensor(rank[:, :, :],
                                      ps[0:TT, BSC, BR:BR + 2 * E].rearrange("p (t e) -> p t e", e=E),
                                      count[0:TT, :].unsqueeze(1).broadcast_to([TT, 2, E]), ALU.add)
                    dve.drain()
                    dve.tensor_tensor(count[:, :], count[:, :], ps[:, BSC, BR + 2 * E:BR + 3 * E],
                                      ALU.add).then_inc(rank_read, 1)

                def place(b):
                    for k in range(2):
                        dve.tensor_tensor(hot[:, k, :, :], hot[:, k, :, :], rank[:, :, :], ALU.mult)
                    dve.drain()
                    for k in range(2):
                        dve.tensor_reduce(slotf[:, :, k:k + 1], hot[:, k, :, :], AX.X, ALU.add)
                    dve.drain()
                    dve.tensor_copy(slot[:, :, :], slotf[:, :, :]).then_inc(slots_ready, 1)

                for b in range(2):
                    if b:
                        dve.wait_ge(xn_ready, b)
                    ln1_stats(b)
                    if b == 0:
                        split_c(0)
                for m in range(3):
                    split_qk(m, m)
                    if m < 2:
                        for q in range(2):
                            maxima(m, q, m == 0)
                        rows_of_max(m)
                    if m == 0:
                        augment(0, 0)

                def body(b, before, last):
                    back1, back2 = before > 0, before > 1
                    for d in range(NG):
                        n = NG * b + d
                        more = not (last and d > 1)
                        if d == 2 and back2:
                            if more:
                                dve.wait_ge(s_ps, 2 * n + 5)
                            logits(b - 2)
                        if more:
                            maxima(n + 2, 0)
                        if d == 3 and back1:
                            add_res(b - 1, not back2)
                        if not (last and d > 0):
                            if back1 or d > 0:
                                dve.wait_ge(st_ps, 2 * n)
                            split_qk(n + 3, (d + 3) % NG)
                        if d == 2 and back1:
                            norm_o(b - 1, 1)
                        if d == 3 and back2:
                            if more:
                                dve.wait_ge(s_ps, 2 * n + 6)
                            take_ranks(b - 2)
                        if more:
                            maxima(n + 2, 1)
                        if not (last and d == 3):
                            augment(n + 1, (d + 1) % NG)
                        if more:
                            rows_of_max(n + 2)
                        if d == 0 and back2:
                            ln2_stats()
                        if d == 0 and not last:
                            split_c(b + 1)
                        if d == 1 and back1:
                            norm_o(b - 1, 0)
                        if d == 1 and not last:
                            ln1_stats(b + 2)
                        if d == 2 and back2:
                            choose(b - 2)
                            gates(b - 2)
                        if d == 3 and back2:
                            place(b - 2)

                for b in range(3):
                    body(b, b, False)
                with dve.Fori(3, LAST) as b:
                    body(b, 3, False)
                body(LAST, 3, True)
                ln2_stats()
                norm_o(LAST, 0)
                logits(LAST - 1)
                norm_o(LAST, 1)
                choose(LAST - 1)
                gates(LAST - 1)
                take_ranks(LAST - 1)
                place(LAST - 1)
                add_res(LAST, False)
                ln2_stats()
                logits(LAST)
                choose(LAST)
                gates(LAST)
                take_ranks(LAST)
                place(LAST)

            @block.tensor
            def _(pe):
                def project(m, g):
                    for k, bank, done in ((0, BQ, q_ps), (1, BK, k_ps)):
                        for r in range(2):
                            o = ps[:, bank, r * S:(r + 1) * S]
                            w = 2 * g + r
                            pe.matmul(o, wuh[k][:, w, :, :, :].rearrange("p a r d -> p (a r d)"), cs[:, k, :],
                                      start=True, stop=False)
                            mm = pe.matmul(o, wul[k][:, w, :, :, :].rearrange("p a r d -> p (a r d)"), cs[:, k, :],
                                           start=False, stop=True)
                        mm.then_inc(done, 1)

                def masked(bank, mask, parts):
                    both = ps[0:TT, bank, 0:2 * S].rearrange("p (k n) -> p k n", k=2)[:, :, 0:HALF]
                    pe.matmul(both, identb[0:TT, 0:TT], mask[:, :, :], start=True, stop=False,
                              skip_group_check=True)
                    for lhs, rhs, o in parts:
                        mm = pe.matmul(o, lhs, rhs, start=False, stop=True, skip_group_check=True)
                    return mm

                def scores(m, g, q):
                    for a in range(2):
                        rr = slice(a * LOW, (a + 1) * LOW)
                        mm = masked(BSC + a, mask_q, [
                            (qs[rr, g, q, 0:TT], ks[rr, g, q, 0:HALF], ps[0:TT, BSC + a, 0:HALF]),
                            (qs[rr, g, q, TT:S], ks[rr, g, q, :], ps[0:TT, BSC + a, HALF:BS])])
                    mm.then_inc(s_ps, 1)

                def scores_t(n, g, q):
                    for a in range(2):
                        rr = slice(a * LOW, (a + 1) * LOW)
                        mm = masked(BST + a, mask_k, [
                            (ks[rr, g, q, 0:TT], qs[rr, g, q, :], ps[0:TT, BST + a, 0:S]),
                            (ks[rr, g, q, TT:S], qs[rr, g, q, S - HALF:S], ps[0:TT, BST + a, S:BS])])
                    mm.then_inc(st_ps, 1)

                def values(n, g):
                    for j in range(4):
                        h = 4 * g + j
                        o = ps[32 * j:32 * j + DK + 1, BO_, 0:S]
                        pe.matmul(o, v[:, 0, h, :], p[:, g % 2, j, 0:S], start=True, stop=False,
                                  skip_group_check=True)
                        mm = pe.matmul(o[:, S - HALF:S], v[:, 1, h, :], p[:, g % 2, j, S:BS], start=False, stop=True,
                                       skip_group_check=True)
                    mm.then_inc(pv_ps, 1)

                def turn_max(n, g):
                    for r in range(2):
                        for t in range(2):
                            mm = pe.transpose(ps[:, BQ, r * S + t * TT:r * S + (t + 1) * TT],
                                              mxt[:, t, r, :, :].rearrange("p a c -> p (a c)"), ident[0:TT, 0:TT])
                    mm.then_inc(max_ps, 1)

                def values_of(b):
                    for t in range(2):
                        o = ps[0:TT, BM, t * D:(t + 1) * D]
                        c = cs[:, 1, t * TT:(t + 1) * TT]
                        pe.matmul(o, c, wvh[:, :], start=True, stop=False)
                        mm = pe.matmul(o, c, wvl[:, :], start=False, stop=True)
                    mm.then_inc(v_ps, 1)

                def compress(b):
                    for k in range(2):
                        for c in range(DC):
                            mm = pe.matmul(ps[:, BM, k * S:(k + 1) * S],
                                           wd[:, c, k, :, :].rearrange("p r l -> p (r l)"), xnt[:, c, :],
                                           start=c == 0, stop=c == DC - 1)
                    mm.then_inc(c_ps, 1)

                def turn(src, done):
                    for c in range(DC):
                        for t in range(2):
                            mm = pe.transpose(ps[:, BM, c * S + t * TT:c * S + (t + 1) * TT],
                                              src[:, t, c * 128:(c + 1) * 128], ident[0:TT, 0:TT])
                    mm.then_inc(done, 1)

                def turn_o(t):
                    for g in range(NG):
                        mm = pe.transpose(ps[0:TT, BM, g * 128:(g + 1) * 128],
                                          os_[:, g, t * TT:(t + 1) * TT], ident[:, :])
                    mm.then_inc(turn_o_ps, 1)

                def out_proj():
                    for t in range(2):
                        for c in range(DC):
                            mm = pe.matmul(ps[0:TT, BM, t * D:(t + 1) * D], ont[:, c, t * TT:(t + 1) * TT],
                                           wo[:, c, :], start=c == 0, stop=c == DC - 1)
                    mm.then_inc(ao_ps, 1)

                def route_logits():
                    for t in range(2):
                        for c in range(DC):
                            mm = pe.matmul(ps[0:TT, BSC, BS + t * E:BS + (t + 1) * E], x2t[:, c, t * TT:(t + 1) * TT],
                                           rw[:, c, :], start=c == 0, stop=c == DC - 1)
                    mm.then_inc(lg_ps, 1)

                def ranks():
                    o = [ps[0:TT if k < 2 else 128, BSC, BR + k * E:BR + (k + 1) * E] for k in range(3)]
                    pe.matmul(o[0], below[:, :], hotb[:, 0, :], start=True, stop=True)
                    pe.matmul(o[1], below[:, :], hotb[:, 1, :], start=True, stop=False)
                    pe.matmul(o[1], ones[:, 0:TT], hotb[:, 0, :], start=False, stop=True)
                    pe.matmul(o[2], ones[:, :], hotb[:, 0, :], start=True, stop=False)
                    pe.matmul(o[2], ones[:, :], hotb[:, 1, :], start=False, stop=True).then_inc(rank_ps, 1)

                pe.wait_ge(xn_ready, 1)
                turn(xn, xt_ps)
                pe.wait_ge(xn_turned, 1)
                compress(0)
                pe.wait_ge(xn_ready, 2)
                pe.wait_ge(c_split, 1)
                turn(xn, xt_ps)
                for m in range(3):
                    if m:
                        pe.wait_ge(q_split, m)
                        pe.wait_ge(k_split, m)
                    project(m, m)
                    if m < 2:
                        pe.wait_ge(q_split, m + 1)
                        pe.wait_ge(k_split, m + 1)
                        for q in range(2):
                            if m or q:
                                pe.wait_ge(max_read, 2 * m + q)
                            scores(m, m, q)
                    if m == 0:
                        pe.wait_ge(max_rows, 1)
                        turn_max(0, 0)
                        pe.wait_ge(max_ps, 1)
                        pe.wait_ge(q_aug, 1)

                def body(b, before, last):
                    back1, back2 = before > 0, before > 1
                    for d in range(NG):
                        n = NG * b + d
                        proj, ahead, turned = not (last and d > 0), not (last and d > 1), not (last and d == 3)
                        if d == 2 and back2:
                            pe.wait_ge(x2_turned, b - 1)
                            pe.wait_ge(max_read, 2 * n + 4)
                            route_logits()
                        if ahead:
                            pe.wait_ge(k_split, n + 3)
                            pe.wait_ge(max_read, 2 * n + 4)
                            scores(n + 2, (d + 2) % NG, 0)
                        pe.wait_ge(q_aug, n + 1)
                        if back1 or d > 0:
                            pe.wait_ge(exp_done, 2 * n)
                        scores_t(n, d, 0)
                        if proj:
                            pe.wait_ge(c_split, b + 1 if d == 0 else b + 2)
                            pe.wait_ge(k_split, n + 3)
                            project(n + 3, (d + 3) % NG)
                        if d == 1 and back2:
                            if last:
                                pe.wait_ge(v_ready, B)
                            pe.wait_ge(x2_ready, b - 1)
                            turn(pay, x2_ps)
                        if d == 2 and back1:
                            pe.wait_ge(o_normed, 2 * b - 1)
                            turn_o(1)
                        if d == 3 and back2:
                            pe.wait_ge(hot_ready, b - 1)
                            if not last:
                                pe.wait_ge(max_read, 2 * n + 5)
                            ranks()
                        if ahead:
                            pe.wait_ge(max_read, 2 * n + 5)
                            scores(n + 2, (d + 2) % NG, 1)
                        if d == 0:
                            pe.wait_ge(xn_turned, b + 2)
                            values_of(b)
                        if back1 or d > 0:
                            if d == 1:
                                pe.wait_ge(v_ready, b + 1)
                            if back1 or d > 1:
                                pe.wait_ge(o_read, n - 1)
                            values(n - 1, (d - 1) % NG)
                        if d == 1 and back1:
                            pe.wait_ge(o_read, NG * b)
                            if back2:
                                pe.wait_ge(x2_turned, b - 1)
                            else:
                                pe.wait_ge(c_split, b + 2)
                            turn_o(0)
                        if d == 2 and back1:
                            pe.wait_ge(o_normed, 2 * b)
                            turn(on, turn_n_ps)
                        if turned:
                            pe.wait_ge(max_rows, n + 2)
                            if proj:
                                pe.wait_ge(q_split, n + 4)
                            turn_max(n + 1, (d + 1) % NG)
                        if d == 0 and not last:
                            pe.wait_ge(v_ready, b + 1)
                            compress(b + 1)
                        pe.wait_ge(exp_done, 2 * n + 1)
                        scores_t(n, d, 1)
                        if d == 2 and back1:
                            pe.wait_ge(on_turned, b)
                            out_proj()
                        if d == 3 and not last:
                            if back1:
                                pe.wait_ge(h_done, b)
                            else:
                                pe.wait_ge(c_split, b + 2)
                            pe.wait_ge(xn_ready, b + 3)
                            turn(xn, xt_ps)

                for b in range(3):
                    body(b, b, False)
                with pe.Fori(3, LAST) as b:
                    body(b, 3, False)
                body(LAST, 3, True)
                pe.wait_ge(x2_ready, LAST)
                pe.wait_ge(h_done, LAST)
                turn(pay, x2_ps)
                pe.wait_ge(exp_done, 2 * NG * B)
                pe.wait_ge(o_read, NG * B - 1)
                values(NG * B - 1, NG - 1)
                pe.wait_ge(o_read, NG * B)
                pe.wait_ge(x2_turned, LAST)
                turn_o(0)
                pe.wait_ge(rank_read, LAST - 1)
                route_logits()
                pe.wait_ge(o_normed, 2 * B - 1)
                turn_o(1)
                pe.wait_ge(o_normed, 2 * B)
                turn(on, turn_n_ps)
                pe.wait_ge(hot_ready, LAST)
                ranks()
                pe.wait_ge(on_turned, B)
                out_proj()
                pe.wait_ge(x2_ready, B)
                pe.wait_ge(h_done, B)
                turn(pay, x2_ps)
                pe.wait_ge(x2_turned, B)
                pe.wait_ge(rank_read, LAST)
                route_logits()
                pe.wait_ge(hot_ready, B)
                ranks()


def experts(env):
    nc, ps, ident, sem = env["nc"], env["ps"], env["ident"], env["sem"]
    acc, rows, out, b2 = (env[k] for k in ("acc", "rows", "out", "b2"))
    w1s, w2s, b1s, count, region0 = (env[k] for k in ("w1s", "w2s", "b1s", "count", "region0"))
    SPARE = E * REGION
    STEPS = NTOK // ROWS + 1

    with ExitStack() as own:
        def sb(name, shape, dt):
            return own.enter_context(nc.sbuf_tensor(name, shape, dt))

        step_i = sb("step_i", [1, STEPS], I32)
        step = sb("step", [1, 1, STEPS], F32)
        tile_i = sb("tile_i", [1, W16], I32)
        tile = sb("tile", [1, W16, 1], F32)
        exp_i = sb("exp_i", [1, E], I32)
        expert = sb("expert", [1, 1, E], F32)
        over = sb("over", [1, E, STEPS], F32)
        used = sb("used", [1, E], F32)
        need = sb("need", [1, E], F32)
        ends = [sb(f"ends{k}", [1, E], F32) for k in range(2)]
        begin = sb("begin", [1, E], F32)
        base = sb("base", [1, E], F32)
        mine = sb("mine", [1, W16, E], F32)
        work = sb("work", [1, W16, E], F32)
        row_f = sb("row_f", [1, W16], F32)
        any_f = sb("any_f", [1, W16], F32)
        exp_f = sb("exp_f", [1, W16], F32)
        table = sb("table", [1, 2, W16], I32)
        part_i = sb("part_i", [128, RP], I32)
        part = sb("part", [128, RP], F32)
        padding = sb("padding", [128, RP, PW], F32)
        starts = sb("starts", [1, E], I32)
        b2_all = sb("b2_all", [128, E, D], F32)
        target = sb("target", [128, RP], I32)
        zero = sb("zero", [128, RP], I32)

        base_ready, pads_ready, padded, spare_out, b2_in = (
            sem("base_ready"), sem("pads_ready"), sem("padded"), sem("spare_out"), sem("b2_in"))

        with nc.Block() as block:
            @block.sync
            def _(sp):
                sp.dma_start(b2_all[:, :, :], b2.rearrange("(o e) d -> o e d", o=1).broadcast_to([128, E, D])
                             ).then_inc(b2_in, 16)
                sp.wait_ge(pads_ready, 1)
                sp.dma_start(rows[SPARE:SPARE + ROWS, :].rearrange("(t p) w -> p t w", p=128),
                             padding[:, :, :]).then_inc(spare_out, 16)
                for e in range(E):
                    at = sp.value_load(starts[0:1, e:e + 1], min_val=0, max_val=SPARE)
                    sp.dma_start(rows[bass.ds(at, ROWS), :].rearrange("(t p) w -> p t w", p=128),
                                 padding[:, :, :]).then_inc(padded, 16)
                sp.wait_ge(padded, 16 * E)
                sp.wait_ge(spare_out, 16)
                sp.wait_ge(b2_in, 16)

            @block.gpsimd
            def _(pool):
                pool.iota(step_i[:, :], pattern=[[ROWS, STEPS]], base=0, channel_multiplier=0)
                pool.iota(tile_i[:, :], pattern=[[1, W16]], base=0, channel_multiplier=0)
                pool.iota(exp_i[:, :], pattern=[[1, E]], base=0, channel_multiplier=0)
                pool.iota(part_i[:, :], pattern=[[128, RP]], base=0, channel_multiplier=1)
                pool.memset(padding[:, :, :], 0.0)
                pool.memset(zero[:, :], 0)
                pool.drain()
                pool.nop().then_inc(base_ready, 1)

            @block.vector
            def _(dve):
                def tt(o, a, b, op):
                    dve.tensor_tensor(o, a, b, op)
                    dve.drain()

                dve.wait_ge(base_ready, 1)
                dve.tensor_copy(part[:, :], part_i[:, :])
                dve.tensor_copy(step[:, 0, :], step_i[:, :])
                dve.tensor_copy(tile[:, :, 0], tile_i[:, :])
                dve.tensor_copy(expert[:, 0, :], exp_i[:, :])
                dve.drain()
                dve.tensor_scalar(padding[:, :, D + E], part[:, :], float(NTOK), None, ALU.add)
                dve.tensor_copy(starts[:, :], count[0:1, :])
                dve.drain()
                dve.nop().then_inc(pads_ready, 1)
                tt(used[:, :], count[0:1, :], region0[0:1, :], ALU.subtract)
                tt(over[:, :, :], used[:, :].unsqueeze(2).broadcast_to([1, E, STEPS]),
                   step[:, :, :].broadcast_to([1, E, STEPS]), ALU.is_gt)
                dve.tensor_reduce(need[:, :], over[:, :, :], AX.X, ALU.add)
                dve.drain()
                src = need
                for k, shift in enumerate((1, 2, 4)):
                    dst = ends[k % 2]
                    dve.tensor_copy(dst[:, 0:shift], src[:, 0:shift])
                    tt(dst[:, shift:E], src[:, shift:E], src[:, 0:E - shift], ALU.add)
                    src = dst
                last = src
                tt(begin[:, :], last[:, :], need[:, :], ALU.subtract)
                dve.scalar_tensor_tensor(out=base[:, :], in0=begin[:, :], scalar=-float(ROWS), in1=region0[0:1, :],
                                         op0=ALU.mult, op1=ALU.add)
                dve.drain()
                wide = [1, W16, E]
                tt(mine[:, :, :], tile[:, :, :].broadcast_to(wide), begin[:, :].unsqueeze(1).broadcast_to(wide), ALU.is_ge)
                tt(work[:, :, :], tile[:, :, :].broadcast_to(wide), last[:, :].unsqueeze(1).broadcast_to(wide), ALU.is_lt)
                tt(mine[:, :, :], mine[:, :, :], work[:, :, :], ALU.mult)
                tt(work[:, :, :], mine[:, :, :], expert[:, :, :].broadcast_to(wide), ALU.mult)
                dve.tensor_reduce(exp_f[:, :], work[:, :, :], AX.X, ALU.add)
                dve.tensor_reduce(any_f[:, :], mine[:, :, :], AX.X, ALU.add)
                dve.drain()
                tt(work[:, :, :], mine[:, :, :], base[:, :].unsqueeze(1).broadcast_to(wide), ALU.mult)
                dve.tensor_reduce(row_f[:, :], work[:, :, :], AX.X, ALU.add)
                dve.drain()
                dve.scalar_tensor_tensor(out=tile[:, :, 0], in0=tile[:, :, 0], scalar=float(ROWS), in1=any_f[:, :],
                                         op0=ALU.mult, op1=ALU.mult)
                dve.drain()
                tt(row_f[:, :], row_f[:, :], tile[:, :, 0], ALU.add)
                dve.scalar_tensor_tensor(out=row_f[:, :], in0=any_f[:, :], scalar=-float(SPARE), in1=row_f[:, :],
                                         op0=ALU.mult, op1=ALU.add)
                dve.drain()
                dve.tensor_scalar(row_f[:, :], row_f[:, :], float(SPARE), None, ALU.add)
                dve.drain()
                dve.tensor_copy(table[:, 0, :], row_f[:, :])
                dve.tensor_copy(table[:, 1, :], exp_f[:, :])
                dve.drain()

        pay = [sb(f"tile_in{u}", [128, RP, PW], F32) for u in range(2)]
        xs = [sb(f"xs{u}", [128, DC, 2, ROWS], BF16) for u in range(2)]
        hg = [sb(f"hg{u}", [128, FC, ROWS], F32) for u in range(2)]
        hs = [sb(f"hs{u}", [128, FC, 2, ROWS], BF16) for u in range(2)]
        yt = [sb(f"yt{u}", [128, RP, D], F32) for u in range(2)]
        gate = [sb(f"gate{u}", [128, RP], F32) for u in range(2)]
        tokf = [sb(f"tokf{u}", [128, RP], F32) for u in range(2)]
        toki = [sb(f"toki{u}", [128, RP], I32) for u in range(2)]

        rows_in = [sem(f"rows_in{u}") for u in range(2)]
        xt_ps, x_high, x_split, meta_read = sem("rt_ps"), sem("x_high"), sem("x_split"), sem("meta_read")
        h_ps, h_act, h_high, h_split = sem("f1_ps"), sem("h_act"), sem("h_high"), sem("h_split")
        y_ps, y_ready, y_added = sem("y_ps"), sem("y_ready"), sem("y_added")
        out_done = sem("out_done")
        BT, BH, BY = 0, 1, 5
        JB = 512 // ROWS
        HC = FC // 2
        LOOPED = (NTILE - 2) // 2

        def hidden(j, n=1):
            if n == 1:
                return ps[:, BH + j // JB, (j % JB) * ROWS:(j % JB + 1) * ROWS]
            return ps[:, BH + j // JB:BH + (j + n) // JB, 0:JB * ROWS]

        with nc.Block() as block:
            @block.sync
            def _(sp):
                def load(i, u):
                    r = sp.value_load(table[0:1, 0, bass.ds(i, 1)], min_val=0, max_val=SPARE)
                    sp.dma_start(pay[u][:, :, :], rows[bass.ds(r, ROWS), :].rearrange("(t p) w -> p t w", p=128)
                                 ).then_inc(rows_in[u], 16)

                load(0, 0)
                load(1, 1)

                def reload(i, u):
                    sp.wait_ge(xt_ps, i + 1)
                    sp.wait_ge(meta_read, i + 1)
                    load(i + 2, u)

                with sp.Fori(0, LOOPED) as k:
                    for u in range(2):
                        reload(2 * k + u, u)
                for i in range(2 * LOOPED, NTILE - 2):
                    reload(i, i % 2)
                sp.wait_ge(y_added, 16 * RP * NTILE)
                sp.dma_start(out.rearrange("b s d -> (b s d)").rearrange("(q n) -> q n", q=128),
                             acc[0:NTOK, :].rearrange("t d -> (t d)").rearrange("(q n) -> q n", q=128)
                             ).then_inc(out_done, 16)
                sp.wait_ge(out_done, 16)

            @block.scalar
            def _(act):
                def high_x(i, u):
                    act.wait_ge(xt_ps, i + 1)
                    act.copy(xs[u][:, :, 0, :], ps[:, BT, 0:DC * ROWS].rearrange("p (c n) -> p c n", c=DC)
                             ).then_inc(x_high, 1)

                def gelu(i, u):
                    e = act.value_load(table[0:1, 1, bass.ds(i, 1)], min_val=0, max_val=E - 1)
                    for j in range(FC):
                        if j % HC == 0:
                            act.wait_ge(h_ps, 2 * i + j // HC + 1)
                        ins = act.activation(hg[u][:, j, :], hidden(j), ACT.Gelu, bias=b1s[:, bass.ds(e, 1), j])
                        if j % HC == HC - 1:
                            ins.then_inc(h_act, 1)

                high_x(0, 0)
                gelu(0, 0)
                high_x(1, 1)

                def step(i, u, first=False, ahead=2):
                    if ahead:
                        if not first:
                            act.wait_ge(h_split, 2 * i)
                        gelu(i + 1, 1 - u)
                    if ahead > 1:
                        high_x(i + 2, u)

                step(0, 0, True)
                step(1, 1)
                with act.Fori(1, LOOPED) as k:
                    step(2 * k, 0)
                    step(2 * k + 1, 1)
                for i in range(2 * LOOPED, NTILE):
                    step(i, i % 2, ahead=min(2, NTILE - 1 - i))

            @block.vector
            def _(dve):
                def low_x(i, u):
                    dve.wait_ge(x_high, i + 1)
                    dve.tensor_tensor(xs[u][:, :, 1, :], ps[:, BT, 0:DC * ROWS].rearrange("p (c n) -> p c n", c=DC),
                                      xs[u][:, :, 0, :], ALU.subtract).then_inc(x_split, 1)

                def meta(i, u):
                    e = dve.value_load(table[0:1, 1, bass.ds(i, 1)], min_val=0, max_val=E - 1)
                    dve.wait_ge(rows_in[u], 8 * i + 16 - 8 * u)
                    dve.tensor_copy(gate[u][:, :], pay[u][:, :, bass.ds(e + D, 1)].rearrange("p t o -> p (t o)"))
                    dve.tensor_copy(tokf[u][:, :], pay[u][:, :, D + E]).then_inc(meta_read, 1)

                def split_h(i, u):
                    for q in range(2):
                        a, b = q * HC, (q + 1) * HC
                        dve.wait_ge(h_act, 2 * i + q + 1)
                        dve.tensor_copy(hs[u][:, a:b, 0, :], hg[u][:, a:b, :]).then_inc(h_high, 1)
                        dve.wait_ge(h_high, 2 * i + q + 1)
                        dve.tensor_tensor(hs[u][:, a:b, 1, :], hg[u][:, a:b, :], hs[u][:, a:b, 0, :],
                                          ALU.subtract).then_inc(h_split, 1)

                def result(i, u, first):
                    e = dve.value_load(table[0:1, 1, bass.ds(i, 1)], min_val=0, max_val=E - 1)
                    dve.wait_ge(y_ps, i + 1)
                    if not first:
                        dve.wait_ge(y_added, 16 * RP * (i - 1))
                    dve.tensor_copy(toki[u][:, :], tokf[u][:, :])
                    dve.tensor_tensor(yt[u][:, :, :], ps[:, BY + u, :].rearrange("p (t d) -> p t d", d=D),
                                      b2_all[:, bass.ds(e, 1), :].broadcast_to([128, RP, D]), ALU.add)
                    dve.drain()
                    for t in range(RP):
                        ins = dve.tensor_scalar(yt[u][:, t, :], yt[u][:, t, :], gate[u][:, t:t + 1], None, ALU.mult)
                    ins.then_inc(y_ready, 1)

                low_x(0, 0)
                meta(0, 0)
                split_h(0, 0)
                low_x(1, 1)
                meta(1, 1)

                def step(i, u, first=False, ahead=2):
                    if ahead:
                        if not (first and u == 0):
                            dve.wait_ge(y_ps, i)
                        split_h(i + 1, 1 - u)
                    if ahead > 1:
                        low_x(i + 2, u)
                    result(i, u, first)
                    if ahead > 1:
                        dve.drain()
                        meta(i + 2, u)

                step(0, 0, True)
                step(1, 1, True)
                with dve.Fori(1, LOOPED) as k:
                    step(2 * k, 0)
                    step(2 * k + 1, 1)
                for i in range(2 * LOOPED, NTILE):
                    step(i, i % 2, ahead=min(2, NTILE - 1 - i))

            @block.gpsimd
            def _(pool):
                def add(i, u, first):
                    if not first:
                        pool.wait_ge(y_added, 16 * RP * i)
                    pool.wait_ge(y_ready, i + 1)
                    pool.tensor_tensor(target[:, :], toki[u][:, :], zero[:, :], ALU.add)
                    pool.drain()
                    for t in range(RP):
                        pool.indirect_dma_start(
                            out=acc[:, :], out_offset=bass.IndirectOffsetOnAxis(ap=target[:, t:t + 1], axis=0),
                            in_=yt[u][:, t, :], in_offset=None, compute_op=ALU.add).then_inc(y_added, 16)

                add(0, 0, True)
                add(1, 1, False)
                with pool.Fori(1, NTILE // 2) as k:
                    for u in range(2):
                        add(2 * k + u, u, False)
                if NTILE % 2:
                    add(NTILE - 1, 0, False)

            @block.tensor
            def _(pe):
                def expert_of(i):
                    return pe.value_load(table[0:1, 1, bass.ds(i, 1)], min_val=0, max_val=E - 1)

                def turn(i, u):
                    pe.wait_ge(rows_in[u], 8 * i + 16 - 8 * u)
                    for c in range(DC):
                        for t in range(RP):
                            mm = pe.transpose(ps[:, BT, c * ROWS + t * 128:c * ROWS + (t + 1) * 128],
                                              pay[u][:, t, c * 128:(c + 1) * 128], ident[:, :])
                    mm.then_inc(xt_ps, 1)

                def up(i, u, e, first=False):
                    pe.wait_ge(x_split, i + 1)
                    for j in range(FC):
                        if j % HC == 0 and not first:
                            pe.wait_ge(h_act, 2 * i - 1 + j // HC)
                        n = 0
                        for c in range(DC):
                            for wp, xp in ((0, 0), (0, 1), (1, 0)):
                                w = w1s[:, bass.ds(e, 1), c, wp, j * 128:(j + 1) * 128].rearrange("p o f -> p (o f)")
                                mm = pe.matmul(hidden(j), w, xs[u][:, c, xp, :], start=n == 0, stop=n == 3 * DC - 1)
                                n += 1
                        if j % HC == HC - 1:
                            mm.then_inc(h_ps, 1)

                def down(i, u, e, first):
                    if not first:
                        pe.wait_ge(y_ready, i - 1)
                    for t in range(RP):
                        for j in range(FC):
                            if t == 0 and j % HC == 0:
                                pe.wait_ge(h_split, 2 * i + j // HC + 1)
                            for hp, wp in ((0, 0), (0, 1), (1, 0)):
                                w = w2s[:, bass.ds(e, 1), j, wp, :].rearrange("p o d -> p (o d)")
                                mm = pe.matmul(ps[:, BY + u, t * D:(t + 1) * D], hs[u][:, j, hp, t * 128:(t + 1) * 128],
                                               w, start=j == 0 and hp == 0 and wp == 0, stop=j == FC - 1 and hp == 1)
                    mm.then_inc(y_ps, 1)

                def step(i, u, e, e_next, first=False, ahead=2):
                    if ahead:
                        up(i + 1, 1 - u, e_next)
                    if ahead > 1:
                        turn(i + 2, u)
                    down(i, u, e, first)

                turn(0, 0)
                e0, e1, e2 = (expert_of(i) for i in range(3))
                up(0, 0, e0, True)
                turn(1, 1)
                step(0, 0, e0, e1, True)
                step(1, 1, e1, e2, True)
                with pe.Fori(1, LOOPED) as k:
                    e0, e1, e2 = (expert_of(2 * k + d) for d in range(3))
                    step(2 * k, 0, e0, e1)
                    step(2 * k + 1, 1, e1, e2)
                left = range(2 * LOOPED, NTILE)
                of = [expert_of(i) for i in left] + [None]
                for n, i in enumerate(left):
                    step(i, i % 2, of[n], of[n + 1], ahead=min(2, NTILE - 1 - i))


_INS = ["x", "L0_tok_W_h", "L0_tok_b_h", "L0_tok_W_o", "L0_tok_b_o", "L0_tok_W_r", "L0_tok_b_r",
        "L0_attn_W_dq", "L0_attn_W_uq", "L0_attn_W_dkv", "L0_attn_W_uk", "L0_attn_W_uv", "L0_attn_W_o",
        "L0_ffn_router_w", "L0_ffn_router_b", "L0_ffn_w1", "L0_ffn_b1", "L0_ffn_w2", "L0_ffn_b2"]


def kernel(**inputs):
    import numpy as _np
    import concourse.bacc as _bacc
    from concourse.bass_utils import run_bass_kernel_spmd as _run

    nc = _bacc.Bacc("TRN2", target_bir_lowering=False, num_devices=1)
    arrays, args = {}, []
    for name in _INS:
        a = _np.ascontiguousarray(inputs[name])
        arrays[f"in_{name}"] = a
        args.append(nc.dram_tensor(f"in_{name}", a.shape, mybir.dt.from_np(a.dtype), kind="ExternalInput").ap())
    args.append(nc.dram_tensor("out_0", (B, S, D), F32, kind="ExternalOutput").ap())
    build(nc, *args)
    r = _run(nc, [arrays], core_ids=[0])
    return r.results[0]["out_0"]
```

```python
from contextlib import ExitStack

import concourse.bass as bass
from concourse import mybir

F32 = mybir.dt.float32
F32R = mybir.dt.float32r
BF16 = mybir.dt.bfloat16
I32 = mybir.dt.int32
U32 = mybir.dt.uint32
ALU = mybir.AluOpType
ACT = mybir.ActivationFunctionType
AX = mybir.AxisListType

B, L = 16, 4000
PATCH = 16
S = L // PATCH
TT = S // 2
NT = B * S // TT
NTOK = B * S
D = 256
DC = D // 128
I = 512
IC = I // 128
H, DK = 16, 16
LOW = 64
NG = H // 4
E, F, TOPK = 8, 1024, 2
FC = F // 128
EPS = 1e-5
NEG = -1e30
SCALE = float(DK) ** -0.5
XT_TERMS = 6 * PATCH
KX = XT_TERMS + 3
ROWS = 256
RP = ROWS // 128
REGION = 4256
NTILE = (NTOK * TOPK + E * (ROWS - 1)) // ROWS
PW = 272
NTAB = NTILE + 2
SPARE = E * REGION
STEPS = NTOK // ROWS + 1


def build(nc, x, W_h, b_h, tW_o, b_o, W_r, b_r, W_dq, W_uq, W_dkv, W_uk, W_uv, aW_o,
          router_w, router_b, w1, b1, w2, b2, out):
    with ExitStack() as ctx:
        def sem(name):
            return ctx.enter_context(nc.semaphore(name))

        def sb(name, shape, dt, c=ctx):
            return c.enter_context(nc.sbuf_tensor(name, shape, dt))

        acc = nc.dram_tensor("acc", (NTOK + ROWS, D), F32, kind="Internal").ap()
        rows = nc.dram_tensor("rows", (E * REGION + ROWS, PW), F32, kind="Internal").ap()

        ps = ctx.enter_context(nc.psum_tensor("ps", [128, 8, 512], F32))

        w1s = sb("w1s", [128, E, DC, 2, F], BF16)
        w2s = sb("w2s", [128, E, FC, 2, D], BF16)
        b1s = sb("b1s", [128, E, FC], F32)
        ident = sb("ident", [128, 128], F32)
        identb = sb("identb", [128, 128], BF16)
        table = sb("table", [1, 2, NTAB], I32)
        starts = sb("starts", [1, E], I32)
        count = sb("count", [128, E], F32)
        region0 = sb("region0", [128, E], F32)

        env = dict(locals())
        tokenizer(env, ctx)
        attention(env)
        experts(env)


def tokenizer(env, ctx):
    nc, ps, ident, identb = env["nc"], env["ps"], env["ident"], env["identb"]
    x, W_h, b_h, tW_o, b_o, W_r, b_r = (env[k] for k in ("x", "W_h", "b_h", "tW_o", "b_o", "W_r", "b_r"))
    acc, w1, w2, b1, w1s, w2s, b1s = (env[k] for k in ("acc", "w1", "w2", "b1", "w1s", "w2s", "b1s"))
    sem = env["sem"]
    NJ = IC + DC
    with ExitStack() as own:
        def sb(name, shape, dt):
            return own.enter_context(nc.sbuf_tensor(name, shape, dt))

        xin = sb("xin", [TT, NT, PATCH], F32)
        xres = sb("xres", [TT, NT, PATCH], F32)
        xst = sb("xst", [TT, NT, KX], BF16)
        win = sb("win", [128, NJ, 2 * PATCH], F32)
        wres = sb("wres", [128, NJ, PATCH], F32)
        wst = sb("wst", [128, NJ, KX], BF16)
        bin_ = sb("bin", [128, NJ], F32)
        bout = sb("bout", [128, DC], F32)
        bsum = sb("bsum", [128, NJ], F32)
        bres = sb("bres", [128, NJ], F32)
        won = sb("won", [128, DC, I], F32)
        xt = sb("xt", [KX, NT * TT], BF16)
        wt = sb("wt", [KX, NJ * 128], BF16)
        wot = sb("wot", [128, IC, D], F32)
        zrow = sb("zrow", [128, RP, D], F32)
        hid = [sb(f"hid{u}", [128, IC, S], F32) for u in range(2)]
        hout = [sb(f"hout{u}", [TT, 2, D], F32) for u in range(2)]
        wraw = [sb(f"wraw{u}", [128, 2 * F], F32) for u in range(2)]

        x_in, w_in, won_in, consts = sem("x_in"), sem("w_in"), sem("won_in"), sem("consts")
        id_zero, ident_ready = sem("id_zero"), sem("ident_ready")
        xst_ready, wst_ready = sem("xst_ready"), sem("wst_ready")
        xt_ps, wt_ps, won_ps = sem("xt_ps"), sem("wt_ps"), sem("won_ps")
        zero_out, b1_in = sem("zero_out"), sem("b1_in")

        w_loaded = [sem(f"w_loaded{u}") for u in range(2)]

        def load_w(sp, e, u):
            src = (w1 if u == 0 else w2)[bass.ds(e, 1), :, :]
            sp.dma_start(wraw[u][:, :].rearrange("p (c n) -> p c n", c=DC if u == 0 else FC),
                         src.rearrange("o (c p) n -> p (o c) n", p=128)).then_inc(w_loaded[u], 16)

        def split3(dve, src, rest, dst, terms):
            for k in range(3):
                first = terms[k][0]
                dve.tensor_copy(dst(first), src if k == 0 else rest)
                dve.drain()
                for t in terms[k][1:]:
                    dve.tensor_copy(dst(t), dst(first))
                if k < 2:
                    dve.tensor_tensor(rest, src if k == 0 else rest, dst(first), ALU.subtract)
                dve.drain()

        with nc.Block() as block:
            @block.sync
            def _(sp):
                sp.dma_start(xin[:, :, :], x.rearrange("b (t p i) -> p (b t) i", p=TT, i=PATCH)).then_inc(x_in, 16)
                sp.dma_start(win[:, 0:IC, :], W_h.rearrange("(c p) f -> p c f", p=128)).then_inc(w_in, 16)
                sp.dma_start(win[:, IC:NJ, :], W_r.rearrange("(c p) f -> p c f", p=128)).then_inc(w_in, 16)
                with nc.allow_non_contiguous_dma(reason="biases, once"):
                    sp.dma_start(bin_[:, 0:IC], b_h.rearrange("(c p) -> p c", p=128)).then_inc(w_in, 16)
                    sp.dma_start(bin_[:, IC:NJ], b_r.rearrange("(c p) -> p c", p=128)).then_inc(w_in, 16)
                    sp.dma_start(bout[:, :], b_o.rearrange("(c p) -> p c", p=128)).then_inc(w_in, 16)
                sp.dma_start(won[:, :, :], tW_o.rearrange("(c p) i -> p c i", p=128)).then_inc(won_in, 16)
                for u in range(2):
                    load_w(sp, 0, u)
                sp.wait_ge(consts, 1)
                sp.dma_start(acc[NTOK:NTOK + ROWS, :].rearrange("(t p) d -> p t d", p=128),
                             zrow[:, :, :]).then_inc(zero_out, 16)
                sp.wait_ge(zero_out, 16)

            @block.scalar
            def _(act):
                with nc.allow_non_contiguous_dma(reason="biases, once"):
                    for e in range(E):
                        act.dma_start(b1s[:, e, :], b1[e, :].rearrange("(c p) -> p c", p=128)).then_inc(b1_in, 16)
                act.wait_ge(b1_in, 16 * E)
                for k in range(2):
                    act.wait_ge(won_ps, k + 1)
                    act.copy(wot[:, 2 * k:2 * k + 2, :].rearrange("p c n -> p (c n)"),
                             ps[:, 5 + k, :])

            @block.gpsimd
            def _(pool):
                pool.memset(ident[:, :], 0.0).then_inc(id_zero, 1)
                pool.memset(identb[:, :], 0.0).then_inc(id_zero, 1)
                pool.memset(zrow[:, :, :], 0.0).then_inc(consts, 1)
                pool.wait_ge(id_zero, 2)
                for m in (ident, identb):
                    pool.affine_select(out=m[:, :], in_=m[:, :], compare_op=ALU.not_equal, fill=1.0, base=0,
                                       pattern=[[-1, 128]], channel_multiplier=1).then_inc(ident_ready, 1)

            @block.vector
            def _(dve):
                dve.memset(xst[:, :, XT_TERMS:KX], 1.0)
                dve.wait_ge(x_in, 16)
                split3(dve, xin[:, :, :], xres[:, :, :],
                       lambda t: xst[:, :, t * PATCH:(t + 1) * PATCH], [[0, 1, 2], [3, 4], [5]])
                dve.nop().then_inc(xst_ready, 1)
                dve.wait_ge(w_in, 80)
                dve.tensor_reduce(bsum[:, :], win[:, :, PATCH:2 * PATCH], AX.X, ALU.add)
                dve.drain()
                dve.tensor_tensor(bsum[:, :], bsum[:, :], bin_[:, :], ALU.add)
                dve.drain()
                dve.tensor_tensor(bsum[:, IC:NJ], bsum[:, IC:NJ], bout[:, :], ALU.add)
                dve.drain()
                split3(dve, win[:, :, 0:PATCH], wres[:, :, :],
                       lambda t: wst[:, :, t * PATCH:(t + 1) * PATCH], [[0, 3, 5], [1, 4], [2]])
                split3(dve, bsum[:, :], bres[:, :], lambda t: wst[:, :, XT_TERMS + t], [[0], [1], [2]])
                dve.nop().then_inc(wst_ready, 1)
                for k in range(4):
                    dve.wait_ge(xt_ps, k + 1)
                    dve.tensor_copy(xt[:, k * 8 * TT:(k + 1) * 8 * TT].rearrange("k (t n) -> k t n", n=TT),
                                    ps[0:KX, k, :].bitcast(BF16).rearrange("k (t n) -> k t n", n=128)[:, :, 0:TT]
                                    )
                dve.wait_ge(wt_ps, 1)
                dve.tensor_copy(wt[:, :], ps[0:KX, 4, :].bitcast(BF16)[:, 0:NJ * 128])

            @block.tensor
            def _(pe):
                pe.wait_ge(ident_ready, 2)
                pe.wait_ge(won_in, 16)
                for k in range(2):
                    for q in range(4):
                        c, n = 2 * k + q // 2, q % 2
                        mm = pe.transpose(ps[:, 5 + k, q * 128:(q + 1) * 128],
                                          won[:, n, c * 128:(c + 1) * 128], ident[:, :])
                    mm.then_inc(won_ps, 1)
                pe.wait_ge(xst_ready, 1)
                for t in range(NT):
                    mm = pe.transpose(ps[0:KX, t // 8, :].bitcast(BF16)[:, (t % 8) * 128:(t % 8) * 128 + TT],
                                      xst[:, t, :], identb[0:TT, 0:TT])
                    if t % 8 == 7:
                        mm.then_inc(xt_ps, 1)
                pe.wait_ge(wst_ready, 1)
                for c in range(NJ):
                    mm = pe.transpose(ps[0:KX, 4, :].bitcast(BF16)[:, c * 128:(c + 1) * 128],
                                      wst[:, c, :], identb[:, :])
                mm.then_inc(wt_ps, 1)

        hid_ps, hid_ready = sem("hid_ps"), sem("hid_ready")
        h_ps, h_ready = sem("h_ps"), sem("h_ready")
        h_stored = [sem(f"h_stored{u}") for u in range(2)]
        w_high, w_low = sem("w_high"), sem("w_low")

        with nc.Block() as block:
            @block.sync
            def _(sp):
                def pair(e, last):
                    for u in range(2):
                        if not last:
                            sp.wait_ge(w_high, 2 * e + u + 1)
                            sp.wait_ge(w_low, 2 * e + u + 1)
                            load_w(sp, e + 1, u)
                        sp.wait_ge(h_ready, 2 * e + u + 1)
                        sp.dma_start(acc[bass.ds((2 * e + u) * S, S), :].rearrange("(t p) d -> p t d", p=TT),
                                     hout[u][:, :, :]).then_inc(h_stored[u], 16)

                with sp.Fori(0, E - 1) as e:
                    pair(e, False)
                pair(E - 1, True)
                for u in range(2):
                    sp.wait_ge(h_stored[u], 16 * E)

            @block.scalar
            def _(act):
                def pair(e, first):
                    for u in range(2):
                        act.wait_ge(hid_ps, 2 * e + u + 1)
                        if not first:
                            act.wait_ge(h_ps, 2 * e + u - 1)
                        act.activation(hid[u][:, :, :].rearrange("p (k c) n -> p k (c n)", k=2),
                                       ps[:, 2 * u:2 * u + 2, 0:2 * S], ACT.Silu).then_inc(hid_ready, 1)
                        act.wait_ge(w_loaded[u], (e + 1) * 16)
                        ws, c = (w1s, DC) if u == 0 else (w2s, FC)
                        act.copy(ws[:, bass.ds(e, 1), :, 0, :].rearrange("p o c n -> p (o c) n"),
                                 wraw[u][:, :].rearrange("p (c n) -> p c n", c=c)).then_inc(w_high, 1)

                pair(0, True)
                with act.Fori(1, E) as e:
                    pair(e, False)

            @block.vector
            def _(dve):
                def pair(e, first):
                    for u in range(2):
                        dve.wait_ge(w_high, 2 * e + u + 1)
                        ws, c = (w1s, DC) if u == 0 else (w2s, FC)
                        dve.tensor_tensor(ws[:, bass.ds(e, 1), :, 1, :].rearrange("p o c n -> p (o c) n"),
                                          wraw[u][:, :].rearrange("p (c n) -> p c n", c=c),
                                          ws[:, bass.ds(e, 1), :, 0, :].rearrange("p o c n -> p (o c) n"),
                                          ALU.subtract).then_inc(w_low, 1)
                        dve.wait_ge(h_ps, 2 * e + u + 1)
                        if not first:
                            dve.wait_ge(h_stored[u], 16 * e)
                        dve.tensor_copy(hout[u][:, :, :].rearrange("p t d -> p (t d)"),
                                        ps[0:TT, 4 + u, :]).then_inc(h_ready, 1)

                pair(0, True)
                with dve.Fori(1, E) as e:
                    pair(e, False)

            @block.tensor
            def _(pe):
                def hidden(s, u):
                    for c in range(IC):
                        mm = pe.matmul(ps[:, 2 * u + c // 2, (c % 2) * S:(c % 2 + 1) * S],
                                       wt[:, c * 128:(c + 1) * 128], xt[:, bass.ds(s * S, S)], start=True, stop=True)
                    mm.then_inc(hid_ps, 1)

                def output(s, u, first):
                    if not first:
                        pe.wait_ge(h_ready, s - 1)
                    for t in range(2):
                        o = ps[0:TT, 4 + u, t * D:(t + 1) * D]
                        pe.matmul(o, xt[:, bass.ds(s * S + t * TT, TT)], wt[:, IC * 128:NJ * 128],
                                  start=True, stop=False)
                        if t == 0:
                            pe.wait_ge(hid_ready, s + 1)
                        for c in range(IC):
                            mm = pe.matmul(o, hid[u][:, c, t * TT:(t + 1) * TT], wot[:, c, :],
                                           start=False, stop=c == IC - 1)
                    mm.then_inc(h_ps, 1)

                def pair(e, first, last):
                    hidden(2 * e + 1, 1)
                    output(2 * e, 0, first)
                    if not last:
                        hidden(2 * e + 2, 0)
                    output(2 * e + 1, 1, first)

                hidden(0, 0)
                pair(0, True, False)
                with pe.Fori(1, E - 1) as e:
                    pair(e, False, False)
                pair(E - 1, False, True)


def attention(env):
    nc, ps, ident, identb, sem = env["nc"], env["ps"], env["ident"], env["identb"], env["sem"]
    W_dq, W_uq, W_dkv, W_uk, W_uv, aW_o = (env[k] for k in ("W_dq", "W_uq", "W_dkv", "W_uk", "W_uv", "aW_o"))
    router_w, router_b, acc, rows = (env[k] for k in ("router_w", "router_b", "acc", "rows"))
    count, region0, table, starts = env["count"], env["region0"], env["table"], env["starts"]
    HALF = TT + 1
    BS = HALF + S
    COPIES, SPAREB = (0, 1, 3), 2
    MAXROW = SPAREB * DK
    BQ, BK, BSC, BST, BO_, BM = 0, 1, 2, 4, 6, 7
    BR = BS + 2 * E
    LAST = B - 1

    with ExitStack() as own:
        def sb(name, shape, dt):
            return own.enter_context(nc.sbuf_tensor(name, shape, dt))

        wd = sb("wd", [128, DC, 2, 2, LOW], F32)
        wuh = [sb(f"wuh{k}", [128, H // 2, 2, 4, DK], F32R) for k in range(2)]
        wul = [sb(f"wul{k}", [128, H // 2, 2, 4, DK], F32R) for k in range(2)]
        wvh, wvl = sb("wvh", [128, D], F32R), sb("wvl", [128, D], F32R)
        wo = sb("wo", [128, DC, D], F32)
        rw = sb("rw", [128, DC, E], F32)
        rb = sb("rb", [TT, 1, E], F32)
        ccol = sb("ccol", [128, 4], F32)
        s_q, s_k, s_c, k_one = (ccol[:, j:j + 1] for j in range(4))
        mask_q = sb("mask_q", [TT, 2, HALF], BF16)
        mask_k = sb("mask_k", [TT, 2, HALF], BF16)
        below = sb("below", [TT, TT], BF16)
        ones = sb("ones", [TT, 128], BF16)
        iota_i = sb("iota_i", [TT, E], I32)
        iota_e = sb("iota_e", [TT, 1, E], F32)
        tok_i = sb("tok_i", [TT, 2], I32)
        token = sb("token", [TT, 2], F32)
        reg_i = sb("reg_i", [128, E], I32)
        minus_half = sb("minus_half", [TT, 2], F32)
        h_ln = sb("h_ln", [TT, 2, D], F32)
        h_new = sb("h_new", [TT, 2, D], F32)
        st6 = sb("st6", [TT, 2, 2, 6], F32)
        mv = sb("mv", [TT, 2, 2, 2], F32)
        var_e = sb("var_e", [TT, 2, 2], F32)
        rstd = sb("rstd", [TT, 2, 2], F32)
        less_mean = sb("less_mean", [TT, 2, 2], F32)
        shift = sb("shift", [TT, 2, 2], F32)
        xn = sb("xn", [TT, 2, D], F32)
        xnt = sb("xnt", [128, DC, S], F32)
        cs = sb("cs", [128, 2, S], F32R)
        q_r, k_r = sb("q_r", [128, 2, S], F32R), sb("k_r", [128, 2, S], F32R)
        c_r = q_r
        qs = sb("qs", [128, NG, 2, S], F32R)
        ks = sb("ks", [128, NG, 2, S], F32R)
        v = sb("v", [TT, 2, H, DK + 1], F32)
        mx = sb("mx", [TT, 2, 4], F32)
        mxt = sb("mxt", [TT, 2, 2, 2, LOW], F32)
        p_all = sb("p", [128, 2, 4, BS], F32)
        p = p_all[0:TT]
        setup_part = p_all[:, :, :, :].rearrange("p a h n -> p (a h n)")
        wu = setup_part[:, 0:3 * D].rearrange("p (k n) -> p k n", n=D)
        crow = setup_part[0:1, 3 * D:3 * D + 512].rearrange("p (k n) -> p k n", n=128)
        taken = [0]

        def carve(parts, shape, dt=F32):
            n = 1
            for k in shape:
                n *= k
            a = setup_part[0:parts, taken[0]:taken[0] + n]
            taken[0] += n
            a = a if dt is F32 else a.bitcast(dt)
            if len(shape) == 2:
                a = a.rearrange("p (a b) -> p a b", b=shape[1])
            return a

        step_i, tile_i, exp_i = (carve(1, [n], I32) for n in (STEPS, NTAB, E))
        step, tile, expert = carve(1, [1, STEPS]), carve(1, [NTAB, 1]), carve(1, [1, E])
        over, mine, work = carve(1, [E, STEPS]), carve(1, [NTAB, E]), carve(1, [NTAB, E])
        used, need, begin, base = (carve(1, [E]) for _ in range(4))
        ends = [carve(1, [E]) for _ in range(2)]
        row_f, any_f, exp_f = (carve(1, [NTAB]) for _ in range(3))
        part_i, part = carve(128, [RP], I32), carve(128, [RP])
        padding = carve(128, [RP, PW])
        os_ = sb("os", [128, NG, S], F32)
        rden = sb("rden", [TT, 2, H], F32)
        on = xn
        ont = xnt
        x2t = sb("x2t", [128, DC, S], F32)
        pay = sb("pay", [TT, 2, PW], F32)
        lg = sb("lg", [TT, 2, E], F32)
        lgx = sb("lgx", [TT, 2, E], F32)
        ex = sb("ex", [TT, 2, E], F32)
        small = sb("small", [TT, 2, 2], F32)
        top = sb("top", [TT, 2, 8], F32)
        topi = sb("topi", [TT, 2, 8], U32)
        topf = sb("topf", [TT, 2, 2], F32)
        hot = sb("hot", [TT, 2, 2, E], F32)
        hotb = sb("hotb", [TT, 2, E], BF16)
        rank = sb("rank", [TT, 2, E], F32)
        slotf = sb("slotf", [TT, 2, 2], F32)
        slot = sb("slot", [TT, 2, 2], I32)

        up_in, proj_in, ccol_in = sem("up_in"), sem("proj_in"), sem("ccol_in")
        crow_ready, up_high = sem("crow_ready"), sem("up_high")
        ln_loaded, res_loaded, scattered = sem("ln_loaded"), sem("res_loaded"), sem("scattered")

        def seq_rows(b):
            return acc[bass.ds(b * S, S), :].rearrange("(t p) d -> p t d", p=TT)

        def load_ln(sp, b):
            sp.dma_start(h_ln[:, :, :], seq_rows(b)).then_inc(ln_loaded, 16)

        def load_res(sp, b):
            sp.dma_start(h_new[:, :, :], seq_rows(b)).then_inc(res_loaded, 16)

        with nc.Block() as block:
            @block.sync
            def _(sp):
                for k, w in enumerate((W_uq, W_uk, W_uv)):
                    for r in range(2):
                        sp.dma_start(wu[r * LOW:(r + 1) * LOW, k, :], w).then_inc(up_in, 16)
                load_ln(sp, 0)
                sp.wait_ge(crow_ready, 1)
                with nc.allow_non_contiguous_dma(reason="512 factors, once"):
                    for j in range(4):
                        sp.dma_start(ccol[:, j:j + 1], crow[0:1, j, :]).then_inc(ccol_in, 16)
                for k, w in enumerate((W_dq, W_dkv)):
                    for r in range(2):
                        sp.dma_start(wd[:, :, k, r, :], w.rearrange("(c p) l -> p c l", p=128)).then_inc(proj_in, 16)
                sp.dma_start(wo[:, :, :], aW_o.rearrange("(c p) n -> p c n", p=128)).then_inc(proj_in, 16)
                sp.dma_start(rw[:, :, :], router_w.rearrange("(c p) n -> p c n", p=128)).then_inc(proj_in, 16)
                sp.dma_start(rb[:, 0, :], router_b.rearrange("(o e) -> o e", o=1).broadcast_to([TT, E])
                             ).then_inc(proj_in, 16)
                load_res(sp, 0)
                sp.wait_ge(ccol_in, 64)

            @block.scalar
            def _(act):
                act.wait_ge(up_in, 96)
                for k in range(2):
                    for r in COPIES:
                        cp = act.activation(wuh[k][:, :, :, r, :],
                                            wu[:, k, :].rearrange("p (h a d) -> p h a d", a=2, d=DK), ACT.Copy)
                    cp.then_inc(up_high, 1)
                act.activation(wvh[:, :], wu[:, 2, :], ACT.Copy).then_inc(up_high, 1)

            @block.gpsimd
            def _(pool):
                for w in (*wuh, *wul):
                    pool.memset(w[:, :, :, SPAREB, :].bitcast(F32), 0.0)
                for m in (mask_q, mask_k, ones):
                    pool.memset(m[:, :] if m is ones else m[:, :, :], 1.0 if m is ones else 0.0)
                pool.memset(below[:, :], 1.0)
                pool.memset(mxt[:, :, :, :, :], 0.0)
                pool.memset(v[:, :, :, :], 0.0)
                pool.memset(minus_half[:, :], -0.5)
                pool.memset(pay[:, :, :], 0.0)
                pool.iota(iota_i[:, :], pattern=[[1, E]], base=0, channel_multiplier=0)
                pool.iota(tok_i[:, :], pattern=[[TT, 2]], base=0, channel_multiplier=1)
                pool.iota(reg_i[:, :], pattern=[[REGION, E]], base=0, channel_multiplier=0)
                pool.drain()
                pool.affine_select(out=mask_q[:, :, :], in_=mask_q[:, :, :], compare_op=ALU.is_ge, fill=NEG, base=0,
                                   pattern=[[1, 2], [-1, HALF]], channel_multiplier=1)
                pool.affine_select(out=mask_k[:, :, :], in_=mask_k[:, :, :], compare_op=ALU.is_ge, fill=NEG, base=0,
                                   pattern=[[-1, 2], [1, HALF]], channel_multiplier=-1)
                pool.affine_select(out=below[:, :], in_=below[:, :], compare_op=ALU.is_gt, fill=0.0, base=0,
                                   pattern=[[1, TT]], channel_multiplier=-1)
                pool.memset(v[:, :, :, DK:DK + 1], 1.0)
                pool.tensor_copy(iota_e[:, 0, :], iota_i[:, :])
                pool.tensor_copy(token[:, :], tok_i[:, :])
                pool.tensor_copy(region0[:, :], reg_i[:, :])
                pool.tensor_copy(count[:, :], reg_i[:, :])
                pool.drain()

            @block.vector
            def _(dve):
                dve.memset(crow[:, :, :], 0.0)
                dve.drain()
                for a in range(2):
                    o = a * LOW
                    dve.memset(crow[:, 0, o + DK:o + 2 * DK], -1.0)
                    dve.memset(crow[:, 1, o + 3 * DK:o + 4 * DK], -1.0)
                    dve.memset(crow[:, 1, o + MAXROW:o + MAXROW + 2], 1.0)
                    dve.memset(crow[:, 3, o + MAXROW:o + MAXROW + 2], 1.0)
                dve.memset(crow[:, 2, LOW:128], -1.0)
                dve.drain()
                dve.nop().then_inc(crow_ready, 1)
                dve.memset(ps[:, BO_, 0:S], 0.0)
                for w in wul:
                    for r in COPIES:
                        dve.memset(w[LOW:128, :, :, r, :].bitcast(F32), 0.0)
                dve.memset(wvl[LOW:128, :].bitcast(F32), 0.0)
                for k in range(2):
                    dve.wait_ge(up_high, k + 1)
                    for r in COPIES:
                        dve.tensor_tensor(wul[k][0:LOW, :, :, r, :],
                                          wu[0:LOW, k, :].rearrange("p (h a d) -> p h a d", a=2, d=DK),
                                          wuh[k][0:LOW, :, :, 0, :], ALU.subtract)
                dve.wait_ge(up_high, 3)
                dve.tensor_tensor(wvl[0:LOW, :], wu[0:LOW, 2, :], wvh[0:LOW, :], ALU.subtract)
                dve.drain()

        q_ps, k_ps, q_round, k_round, q_split, k_split = (
            sem("q_ps"), sem("k_ps"), sem("q_round"), sem("k_round"), sem("q_split"), sem("k_split"))
        s_ps, max_read, max_rows, max_ps, q_aug = (
            sem("s_ps"), sem("max_read"), sem("max_rows"), sem("max_ps"), sem("q_aug"))
        st_ps, exp_done, pv_ps, o_read = sem("st_ps"), sem("exp_done"), sem("pv_ps"), sem("o_read")
        v_ps, v_ready, c_ps, c_round, c_split = (
            sem("v_ps"), sem("v_ready"), sem("c_ps"), sem("c_round"), sem("c_split"))
        turn_o_ps, o_normed, turn_n_ps, on_turned, ao_ps, h_done = (
            sem("turn_o_ps"), sem("o_normed"), sem("turn_n_ps"), sem("on_turned"), sem("ao_ps"), sem("h_done"))
        h_kept = sem("h_kept")
        base_ready, pads_ready, padded = sem("base_ready"), sem("pads_ready"), sem("padded")
        ln1_var, ln1_ready, xn_ready, xt_ps, xn_turned = (
            sem("ln1_var"), sem("ln1_ready"), sem("xn_ready"), sem("xn_ps"), sem("xn_turned"))
        ln2_var, ln2_ready, x2_ready, x2_ps, x2_turned = (
            sem("ln2_var"), sem("ln2_ready"), sem("x2_ready"), sem("x2_ps"), sem("x2_turned"))
        lg_ps, lg_ready, lg_exp, hot_ready, rank_ps, slots_ready = (
            sem("lg_ps"), sem("lg_ready"), sem("lg_exp"), sem("hot_ready"), sem("rank_ps"), sem("slots_ready"))
        rank_read = sem("rank_read")
        def pad(queue, experts_):
            for e in experts_:
                at = queue.value_load(starts[0:1, e:e + 1], min_val=0, max_val=SPARE)
                queue.dma_start(rows[bass.ds(at, ROWS), :].rearrange("(t p) w -> p t w", p=128),
                                padding).then_inc(padded, 16)

        with nc.Block() as block:
            @block.sync
            def _(sp):
                def keep(b):
                    sp.wait_ge(h_done, b + 1)
                    sp.dma_start(seq_rows(b), h_new[:, :, :]).then_inc(h_kept, 16)

                def ahead(b):
                    sp.wait_ge(xn_ready, b + 2)
                    load_ln(sp, b + 2)

                def residual(b):
                    sp.wait_ge(h_kept, 16 * b)
                    sp.wait_ge(x2_ready, b)
                    load_res(sp, b)

                ahead(-1)
                ahead(0)
                ahead(1)
                keep(0)
                with sp.Fori(2, LAST) as b:
                    ahead(b)
                    residual(b - 1)
                    keep(b - 1)
                for b in (LAST - 1, LAST):
                    residual(b)
                    keep(b)
                sp.wait_ge(pads_ready, 1)
                sp.dma_start(rows[SPARE:SPARE + ROWS, :].rearrange("(t p) w -> p t w", p=128),
                             padding).then_inc(padded, 16)
                pad(sp, range(0, E, 2))
                sp.wait_ge(padded, 16 * (E + 1))
                sp.wait_ge(h_kept, 16 * B)

            @block.scalar
            def _(act):
                def exps(n, g, q):
                    act.wait_ge(st_ps, 2 * n + q + 1)
                    act.activation(p[:, g % 2, 2 * q:2 * q + 2, :], ps[0:TT, BST:BST + 2, 0:BS],
                                   ACT.Exp, scale=SCALE).then_inc(exp_done, 1)

                def round_qk(m, g):
                    act.wait_ge(q_ps, m + 1)
                    act.activation(q_r[:, :, :].rearrange("p a n -> p (a n)"), ps[:, BQ, 0:2 * S],
                                   ACT.Copy).then_inc(q_round, 1)
                    act.wait_ge(k_ps, m + 1)
                    act.activation(k_r[:, :, :].rearrange("p a n -> p (a n)"), ps[:, BK, 0:2 * S],
                                   ACT.Identity, bias=k_one).then_inc(k_round, 1)

                def augment(n, g):
                    act.wait_ge(max_ps, n + 1)
                    for a in range(2):
                        row = slice(a * LOW + MAXROW, a * LOW + MAXROW + 2)
                        cp = act.activation(qs[row, g, :, :].rearrange("p a n -> p (a n)"), ps[row, BQ, 0:2 * S],
                                            ACT.Copy)
                    cp.then_inc(q_aug, 1)

                def round_c(b):
                    act.wait_ge(c_ps, b + 1)
                    act.activation(c_r[:, :, :].rearrange("p a n -> p (a n)"), ps[:, BM, 0:2 * S],
                                   ACT.Copy).then_inc(c_round, 1)

                def copy_v(b, first):
                    act.wait_ge(v_ps, b + 1)
                    if not first:
                        act.wait_ge(pv_ps, NG * b)
                    act.copy(v[:, :, :, 0:DK], ps[0:TT, BM, :].rearrange("p (t h d) -> p t h d", t=2, d=DK)
                             ).then_inc(v_ready, 1)

                def copy_o(n, g):
                    act.wait_ge(pv_ps, n + 1)
                    act.copy(os_[:, g, :], ps[:, BO_, 0:S]).then_inc(o_read, 1)

                def copy_turned(ready, b, dst, done):
                    act.wait_ge(ready, b + 1)
                    act.copy(dst[:, :, :].rearrange("p c n -> p (c n)"), ps[:, BM, 0:2 * S]).then_inc(done, 1)

                def exp_logits(b):
                    act.wait_ge(lg_ready, b + 1)
                    act.activation(ex[:, :, :], lgx[:, :, :], ACT.Exp).then_inc(lg_exp, 1)

                def normalise(h, k, dst, done):
                    for t in range(2):
                        ins = act.activation(dst[:, t, 0:D], h[:, t, :], ACT.Identity, bias=shift[:, k, t:t + 1],
                                             scale=rstd[:, k, t:t + 1])
                    ins.then_inc(done, 1)

                def ln1(b, turned=None, n=0):
                    act.wait_ge(ln1_ready, b + 1)
                    if turned is not None:
                        act.wait_ge(turned, n)
                    normalise(h_ln, 0, xn, xn_ready)

                def ln2(b, first=False):
                    act.wait_ge(ln2_ready, b + 1)
                    if not first:
                        act.wait_ge(scattered, 64 * b)
                    normalise(h_new, 1, pay, x2_ready)

                ln1(0)
                copy_turned(xt_ps, 0, xnt, xn_turned)
                ln1(1)
                round_c(0)
                copy_turned(xt_ps, 1, xnt, xn_turned)
                for m in range(3):
                    if m:
                        act.wait_ge(q_split, m)
                        act.wait_ge(k_split, m)
                    if m == 2:
                        augment(0, 0)
                    round_qk(m, m)

                def body(b, before, last):
                    back1, back2 = before > 0, before > 1
                    for d in range(NG):
                        n = NG * b + d
                        if d == 1 and back2:
                            ln2(b - 2, before == 2)
                        if back1 or d >= 2:
                            act.wait_ge(pv_ps, n - 1)
                        exps(n, d, 0)
                        if not (last and d > 0):
                            act.wait_ge(q_split, n + 3)
                            act.wait_ge(k_split, n + 3)
                            round_qk(n + 3, (d + 3) % NG)
                        if d == 3 and not last:
                            if back1:
                                ln1(b + 2, turn_n_ps, b)
                            else:
                                ln1(2)
                        if d == 2:
                            if back1:
                                act.wait_ge(turn_o_ps, 2 * b)
                            copy_o(n - 2, 0)
                        if d == 1 and back2:
                            copy_turned(x2_ps, b - 2, x2t, x2_turned)
                        if d == 0 and back1 or d > 1:
                            copy_o(n - 1, (d - 1) % NG)
                        if d == 0:
                            copy_v(b, not back1)
                        if d == 2 and back1:
                            copy_turned(turn_n_ps, b - 1, ont, on_turned)
                        if not (last and d == 3):
                            augment(n + 1, (d + 1) % NG)
                        if d == 0 and not last:
                            round_c(b + 1)
                        exps(n, d, 1)
                        if d == 2 and back2:
                            exp_logits(b - 2)
                        if d == 3 and not last:
                            copy_turned(xt_ps, b + 2, xnt, xn_turned)

                for b in range(3):
                    body(b, b, False)
                with act.Fori(3, LAST) as b:
                    body(b, 3, False)
                body(LAST, 3, True)
                copy_o(NG * B - 1, NG - 1)
                ln2(LAST - 1)
                copy_turned(x2_ps, LAST - 1, x2t, x2_turned)
                copy_turned(turn_n_ps, LAST, ont, on_turned)
                exp_logits(LAST - 1)
                ln2(LAST)
                copy_turned(x2_ps, LAST, x2t, x2_turned)
                exp_logits(LAST)
                act.wait_ge(pads_ready, 1)
                pad(act, range(1, E, 2))

            @block.gpsimd
            def _(pool):
                def factors(b, k, var_ready, done):
                    pool.wait_ge(var_ready, b + 1)
                    pool.tensor_tensor(rstd[:, k, :], var_e[:, k, :], minus_half[:, :], ALU.pow)
                    pool.drain()
                    pool.tensor_tensor(shift[:, k, :], less_mean[:, k, :], rstd[:, k, :], ALU.mult).then_inc(done, 1)

                def scatter(placed):
                    pool.wait_ge(ln1_var, 1)
                    pool.wait_ge(slots_ready, placed)
                    for t in range(2):
                        for k in range(2):
                            pool.indirect_dma_start(
                                out=rows[:, :], out_offset=bass.IndirectOffsetOnAxis(ap=slot[:, t, k:k + 1], axis=0),
                                in_=pay[:, t, :], in_offset=None).then_inc(scattered, 16)

                for b in range(4):
                    factors(b, 0, ln1_var, ln1_ready)
                factors(0, 1, ln2_var, ln2_ready)
                with pool.Fori(1, LAST - 1) as placed:
                    factors(placed + 3, 0, ln1_var, ln1_ready)
                    scatter(placed)
                    factors(placed, 1, ln2_var, ln2_ready)
                for b in (LAST - 1, LAST):
                    scatter(b)
                    factors(b, 1, ln2_var, ln2_ready)
                pool.wait_ge(pv_ps, NG * B)
                pool.iota(step_i, pattern=[[ROWS, STEPS]], base=0, channel_multiplier=0)
                pool.iota(tile_i, pattern=[[1, NTAB]], base=0, channel_multiplier=0)
                pool.iota(exp_i, pattern=[[1, E]], base=0, channel_multiplier=0)
                pool.iota(part_i, pattern=[[128, RP]], base=0, channel_multiplier=1)
                pool.memset(padding, 0.0)
                pool.drain()
                pool.nop().then_inc(base_ready, 1)
                scatter(B)
                pool.wait_ge(scattered, 64 * B)

            @block.vector
            def _(dve):
                def split(out, r, factor, src, done):
                    dve.scalar_tensor_tensor(out=out, in0=r, scalar=factor, in1=src,
                                             op0=ALU.mult, op1=ALU.add).then_inc(done, 1)

                def split_qk(m, g):
                    dve.wait_ge(q_round, m + 1)
                    split(qs[:, g, :, :].rearrange("p a n -> p (a n)"), q_r[:, :, :].rearrange("p a n -> p (a n)"),
                          s_q, ps[:, BQ, 0:2 * S], q_split)
                    dve.wait_ge(k_round, m + 1)
                    split(ks[:, g, :, :].rearrange("p a n -> p (a n)"), k_r[:, :, :].rearrange("p a n -> p (a n)"),
                          s_k, ps[:, BK, 0:2 * S], k_split)

                def split_c(b):
                    dve.wait_ge(c_round, b + 1)
                    split(cs[:, :, :].rearrange("p a n -> p (a n)"), c_r[:, :, :].rearrange("p a n -> p (a n)"),
                          s_c, ps[:, BM, 0:2 * S], c_split)

                def maxima(m, q, first=False):
                    if q == 0 and not first:
                        dve.wait_ge(max_rows, m)
                    dve.wait_ge(s_ps, 2 * m + q + 1)
                    dve.tensor_reduce(mx[:, 0, 2 * q:2 * q + 2], ps[0:TT, BSC:BSC + 2, 0:HALF], AX.X, ALU.max)
                    dve.tensor_reduce(mx[:, 1, 2 * q:2 * q + 2], ps[0:TT, BSC:BSC + 2, HALF:BS], AX.X,
                                      ALU.max).then_inc(max_read, 1)

                def rows_of_max(m, first=False):
                    dve.drain()
                    if not first:
                        dve.wait_ge(max_ps, m)
                    m4 = mx[:, :, :].rearrange("p t (r a) -> p t r a", a=2)
                    dve.tensor_scalar(mxt[:, :, :, :, MAXROW].bitcast(F32R), m4, -1.0, None, ALU.mult)
                    dve.drain()
                    dve.scalar_tensor_tensor(out=mxt[:, :, :, :, MAXROW + 1].bitcast(F32R), in0=m4, scalar=-1.0,
                                             in1=mxt[:, :, :, :, MAXROW], op0=ALU.mult,
                                             op1=ALU.subtract).then_inc(max_rows, 1)

                def norm_o(b, t):
                    dve.wait_ge(turn_o_ps, 2 * b + t + 1)
                    o = ps[0:TT, BM, :].rearrange("p (h c) -> p h c", c=32)
                    dve.reciprocal(rden[:, t, :], o[:, :, DK])
                    dve.drain()
                    dve.tensor_tensor(on[:, t, :].rearrange("p (h c) -> p h c", c=DK), o[:, :, 0:DK],
                                      rden[:, t, :].unsqueeze(2).broadcast_to([TT, H, DK]),
                                      ALU.mult).then_inc(o_normed, 1)

                def stats(h, k, done):
                    for t in range(2):
                        dve.bn_stats(st6[:, k, t, :], h[:, t, :])
                    dve.drain()
                    for t in range(2):
                        dve.bn_aggr(mv[:, k, t, :], st6[:, k, t, :])
                    dve.drain()
                    dve.tensor_scalar(less_mean[:, k, :], mv[:, k, :, 0], -1.0, None, ALU.mult)
                    dve.tensor_scalar(var_e[:, k, :], mv[:, k, :, 1], EPS, None, ALU.add).then_inc(done, 1)

                def ln1_stats(b):
                    dve.wait_ge(ln_loaded, 16 * b + 16)
                    stats(h_ln, 0, ln1_var)

                def add_res(b, first):
                    dve.wait_ge(ao_ps, b + 1)
                    dve.wait_ge(res_loaded, 16 * b + 16)
                    if not first:
                        dve.wait_ge(h_kept, 16 * b)
                    dve.tensor_tensor(h_new[:, :, :].rearrange("p t d -> p (t d)"), ps[0:TT, BM, :],
                                      h_new[:, :, :].rearrange("p t d -> p (t d)"), ALU.add).then_inc(h_done, 1)

                def ln2_stats():
                    dve.drain()
                    stats(h_new, 1, ln2_var)

                def logits(b):
                    dve.wait_ge(lg_ps, b + 1)
                    dve.tensor_tensor(lg[:, :, :], ps[0:TT, BSC, BS:BS + 2 * E].rearrange("p (t e) -> p t e", e=E),
                                      rb[:, :, :].broadcast_to([TT, 2, E]), ALU.add)
                    dve.drain()
                    for t in range(2):
                        dve.max(top[:, t, :], lg[:, t, :])
                    dve.drain()
                    dve.tensor_tensor(lgx[:, :, :], lg[:, :, :], top[:, :, 0:1].broadcast_to([TT, 2, E]),
                                      ALU.subtract).then_inc(lg_ready, 1)

                def choose(b):
                    for t in range(2):
                        dve.max_index(topi[:, t, :], top[:, t, :], lg[:, t, :])
                    dve.drain()
                    dve.tensor_copy(topf[:, :, :], topi[:, :, 0:2])
                    dve.drain()
                    for k in range(2):
                        dve.tensor_tensor(hot[:, k, :, :], iota_e[:, :, :].broadcast_to([TT, 2, E]),
                                          topf[:, :, k:k + 1].broadcast_to([TT, 2, E]), ALU.is_equal)
                    dve.drain()
                    dve.tensor_tensor(hotb[:, :, :], hot[:, 0, :, :], hot[:, 1, :, :], ALU.add).then_inc(hot_ready, 1)

                def gates(b):
                    dve.wait_ge(lg_exp, b + 1)
                    dve.tensor_reduce(small[:, 0, :], ex[:, :, :], AX.X, ALU.add)
                    dve.drain()
                    dve.reciprocal(small[:, 1, :], small[:, 0, :])
                    dve.drain()
                    dve.tensor_tensor(ex[:, :, :], ex[:, :, :],
                                      small[:, 1, :].unsqueeze(2).broadcast_to([TT, 2, E]), ALU.mult)
                    dve.drain()
                    dve.tensor_tensor(pay[:, :, D:D + E], ex[:, :, :], hotb[:, :, :], ALU.mult)
                    dve.tensor_copy(pay[:, :, D + E], token[:, :])
                    dve.drain()
                    dve.tensor_scalar(token[:, :], token[:, :], float(S), None, ALU.add)

                def take_ranks(b):
                    dve.wait_ge(rank_ps, b + 1)
                    dve.tensor_tensor(rank[:, :, :],
                                      ps[0:TT, BSC, BR:BR + 2 * E].rearrange("p (t e) -> p t e", e=E),
                                      count[0:TT, :].unsqueeze(1).broadcast_to([TT, 2, E]), ALU.add)
                    dve.drain()
                    dve.tensor_tensor(count[:, :], count[:, :], ps[:, BSC, BR + 2 * E:BR + 3 * E],
                                      ALU.add).then_inc(rank_read, 1)

                def place(b):
                    for k in range(2):
                        dve.tensor_tensor(hot[:, k, :, :], hot[:, k, :, :], rank[:, :, :], ALU.mult)
                    dve.drain()
                    for k in range(2):
                        dve.tensor_reduce(slotf[:, :, k:k + 1], hot[:, k, :, :], AX.X, ALU.add)
                    dve.drain()
                    dve.tensor_copy(slot[:, :, :], slotf[:, :, :]).then_inc(slots_ready, 1)

                ln1_stats(0)
                dve.wait_ge(xn_ready, 1)
                ln1_stats(1)
                split_c(0)
                dve.wait_ge(proj_in, 16 * 7)
                split_qk(0, 0)
                for m in range(2):
                    maxima(m, 0, m == 0)
                    split_qk(m + 1, m + 1)
                    maxima(m, 1)
                    rows_of_max(m, m == 0)

                def body(b, before, last):
                    back1, back2 = before > 0, before > 1
                    for d in range(NG):
                        n = NG * b + d
                        more = not (last and d > 1)
                        if d == 2 and back2:
                            if more:
                                dve.wait_ge(s_ps, 2 * n + 5)
                            logits(b - 2)
                        if more:
                            maxima(n + 2, 0)
                        if d == 3 and back1:
                            add_res(b - 1, not back2)
                        if not (last and d > 0):
                            if back1 or d > 0:
                                dve.wait_ge(st_ps, 2 * n)
                            split_qk(n + 3, (d + 3) % NG)
                        if d == 2 and back1:
                            norm_o(b - 1, 1)
                        if d == 3 and back2:
                            if more:
                                dve.wait_ge(s_ps, 2 * n + 6)
                            take_ranks(b - 2)
                        if more:
                            maxima(n + 2, 1)
                        if more:
                            rows_of_max(n + 2)
                        if d == 0 and back2:
                            ln2_stats()
                        if d == 0 and not last:
                            split_c(b + 1)
                        if d == 1 and back1:
                            norm_o(b - 1, 0)
                        if d == 1 and not last:
                            ln1_stats(b + 2)
                        if d == 2 and back2:
                            choose(b - 2)
                            gates(b - 2)
                        if d == 3 and back2:
                            place(b - 2)

                for b in range(3):
                    body(b, b, False)
                with dve.Fori(3, LAST) as b:
                    body(b, 3, False)
                body(LAST, 3, True)
                ln2_stats()
                norm_o(LAST, 0)
                norm_o(LAST, 1)
                logits(LAST - 1)
                choose(LAST - 1)
                gates(LAST - 1)
                take_ranks(LAST - 1)
                place(LAST - 1)
                add_res(LAST, False)
                ln2_stats()
                logits(LAST)
                choose(LAST)
                gates(LAST)
                take_ranks(LAST)
                place(LAST)

                def tt(o, a, b, op):
                    dve.tensor_tensor(o, a, b, op)
                    dve.drain()

                dve.wait_ge(base_ready, 1)
                dve.tensor_copy(part[:, :], part_i[:, :])
                dve.tensor_copy(step[:, 0, :], step_i[:, :])
                dve.tensor_copy(tile[:, :, 0], tile_i[:, :])
                dve.tensor_copy(expert[:, 0, :], exp_i[:, :])
                dve.drain()
                dve.tensor_scalar(padding[:, :, D + E], part[:, :], float(NTOK), None, ALU.add)
                dve.tensor_copy(starts[:, :], count[0:1, :])
                dve.drain()
                dve.nop().then_inc(pads_ready, 1)
                tt(used[:, :], count[0:1, :], region0[0:1, :], ALU.subtract)
                tt(over[:, :, :], used[:, :].unsqueeze(2).broadcast_to([1, E, STEPS]),
                   step[:, :, :].broadcast_to([1, E, STEPS]), ALU.is_gt)
                dve.tensor_reduce(need[:, :], over[:, :, :], AX.X, ALU.add)
                dve.drain()
                src = need
                for k, shift in enumerate((1, 2, 4)):
                    dst = ends[k % 2]
                    dve.tensor_copy(dst[:, 0:shift], src[:, 0:shift])
                    tt(dst[:, shift:E], src[:, shift:E], src[:, 0:E - shift], ALU.add)
                    src = dst
                last = src
                tt(begin[:, :], last[:, :], need[:, :], ALU.subtract)
                dve.scalar_tensor_tensor(out=base[:, :], in0=begin[:, :], scalar=-float(ROWS), in1=region0[0:1, :],
                                         op0=ALU.mult, op1=ALU.add)
                dve.drain()
                wide = [1, NTAB, E]
                tt(mine[:, :, :], tile[:, :, :].broadcast_to(wide),
                   begin[:, :].unsqueeze(1).broadcast_to(wide), ALU.is_ge)
                tt(work[:, :, :], tile[:, :, :].broadcast_to(wide),
                   last[:, :].unsqueeze(1).broadcast_to(wide), ALU.is_lt)
                tt(mine[:, :, :], mine[:, :, :], work[:, :, :], ALU.mult)
                tt(work[:, :, :], mine[:, :, :], expert[:, :, :].broadcast_to(wide), ALU.mult)
                dve.tensor_reduce(exp_f[:, :], work[:, :, :], AX.X, ALU.add)
                dve.tensor_reduce(any_f[:, :], mine[:, :, :], AX.X, ALU.add)
                dve.drain()
                tt(work[:, :, :], mine[:, :, :], base[:, :].unsqueeze(1).broadcast_to(wide), ALU.mult)
                dve.tensor_reduce(row_f[:, :], work[:, :, :], AX.X, ALU.add)
                dve.drain()
                dve.scalar_tensor_tensor(out=tile[:, :, 0], in0=tile[:, :, 0], scalar=float(ROWS), in1=any_f[:, :],
                                         op0=ALU.mult, op1=ALU.mult)
                dve.drain()
                tt(row_f[:, :], row_f[:, :], tile[:, :, 0], ALU.add)
                dve.scalar_tensor_tensor(out=row_f[:, :], in0=any_f[:, :], scalar=-float(SPARE), in1=row_f[:, :],
                                         op0=ALU.mult, op1=ALU.add)
                dve.drain()
                dve.tensor_scalar(row_f[:, :], row_f[:, :], float(SPARE), None, ALU.add)
                dve.drain()
                dve.tensor_copy(table[:, 0, :], row_f[:, :])
                dve.tensor_copy(table[:, 1, :], exp_f[:, :])
                dve.drain()

            @block.tensor
            def _(pe):
                def project(m, g):
                    for k, bank, done in ((0, BQ, q_ps), (1, BK, k_ps)):
                        for r in range(2):
                            o = ps[:, bank, r * S:(r + 1) * S]
                            w = 2 * g + r
                            pe.matmul(o, wuh[k][:, w, :, :, :].rearrange("p a r d -> p (a r d)"), cs[:, k, :],
                                      start=True, stop=False)
                            mm = pe.matmul(o, wul[k][:, w, :, :, :].rearrange("p a r d -> p (a r d)"), cs[:, k, :],
                                           start=False, stop=True)
                        mm.then_inc(done, 1)

                def masked(bank, mask, parts):
                    both = ps[0:TT, bank, 0:2 * S].rearrange("p (k n) -> p k n", k=2)[:, :, 0:HALF]
                    pe.matmul(both, identb[0:TT, 0:TT], mask[:, :, :], start=True, stop=False,
                              skip_group_check=True)
                    for lhs, rhs, o in parts:
                        mm = pe.matmul(o, lhs, rhs, start=False, stop=True, skip_group_check=True)
                    return mm

                def scores(m, g, q):
                    for a in range(2):
                        rr = slice(a * LOW, (a + 1) * LOW)
                        mm = masked(BSC + a, mask_q, [
                            (qs[rr, g, q, 0:TT], ks[rr, g, q, 0:HALF], ps[0:TT, BSC + a, 0:HALF]),
                            (qs[rr, g, q, TT:S], ks[rr, g, q, :], ps[0:TT, BSC + a, HALF:BS])])
                    mm.then_inc(s_ps, 1)

                def scores_t(n, g, q):
                    for a in range(2):
                        rr = slice(a * LOW, (a + 1) * LOW)
                        mm = masked(BST + a, mask_k, [
                            (ks[rr, g, q, 0:TT], qs[rr, g, q, :], ps[0:TT, BST + a, 0:S]),
                            (ks[rr, g, q, TT:S], qs[rr, g, q, S - HALF:S], ps[0:TT, BST + a, S:BS])])
                    mm.then_inc(st_ps, 1)

                def values(n, g):
                    for j in range(4):
                        h = 4 * g + j
                        o = ps[32 * j:32 * j + DK + 1, BO_, 0:S]
                        pe.matmul(o, v[:, 0, h, :], p[:, g % 2, j, 0:S], start=True, stop=False,
                                  skip_group_check=True)
                        mm = pe.matmul(o[:, S - HALF:S], v[:, 1, h, :], p[:, g % 2, j, S:BS], start=False, stop=True,
                                       skip_group_check=True)
                    mm.then_inc(pv_ps, 1)

                def turn_max(n, g):
                    for r in range(2):
                        for t in range(2):
                            mm = pe.transpose(ps[:, BQ, r * S + t * TT:r * S + (t + 1) * TT],
                                              mxt[:, t, r, :, :].rearrange("p a c -> p (a c)"), ident[0:TT, 0:TT])
                    mm.then_inc(max_ps, 1)

                def values_of(b):
                    for t in range(2):
                        o = ps[0:TT, BM, t * D:(t + 1) * D]
                        c = cs[:, 1, t * TT:(t + 1) * TT]
                        pe.matmul(o, c, wvh[:, :], start=True, stop=False)
                        mm = pe.matmul(o, c, wvl[:, :], start=False, stop=True)
                    mm.then_inc(v_ps, 1)

                def compress(b):
                    for k in range(2):
                        for c in range(DC):
                            mm = pe.matmul(ps[:, BM, k * S:(k + 1) * S],
                                           wd[:, c, k, :, :].rearrange("p r l -> p (r l)"), xnt[:, c, :],
                                           start=c == 0, stop=c == DC - 1)
                    mm.then_inc(c_ps, 1)

                def turn(src, done):
                    for c in range(DC):
                        for t in range(2):
                            mm = pe.transpose(ps[:, BM, c * S + t * TT:c * S + (t + 1) * TT],
                                              src[:, t, c * 128:(c + 1) * 128], ident[0:TT, 0:TT])
                    mm.then_inc(done, 1)

                def turn_o(t):
                    for g in range(NG):
                        mm = pe.transpose(ps[0:TT, BM, g * 128:(g + 1) * 128],
                                          os_[:, g, t * TT:(t + 1) * TT], ident[:, :])
                    mm.then_inc(turn_o_ps, 1)

                def out_proj():
                    for t in range(2):
                        for c in range(DC):
                            mm = pe.matmul(ps[0:TT, BM, t * D:(t + 1) * D], ont[:, c, t * TT:(t + 1) * TT],
                                           wo[:, c, :], start=c == 0, stop=c == DC - 1)
                    mm.then_inc(ao_ps, 1)

                def route_logits():
                    for t in range(2):
                        for c in range(DC):
                            mm = pe.matmul(ps[0:TT, BSC, BS + t * E:BS + (t + 1) * E], x2t[:, c, t * TT:(t + 1) * TT],
                                           rw[:, c, :], start=c == 0, stop=c == DC - 1)
                    mm.then_inc(lg_ps, 1)

                def ranks():
                    o = [ps[0:TT if k < 2 else 128, BSC, BR + k * E:BR + (k + 1) * E] for k in range(3)]
                    pe.matmul(o[0], below[:, :], hotb[:, 0, :], start=True, stop=True)
                    pe.matmul(o[1], below[:, :], hotb[:, 1, :], start=True, stop=False)
                    pe.matmul(o[1], ones[:, 0:TT], hotb[:, 0, :], start=False, stop=True)
                    pe.matmul(o[2], ones[:, :], hotb[:, 0, :], start=True, stop=False)
                    pe.matmul(o[2], ones[:, :], hotb[:, 1, :], start=False, stop=True).then_inc(rank_ps, 1)

                pe.wait_ge(xn_ready, 1)
                turn(xn, xt_ps)
                pe.wait_ge(xn_turned, 1)
                pe.wait_ge(proj_in, 16 * 7)
                compress(0)
                pe.wait_ge(xn_ready, 2)
                pe.wait_ge(c_split, 1)
                turn(xn, xt_ps)
                project(0, 0)
                for m in range(2):
                    pe.wait_ge(q_split, m + 1)
                    pe.wait_ge(k_split, m + 1)
                    if m:
                        pe.wait_ge(max_read, 2)
                    scores(m, m, 0)
                    if m:
                        pe.wait_ge(q_aug, 1)
                    project(m + 1, m + 1)
                    pe.wait_ge(max_read, 2 * m + 1)
                    scores(m, m, 1)
                    if m == 0:
                        pe.wait_ge(max_rows, 1)
                        pe.wait_ge(q_split, 2)
                        turn_max(0, 0)

                def body(b, before, last):
                    back1, back2 = before > 0, before > 1
                    for d in range(NG):
                        n = NG * b + d
                        proj, ahead, turned = not (last and d > 0), not (last and d > 1), not (last and d == 3)
                        if d == 2 and back2:
                            pe.wait_ge(x2_turned, b - 1)
                            pe.wait_ge(max_read, 2 * n + 4)
                            route_logits()
                        if ahead:
                            pe.wait_ge(k_split, n + 3)
                            pe.wait_ge(max_read, 2 * n + 4)
                            scores(n + 2, (d + 2) % NG, 0)
                        pe.wait_ge(q_aug, n + 1)
                        if back1 or d > 0:
                            pe.wait_ge(exp_done, 2 * n)
                        scores_t(n, d, 0)
                        if proj:
                            pe.wait_ge(c_split, b + 1 if d == 0 else b + 2)
                            pe.wait_ge(k_split, n + 3)
                            project(n + 3, (d + 3) % NG)
                        if d == 1 and back2:
                            if last:
                                pe.wait_ge(v_ready, B)
                            pe.wait_ge(x2_ready, b - 1)
                            turn(pay, x2_ps)
                        if d == 2 and back1:
                            pe.wait_ge(o_normed, 2 * b - 1)
                            turn_o(1)
                        if d == 0:
                            pe.wait_ge(xn_turned, b + 2)
                            values_of(b)
                        if back1 or d > 0:
                            if d == 1:
                                pe.wait_ge(v_ready, b + 1)
                            if back1 or d > 1:
                                pe.wait_ge(o_read, n - 1)
                            values(n - 1, (d - 1) % NG)
                        if d == 3 and back2:
                            pe.wait_ge(hot_ready, b - 1)
                            if not last:
                                pe.wait_ge(max_read, 2 * n + 5)
                            ranks()
                        if ahead:
                            pe.wait_ge(max_read, 2 * n + 5)
                            scores(n + 2, (d + 2) % NG, 1)
                        if d == 1 and back1:
                            pe.wait_ge(o_read, NG * b)
                            if back2:
                                pe.wait_ge(x2_turned, b - 1)
                            else:
                                pe.wait_ge(c_split, b + 2)
                            turn_o(0)
                        if d == 2 and back1:
                            pe.wait_ge(o_normed, 2 * b)
                            turn(on, turn_n_ps)
                        if turned:
                            pe.wait_ge(max_rows, n + 2)
                            if proj:
                                pe.wait_ge(q_split, n + 4)
                            turn_max(n + 1, (d + 1) % NG)
                        if d == 0 and not last:
                            pe.wait_ge(v_ready, b + 1)
                            compress(b + 1)
                        pe.wait_ge(exp_done, 2 * n + 1)
                        scores_t(n, d, 1)
                        if d == 2 and back1:
                            pe.wait_ge(on_turned, b)
                            out_proj()
                        if d == 3 and not last:
                            if back1:
                                pe.wait_ge(h_done, b)
                            else:
                                pe.wait_ge(c_split, b + 2)
                            pe.wait_ge(xn_ready, b + 3)
                            turn(xn, xt_ps)

                for b in range(3):
                    body(b, b, False)
                with pe.Fori(3, LAST) as b:
                    body(b, 3, False)
                body(LAST, 3, True)
                pe.wait_ge(exp_done, 2 * NG * B)
                pe.wait_ge(o_read, NG * B - 1)
                values(NG * B - 1, NG - 1)
                pe.wait_ge(o_read, NG * B)
                pe.wait_ge(h_done, LAST)
                turn_o(0)
                pe.wait_ge(o_normed, 2 * B - 1)
                turn_o(1)
                pe.wait_ge(x2_ready, LAST)
                pe.wait_ge(o_normed, 2 * B)
                turn(pay, x2_ps)
                pe.wait_ge(x2_turned, LAST)
                pe.wait_ge(rank_read, LAST - 1)
                route_logits()
                turn(on, turn_n_ps)
                pe.wait_ge(hot_ready, LAST)
                ranks()
                pe.wait_ge(on_turned, B)
                out_proj()
                pe.wait_ge(x2_ready, B)
                pe.wait_ge(h_done, B)
                turn(pay, x2_ps)
                pe.wait_ge(x2_turned, B)
                pe.wait_ge(rank_read, LAST)
                route_logits()
                pe.wait_ge(hot_ready, B)
                ranks()


def experts(env):
    nc, ps, ident, sem = env["nc"], env["ps"], env["ident"], env["sem"]
    acc, rows, out, b2 = (env[k] for k in ("acc", "rows", "out", "b2"))
    w1s, w2s, b1s, table = (env[k] for k in ("w1s", "w2s", "b1s", "table"))
    with ExitStack() as own:
        def sb(name, shape, dt):
            return own.enter_context(nc.sbuf_tensor(name, shape, dt))

        b2_all = sb("b2_all", [128, E, D], F32)
        target = sb("target", [128, RP], I32)
        zero = sb("zero", [128, RP], I32)
        b2_in = sem("b2_in")

        pay = [sb(f"tile_in{u}", [128, RP, PW], F32) for u in range(2)]
        xs = [sb(f"xs{u}", [128, DC, 2, ROWS], BF16) for u in range(2)]
        hg = [sb(f"hg{u}", [128, FC, ROWS], F32) for u in range(2)]
        hs = [sb(f"hs{u}", [128, FC, 2, ROWS], BF16) for u in range(2)]
        yt = [sb(f"yt{u}", [128, RP, D], F32) for u in range(2)]
        gate = [sb(f"gate{u}", [128, RP], F32) for u in range(2)]
        tokf = [sb(f"tokf{u}", [128, RP], F32) for u in range(2)]
        toki = [sb(f"toki{u}", [128, RP], I32) for u in range(2)]

        rows_in = [sem(f"rows_in{u}") for u in range(2)]
        xt_ps, x_high, x_split, meta_read = sem("rows_ps"), sem("x_high"), sem("x_split"), sem("meta_read")
        h_ps, h_act, h_high, h_split = sem("up_ps"), sem("h_act"), sem("h_high"), sem("h_split")
        y_ps, y_ready, y_added = sem("y_ps"), sem("y_ready"), sem("y_added")
        out_done = sem("out_done")
        BT, BH, BY = 0, 1, 5
        JB = 512 // ROWS
        HC = FC // 2
        LOOPED = (NTILE - 2) // 2

        def hidden(j, n=1):
            if n == 1:
                return ps[:, BH + j // JB, (j % JB) * ROWS:(j % JB + 1) * ROWS]
            return ps[:, BH + j // JB:BH + (j + n) // JB, 0:JB * ROWS]

        with nc.Block() as block:
            @block.sync
            def _(sp):
                def load(i, u):
                    r = sp.value_load(table[0:1, 0, bass.ds(i, 1)], min_val=0, max_val=SPARE)
                    sp.dma_start(pay[u][:, :, :], rows[bass.ds(r, ROWS), :].rearrange("(t p) w -> p t w", p=128)
                                 ).then_inc(rows_in[u], 16)

                load(0, 0)
                load(1, 1)
                sp.dma_start(b2_all[:, :, :], b2.rearrange("(o e) d -> o e d", o=1).broadcast_to([128, E, D])
                             ).then_inc(b2_in, 16)

                def reload(i, u):
                    sp.wait_ge(xt_ps, i + 1)
                    sp.wait_ge(meta_read, i + 1)
                    load(i + 2, u)

                with sp.Fori(0, LOOPED) as k:
                    for u in range(2):
                        reload(2 * k + u, u)
                for i in range(2 * LOOPED, NTILE - 2):
                    reload(i, i % 2)
                sp.wait_ge(y_added, 16 * RP * NTILE)
                sp.dma_start(out.rearrange("b s d -> (b s d)").rearrange("(q n) -> q n", q=128),
                             acc[0:NTOK, :].rearrange("t d -> (t d)").rearrange("(q n) -> q n", q=128)
                             ).then_inc(out_done, 16)
                sp.wait_ge(out_done, 16)

            @block.scalar
            def _(act):
                def high_x(i, u):
                    act.wait_ge(xt_ps, i + 1)
                    act.copy(xs[u][:, :, 0, :], ps[:, BT, 0:DC * ROWS].rearrange("p (c n) -> p c n", c=DC)
                             ).then_inc(x_high, 1)

                def gelu(i, u):
                    e = act.value_load(table[0:1, 1, bass.ds(i, 1)], min_val=0, max_val=E - 1)
                    for j in range(FC):
                        if j % HC == 0:
                            act.wait_ge(h_ps, 2 * i + j // HC + 1)
                        ins = act.activation(hg[u][:, j, :], hidden(j), ACT.Gelu, bias=b1s[:, bass.ds(e, 1), j])
                        if j % HC == HC - 1:
                            ins.then_inc(h_act, 1)

                high_x(0, 0)
                gelu(0, 0)
                high_x(1, 1)

                def step(i, u, first=False, ahead=2):
                    if ahead:
                        if not first:
                            act.wait_ge(h_split, 2 * i)
                        gelu(i + 1, 1 - u)
                    if ahead > 1:
                        high_x(i + 2, u)

                step(0, 0, True)
                step(1, 1)
                with act.Fori(1, LOOPED) as k:
                    step(2 * k, 0)
                    step(2 * k + 1, 1)
                for i in range(2 * LOOPED, NTILE):
                    step(i, i % 2, ahead=min(2, NTILE - 1 - i))

            @block.vector
            def _(dve):
                def low_x(i, u):
                    dve.wait_ge(x_high, i + 1)
                    dve.tensor_tensor(xs[u][:, :, 1, :], ps[:, BT, 0:DC * ROWS].rearrange("p (c n) -> p c n", c=DC),
                                      xs[u][:, :, 0, :], ALU.subtract).then_inc(x_split, 1)

                def meta(i, u):
                    e = dve.value_load(table[0:1, 1, bass.ds(i, 1)], min_val=0, max_val=E - 1)
                    dve.wait_ge(rows_in[u], 8 * i + 16 - 8 * u)
                    dve.tensor_copy(gate[u][:, :], pay[u][:, :, bass.ds(e + D, 1)].rearrange("p t o -> p (t o)"))
                    dve.tensor_copy(tokf[u][:, :], pay[u][:, :, D + E]).then_inc(meta_read, 1)

                def split_h(i, u):
                    for q in range(2):
                        a, b = q * HC, (q + 1) * HC
                        dve.wait_ge(h_act, 2 * i + q + 1)
                        dve.tensor_copy(hs[u][:, a:b, 0, :], hg[u][:, a:b, :]).then_inc(h_high, 1)
                        dve.wait_ge(h_high, 2 * i + q + 1)
                        dve.tensor_tensor(hs[u][:, a:b, 1, :], hg[u][:, a:b, :], hs[u][:, a:b, 0, :],
                                          ALU.subtract).then_inc(h_split, 1)

                def result(i, u, first):
                    e = dve.value_load(table[0:1, 1, bass.ds(i, 1)], min_val=0, max_val=E - 1)
                    dve.wait_ge(y_ps, i + 1)
                    if not first:
                        dve.wait_ge(y_added, 16 * RP * (i - 1))
                    dve.tensor_copy(toki[u][:, :], tokf[u][:, :])
                    dve.tensor_tensor(yt[u][:, :, :], ps[:, BY + u, :].rearrange("p (t d) -> p t d", d=D),
                                      b2_all[:, bass.ds(e, 1), :].broadcast_to([128, RP, D]), ALU.add)
                    dve.drain()
                    for t in range(RP):
                        ins = dve.tensor_scalar(yt[u][:, t, :], yt[u][:, t, :], gate[u][:, t:t + 1], None, ALU.mult)
                    ins.then_inc(y_ready, 1)

                low_x(0, 0)
                meta(0, 0)
                dve.wait_ge(b2_in, 16)
                split_h(0, 0)
                low_x(1, 1)
                meta(1, 1)

                def step(i, u, first=False, ahead=2):
                    if ahead:
                        if not (first and u == 0):
                            dve.wait_ge(y_ps, i)
                        split_h(i + 1, 1 - u)
                    if ahead > 1:
                        low_x(i + 2, u)
                    result(i, u, first)
                    if ahead > 1:
                        dve.drain()
                        meta(i + 2, u)

                step(0, 0, True)
                step(1, 1, True)
                with dve.Fori(1, LOOPED) as k:
                    step(2 * k, 0)
                    step(2 * k + 1, 1)
                for i in range(2 * LOOPED, NTILE):
                    step(i, i % 2, ahead=min(2, NTILE - 1 - i))

            @block.gpsimd
            def _(pool):
                def add(i, u, first):
                    if not first:
                        pool.wait_ge(y_added, 16 * RP * i)
                    pool.wait_ge(y_ready, i + 1)
                    pool.tensor_tensor(target[:, :], toki[u][:, :], zero[:, :], ALU.add)
                    pool.drain()
                    for t in range(RP):
                        pool.indirect_dma_start(
                            out=acc[:, :], out_offset=bass.IndirectOffsetOnAxis(ap=target[:, t:t + 1], axis=0),
                            in_=yt[u][:, t, :], in_offset=None, compute_op=ALU.add).then_inc(y_added, 16)

                pool.memset(zero[:, :], 0)
                pool.drain()
                add(0, 0, True)
                add(1, 1, False)
                with pool.Fori(1, NTILE // 2) as k:
                    for u in range(2):
                        add(2 * k + u, u, False)
                if NTILE % 2:
                    add(NTILE - 1, 0, False)

            @block.tensor
            def _(pe):
                def expert_of(i):
                    return pe.value_load(table[0:1, 1, bass.ds(i, 1)], min_val=0, max_val=E - 1)

                def turn(i, u):
                    pe.wait_ge(rows_in[u], 8 * i + 16 - 8 * u)
                    for c in range(DC):
                        for t in range(RP):
                            mm = pe.transpose(ps[:, BT, c * ROWS + t * 128:c * ROWS + (t + 1) * 128],
                                              pay[u][:, t, c * 128:(c + 1) * 128], ident[:, :])
                    mm.then_inc(xt_ps, 1)

                def up(i, u, e, first=False):
                    pe.wait_ge(x_split, i + 1)
                    for j in range(FC):
                        if j % HC == 0 and not first:
                            pe.wait_ge(h_act, 2 * i - 1 + j // HC)
                        n = 0
                        for c in range(DC):
                            for wp, xp in ((0, 0), (0, 1), (1, 0)):
                                w = w1s[:, bass.ds(e, 1), c, wp, j * 128:(j + 1) * 128].rearrange("p o f -> p (o f)")
                                mm = pe.matmul(hidden(j), w, xs[u][:, c, xp, :], start=n == 0, stop=n == 3 * DC - 1)
                                n += 1
                        if j % HC == HC - 1:
                            mm.then_inc(h_ps, 1)

                def down(i, u, e, first):
                    if not first:
                        pe.wait_ge(y_ready, i - 1)
                    for t in range(RP):
                        for j in range(FC):
                            if t == 0 and j % HC == 0:
                                pe.wait_ge(h_split, 2 * i + j // HC + 1)
                            for hp, wp in ((0, 0), (0, 1), (1, 0)):
                                w = w2s[:, bass.ds(e, 1), j, wp, :].rearrange("p o d -> p (o d)")
                                mm = pe.matmul(ps[:, BY + u, t * D:(t + 1) * D], hs[u][:, j, hp, t * 128:(t + 1) * 128],
                                               w, start=j == 0 and hp == 0 and wp == 0, stop=j == FC - 1 and hp == 1)
                    mm.then_inc(y_ps, 1)

                def step(i, u, e, e_next, first=False, ahead=2):
                    if ahead:
                        up(i + 1, 1 - u, e_next)
                    if ahead > 1:
                        turn(i + 2, u)
                    down(i, u, e, first)

                turn(0, 0)
                e0, e1, e2 = (expert_of(i) for i in range(3))
                up(0, 0, e0, True)
                turn(1, 1)
                step(0, 0, e0, e1, True)
                step(1, 1, e1, e2, True)
                with pe.Fori(1, LOOPED) as k:
                    e0, e1, e2 = (expert_of(2 * k + d) for d in range(3))
                    step(2 * k, 0, e0, e1)
                    step(2 * k + 1, 1, e1, e2)
                left = range(2 * LOOPED, NTILE)
                of = [expert_of(i) for i in left] + [None]
                for n, i in enumerate(left):
                    step(i, i % 2, of[n], of[n + 1], ahead=min(2, NTILE - 1 - i))


_INS = ["x", "L0_tok_W_h", "L0_tok_b_h", "L0_tok_W_o", "L0_tok_b_o", "L0_tok_W_r", "L0_tok_b_r",
        "L0_attn_W_dq", "L0_attn_W_uq", "L0_attn_W_dkv", "L0_attn_W_uk", "L0_attn_W_uv", "L0_attn_W_o",
        "L0_ffn_router_w", "L0_ffn_router_b", "L0_ffn_w1", "L0_ffn_b1", "L0_ffn_w2", "L0_ffn_b2"]


def kernel(**inputs):
    import numpy as _np
    import concourse.bacc as _bacc
    from concourse.bass_utils import run_bass_kernel_spmd as _run

    nc = _bacc.Bacc("TRN2", target_bir_lowering=False, num_devices=1)
    arrays, args = {}, []
    for name in _INS:
        a = _np.ascontiguousarray(inputs[name])
        arrays[f"in_{name}"] = a
        args.append(nc.dram_tensor(f"in_{name}", a.shape, mybir.dt.from_np(a.dtype), kind="ExternalInput").ap())
    args.append(nc.dram_tensor("out_0", (B, S, D), F32, kind="ExternalOutput").ap())
    build(nc, *args)
    r = _run(nc, [arrays], core_ids=[0])
    return r.results[0]["out_0"]
```
